# Optimizing a Trainium2 kernel written in Bass

```python
import numpy as np
import jax
import jax.numpy as jnp

def _softmax(x, axis=-1):
    return jax.nn.softmax(x, axis=axis)

def _gelu(x):
    return jax.nn.gelu(x, approximate=True)

def _silu(x):
    return jax.nn.silu(x)

def _sigmoid(x):
    return jax.nn.sigmoid(x)

def _layernorm(x, axis=-1, eps=1e-05):
    m = jnp.mean(x, axis=axis, keepdims=True)
    v = jnp.var(x, axis=axis, keepdims=True)
    return (x - m) / jnp.sqrt(v + eps)

def _scatter_add(tgt, idx, src, axis=0):
    return tgt.at[idx].add(src)

def _segment_sum(src, seg, n):
    return jax.ops.segment_sum(src, seg, n)
kernel_name = 'mk_prb_d4_jaxref_r8_f3f353'

def setup_inputs(seed: int=0):
    np.random.seed(seed)
    _w = jnp.asarray

    def _L0_attn_setup():
        import math
        import jax, jax.numpy as jnp
        import numpy as np

        def _rope_tables(T, h, dtype):
            pos = jnp.arange(T, dtype=jnp.float32)
            thetas = 1.0 / 10000.0 ** (jnp.arange(0, h, 2, dtype=jnp.float32) / h)
            pt = jnp.outer(pos, thetas)
            pt = jnp.concatenate([pt, pt], axis=-1)
            return (jnp.sin(pt).astype(dtype), jnp.cos(pt).astype(dtype))

        def _apply_rope(x, sin, cos):
            h = x.shape[-1]
            rot = jnp.concatenate([-x[..., h // 2:], x[..., :h // 2]], axis=-1)
            return x * cos + rot * sin
        key = jax.random.key(seed)
        ks = jax.random.split(key, 5)
        B, T, C = (2, 256, 512)
        s = 1.0 / math.sqrt(C)
        return {'x': jax.random.normal(ks[0], (B, T, C), dtype=jnp.float32), 'wq': jax.random.normal(ks[1], (C, C), dtype=jnp.float32) * s, 'wk': jax.random.normal(ks[2], (C, C), dtype=jnp.float32) * s, 'wv': jax.random.normal(ks[3], (C, C), dtype=jnp.float32) * s, 'wo': jax.random.normal(ks[4], (C, C), dtype=jnp.float32) * s}
    _L0_attn_in = _L0_attn_setup()

    def _L0_ffn_setup():
        import jax, jax.numpy as jnp
        import numpy as np
        HIDDEN = 512
        INTER = 1376
        GROUPSIZE = 128
        PACK = 8

        def dequant_gptq(qweight, scales, zeros, groupsize):
            K = qweight.shape[0] * PACK
            N = qweight.shape[1]
            k = jnp.arange(K)
            q = qweight[k // PACK, :] >> (k % PACK * 4)[:, None] & 15
            n = jnp.arange(N)
            z = zeros[:, n // PACK] >> (n % PACK * 4)[None, :] & 15
            s = scales.astype(jnp.float32)
            zp = (z.astype(jnp.float32) + 1.0) * s
            g = k // groupsize
            return q.astype(jnp.float32) * s[g] - zp[g]
        key = jax.random.key(seed)
        ks = jax.random.split(key, 11)
        imax = 2147483647
        G_h = HIDDEN // GROUPSIZE
        G_i = (INTER + GROUPSIZE - 1) // GROUPSIZE
        x = (jax.random.normal(ks[0], (2, 256, HIDDEN), dtype=jnp.float32) * 0.5).astype(jnp.float16)
        return {'x': x, 'gate_qweight': jax.random.randint(ks[1], (HIDDEN // PACK, INTER), 0, imax, dtype=jnp.int32), 'gate_scales': (jax.random.uniform(ks[2], (G_h, INTER), dtype=jnp.float32) * 0.01 + 0.001).astype(jnp.float16), 'gate_zeros': jax.random.randint(ks[3], (G_h, INTER // PACK), 0, imax, dtype=jnp.int32), 'up_qweight': jax.random.randint(ks[4], (HIDDEN // PACK, INTER), 0, imax, dtype=jnp.int32), 'up_scales': (jax.random.uniform(ks[5], (G_h, INTER), dtype=jnp.float32) * 0.01 + 0.001).astype(jnp.float16), 'up_zeros': jax.random.randint(ks[6], (G_h, INTER // PACK), 0, imax, dtype=jnp.int32), 'down_qweight': jax.random.randint(ks[7], (INTER // PACK, HIDDEN), 0, imax, dtype=jnp.int32), 'down_scales': (jax.random.uniform(ks[8], (G_i, HIDDEN), dtype=jnp.float32) * 0.01 + 0.001).astype(jnp.float16), 'down_zeros': jax.random.randint(ks[9], (G_i, HIDDEN // PACK), 0, imax, dtype=jnp.int32)}
    _L0_ffn_in = _L0_ffn_setup()

    def _L1_attn_setup():
        import jax, jax.numpy as jnp
        import numpy as np
        HDC_DIM = 512
        N_HEADS = 4
        HEAD_DIM = HDC_DIM // N_HEADS

        def _ste_sign(w):
            alpha = jnp.mean(jnp.abs(w), axis=-1, keepdims=True)
            hard = alpha * jnp.sign(w)
            hard = jnp.where(hard == 0, alpha, hard)
            return jax.lax.stop_gradient(hard - w) + w
        key = jax.random.key(seed)
        kx, kq, kk, kv = jax.random.split(key, 4)
        B, T = (4, 256)
        x = jax.random.normal(kx, (B, T, HDC_DIM), dtype=jnp.float32)
        bv_q = jax.random.normal(kq, (N_HEADS, HEAD_DIM), dtype=jnp.float32) * 0.02
        bv_k = jax.random.normal(kk, (N_HEADS, HEAD_DIM), dtype=jnp.float32) * 0.02
        bv_v = jax.random.normal(kv, (N_HEADS, HEAD_DIM), dtype=jnp.float32) * 0.02
        return {'x': x, 'bv_q': bv_q, 'bv_k': bv_k, 'bv_v': bv_v}
    _L1_attn_in = _L1_attn_setup()

    def _L1_ffn_setup():
        import jax, jax.numpy as jnp
        import numpy as np
        RANKS = (8, 16, 32, 64)
        TOPK = 1
        SCALING = 1.0 / 4
        key = jax.random.key(seed)
        ks = jax.random.split(key, 7)
        D_IN, D_OUT, MAX_R, N_RANKS = (512, 512, 64, len(RANKS))
        B_, S_ = (4, 256)
        return {'hidden_states': jax.random.normal(ks[0], (B_, S_, D_IN), jnp.float32), 'W': jax.random.normal(ks[1], (D_OUT, D_IN), jnp.float32) * 0.02, 'b': jax.random.normal(ks[2], (D_OUT,), jnp.float32) * 0.02, 'A': jax.random.normal(ks[3], (MAX_R, D_IN), jnp.float32) * 0.02, 'B': jnp.zeros((D_OUT, MAX_R), jnp.float32) + jax.random.normal(ks[4], (D_OUT, MAX_R), jnp.float32) * 0.02, 'gate_w': jax.random.normal(ks[5], (N_RANKS, D_IN), jnp.float32) * 0.02, 'gate_b': jax.random.normal(ks[6], (N_RANKS,), jnp.float32) * 0.02}
    _L1_ffn_in = _L1_ffn_setup()

    def _L2_attn_setup():
        import jax, jax.numpy as jnp
        import numpy as np
        B, S, H = (1, 256, 512)
        N_HEADS, N_KV, HEAD_DIM = (32, 8, 128)
        ROPE_THETA = 10000.0

        def _rope_tables(seqlen, dim, theta):
            inv_freq = 1.0 / theta ** (jnp.arange(0, dim, 2, dtype=jnp.float32) / dim)
            t = jnp.arange(seqlen, dtype=jnp.float32)
            freqs = jnp.outer(t, inv_freq)
            return (jnp.cos(freqs), jnp.sin(freqs))

        def _apply_rope(x, cos, sin):
            d2 = x.shape[-1] // 2
            x1, x2 = (x[..., :d2], x[..., d2:])
            c = cos[None, :, None, :]
            s = sin[None, :, None, :]
            return jnp.concatenate([x1 * c - x2 * s, x1 * s + x2 * c], axis=-1)
        key = jax.random.key(seed)
        k1, k2, k3 = jax.random.split(key, 3)
        hidden_states = jax.random.normal(k1, (B, S, H), dtype=jnp.float32)
        Wqkv = jax.random.normal(k2, ((N_HEADS + 2 * N_KV) * HEAD_DIM, H), dtype=jnp.float32) * 0.02
        Wo = jax.random.normal(k3, (H, N_HEADS * HEAD_DIM), dtype=jnp.float32) * 0.02
        return {'hidden_states': hidden_states, 'Wqkv': Wqkv, 'Wo': Wo}
    _L2_attn_in = _L2_attn_setup()

    def _L2_ffn_setup():
        import jax, jax.numpy as jnp
        import numpy as np
        B, S, D, O, R, E = (4, 256, 512, 512, 16, 8)
        SCALING = 32.0 / 16.0
        key = jax.random.key(seed)
        ks = jax.random.split(key, 7)
        x = jax.random.normal(ks[0], (B, S, D), dtype=jnp.float32)
        W_base = jax.random.normal(ks[1], (O, D), dtype=jnp.float32) * 0.02
        b_base = jnp.zeros((O,), dtype=jnp.float32)
        A_w = jax.random.normal(ks[2], (R, D), dtype=jnp.float32) * 0.02
        B_w = jax.random.normal(ks[3], (O, R), dtype=jnp.float32) * 0.02
        router_w = jax.random.normal(ks[4], (E, D), dtype=jnp.float32) * 0.02
        cores = jax.random.normal(ks[5], (E, R, R), dtype=jnp.float32)
        return {'x': x, 'W_base': W_base, 'b_base': b_base, 'A_w': A_w, 'B_w': B_w, 'router_w': router_w, 'cores': cores}
    _L2_ffn_in = _L2_ffn_setup()

    def _L3_attn_setup():
        import jax, jax.numpy as jnp
        import numpy as np
        B, S, HID = (2, 512, 512)
        H, HKV, D = (32, 8, 128)
        G = H // HKV
        EPS = 1e-06

        def _reference_tuple_inner(hidden_states, Wq, bq, Wk, bk, Wv, bv, Wo, M, z):
            b, s, _ = hidden_states.shape
            q = (hidden_states @ Wq.T + bq).reshape(b, s, H, D)
            k = (hidden_states @ Wk.T + bk).reshape(b, s, HKV, D)
            v = (hidden_states @ Wv.T + bv).reshape(b, s, HKV, D)
            sig_q = jax.nn.elu(q) + 1.0
            sig_k = jax.nn.elu(k) + 1.0
            q_sel = sig_q[:, :, ::G, :]
            num = jnp.einsum('bshd,hde->bshe', q_sel, M)
            den = jnp.einsum('bshd,hd->bsh', q_sel, z)[..., None] + EPS
            retrieved = num / den
            out_heads = jnp.repeat(retrieved, G, axis=2)
            output = out_heads.reshape(b, s, H * D) @ Wo.T
            M_new = M + jnp.einsum('bshd,bshe->hde', sig_k, v)
            z_new = z + sig_k.sum(axis=(0, 1))
            return (output, M_new, z_new)
        key = jax.random.key(seed)
        ks = jax.random.split(key, 10)
        s = 0.02
        return {'hidden_states': jax.random.normal(ks[0], (B, S, HID), jnp.float32), 'Wq': jax.random.normal(ks[1], (H * D, HID), jnp.float32) * s, 'bq': jnp.zeros((H * D,), jnp.float32), 'Wk': jax.random.normal(ks[2], (HKV * D, HID), jnp.float32) * s, 'bk': jnp.zeros((HKV * D,), jnp.float32), 'Wv': jax.random.normal(ks[3], (HKV * D, HID), jnp.float32) * s, 'bv': jnp.zeros((HKV * D,), jnp.float32), 'Wo': jax.random.normal(ks[4], (HID, H * D), jnp.float32) * s, 'M': jax.random.normal(ks[5], (HKV, D, D), jnp.float32), 'z': jax.random.uniform(ks[6], (HKV, D), jnp.float32) * 100.0 + 1.0}
    _L3_attn_in = _L3_attn_setup()

    def _L3_ffn_setup():
        import jax, jax.numpy as jnp
        import numpy as np
        OUT, IN = (512, 512)
        PACKED = (OUT * IN + 1) // 2

        def _dequant_weight(weight_packed, scale, zero_point):
            low = (weight_packed & 15).astype(jnp.float32)
            high = (weight_packed >> 4 & 15).astype(jnp.float32)
            unpacked = jnp.stack([low, high], axis=1).reshape(-1)
            w = unpacked[:OUT * IN].reshape(OUT, IN)
            return (w - zero_point) * scale
        key = jax.random.key(seed)
        k1, k2, k3, k4, k5 = jax.random.split(key, 5)
        x = jax.random.normal(k1, (4, 256, IN), dtype=jnp.float32)
        weight_packed = jax.random.randint(k2, (PACKED,), 0, 32, dtype=jnp.int32)
        scale = jax.random.uniform(k3, (OUT, 1), dtype=jnp.float32) * 0.01 + 0.0001
        zero_point = jax.random.uniform(k4, (OUT, 1), dtype=jnp.float32) * 8.0
        bias = jax.random.normal(k5, (OUT,), dtype=jnp.float32) * 0.02
        return {'x': x, 'weight_packed': weight_packed, 'scale': scale, 'zero_point': zero_point, 'bias': bias}
    _L3_ffn_in = _L3_ffn_setup()
    _d = {'L0_attn_x': _L0_attn_in['x'], 'L0_attn_wq': _L0_attn_in['wq'], 'L0_attn_wk': _L0_attn_in['wk'], 'L0_attn_wv': _L0_attn_in['wv'], 'L0_attn_wo': _L0_attn_in['wo'], 'L0_ffn_gate_qweight': _L0_ffn_in['gate_qweight'], 'L0_ffn_gate_scales': _L0_ffn_in['gate_scales'], 'L0_ffn_gate_zeros': _L0_ffn_in['gate_zeros'], 'L0_ffn_up_qweight': _L0_ffn_in['up_qweight'], 'L0_ffn_up_scales': _L0_ffn_in['up_scales'], 'L0_ffn_up_zeros': _L0_ffn_in['up_zeros'], 'L0_ffn_down_qweight': _L0_ffn_in['down_qweight'], 'L0_ffn_down_scales': _L0_ffn_in['down_scales'], 'L0_ffn_down_zeros': _L0_ffn_in['down_zeros'], 'L1_attn_bv_q': _L1_attn_in['bv_q'], 'L1_attn_bv_k': _L1_attn_in['bv_k'], 'L1_attn_bv_v': _L1_attn_in['bv_v'], 'L1_ffn_W': _L1_ffn_in['W'], 'L1_ffn_b': _L1_ffn_in['b'], 'L1_ffn_A': _L1_ffn_in['A'], 'L1_ffn_B': _L1_ffn_in['B'], 'L1_ffn_gate_w': _L1_ffn_in['gate_w'], 'L1_ffn_gate_b': _L1_ffn_in['gate_b'], 'L2_attn_Wqkv': _L2_attn_in['Wqkv'], 'L2_attn_Wo': _L2_attn_in['Wo'], 'L2_ffn_W_base': _L2_ffn_in['W_base'], 'L2_ffn_b_base': _L2_ffn_in['b_base'], 'L2_ffn_A_w': _L2_ffn_in['A_w'], 'L2_ffn_B_w': _L2_ffn_in['B_w'], 'L2_ffn_router_w': _L2_ffn_in['router_w'], 'L2_ffn_cores': _L2_ffn_in['cores'], 'L3_attn_Wq': _L3_attn_in['Wq'], 'L3_attn_bq': _L3_attn_in['bq'], 'L3_attn_Wk': _L3_attn_in['Wk'], 'L3_attn_bk': _L3_attn_in['bk'], 'L3_attn_Wv': _L3_attn_in['Wv'], 'L3_attn_bv': _L3_attn_in['bv'], 'L3_attn_Wo': _L3_attn_in['Wo'], 'L3_attn_M': _L3_attn_in['M'], 'L3_attn_z': _L3_attn_in['z'], 'L3_ffn_weight_packed': _L3_ffn_in['weight_packed'], 'L3_ffn_scale': _L3_ffn_in['scale'], 'L3_ffn_zero_point': _L3_ffn_in['zero_point'], 'L3_ffn_bias': _L3_ffn_in['bias']}
    _x0 = _d['L0_attn_x']
    _d['L0_attn_x'] = jax.random.normal(jax.random.fold_in(jax.random.key(seed), 1), (4, 256, 512), dtype=_x0.dtype)
    del _x0
    return _d

def reference(L0_attn_x, L0_attn_wq, L0_attn_wk, L0_attn_wv, L0_attn_wo, L0_ffn_gate_qweight, L0_ffn_gate_scales, L0_ffn_gate_zeros, L0_ffn_up_qweight, L0_ffn_up_scales, L0_ffn_up_zeros, L0_ffn_down_qweight, L0_ffn_down_scales, L0_ffn_down_zeros, L1_attn_bv_q, L1_attn_bv_k, L1_attn_bv_v, L1_ffn_W, L1_ffn_b, L1_ffn_A, L1_ffn_B, L1_ffn_gate_w, L1_ffn_gate_b, L2_attn_Wqkv, L2_attn_Wo, L2_ffn_W_base, L2_ffn_b_base, L2_ffn_A_w, L2_ffn_B_w, L2_ffn_router_w, L2_ffn_cores, L3_attn_Wq, L3_attn_bq, L3_attn_Wk, L3_attn_bk, L3_attn_Wv, L3_attn_bv, L3_attn_Wo, L3_attn_M, L3_attn_z, L3_ffn_weight_packed, L3_ffn_scale, L3_ffn_zero_point, L3_ffn_bias):

    def _L0_attn_ref(x, wq, wk, wv, wo):
        import math
        import jax, jax.numpy as jnp
        import numpy as np

        def _rope_tables(T, h, dtype):
            pos = jnp.arange(T, dtype=jnp.float32)
            thetas = 1.0 / 10000.0 ** (jnp.arange(0, h, 2, dtype=jnp.float32) / h)
            pt = jnp.outer(pos, thetas)
            pt = jnp.concatenate([pt, pt], axis=-1)
            return (jnp.sin(pt).astype(dtype), jnp.cos(pt).astype(dtype))

        def _apply_rope(x, sin, cos):
            h = x.shape[-1]
            rot = jnp.concatenate([-x[..., h // 2:], x[..., :h // 2]], axis=-1)
            return x * cos + rot * sin
        B, T, C = x.shape
        n_head = 32
        h = C // n_head

        def proj(w):
            y = jnp.einsum('btc,dc->btd', x, w)
            return y.reshape(B, T, n_head, h).transpose(0, 2, 1, 3)
        q, k, v = (proj(wq), proj(wk), proj(wv))
        sin, cos = _rope_tables(T, h, x.dtype)
        q = _apply_rope(q, sin, cos)
        k = _apply_rope(k, sin, cos)
        scores = jnp.einsum('bnth,bnsh->bnts', q, k) * (1.0 / math.sqrt(h))
        causal = jnp.tril(jnp.ones((T, T), dtype=bool))
        scores = jnp.where(causal, scores, -jnp.inf)
        attn = jax.nn.softmax(scores, axis=-1)
        out = jnp.einsum('bnts,bnsh->bnth', attn, v)
        out = out.transpose(0, 2, 1, 3).reshape(B, T, C)
        return jnp.einsum('btc,dc->btd', out, wo)

    def _L0_ffn_ref(x, gate_qweight, gate_scales, gate_zeros, up_qweight, up_scales, up_zeros, down_qweight, down_scales, down_zeros):
        import jax, jax.numpy as jnp
        import numpy as np
        HIDDEN = 512
        INTER = 1376
        GROUPSIZE = 128
        PACK = 8

        def dequant_gptq(qweight, scales, zeros, groupsize):
            K = qweight.shape[0] * PACK
            N = qweight.shape[1]
            k = jnp.arange(K)
            q = qweight[k // PACK, :] >> (k % PACK * 4)[:, None] & 15
            n = jnp.arange(N)
            z = zeros[:, n // PACK] >> (n % PACK * 4)[None, :] & 15
            s = scales.astype(jnp.float32)
            zp = (z.astype(jnp.float32) + 1.0) * s
            g = k // groupsize
            return q.astype(jnp.float32) * s[g] - zp[g]
        B, S, H = x.shape
        x2 = x.reshape(-1, H).astype(jnp.float32)
        Wg = dequant_gptq(gate_qweight, gate_scales, gate_zeros, GROUPSIZE)
        Wu = dequant_gptq(up_qweight, up_scales, up_zeros, GROUPSIZE)
        Wd = dequant_gptq(down_qweight, down_scales, down_zeros, GROUPSIZE)
        gate = x2 @ Wg
        up = x2 @ Wu
        inter = gate * jax.nn.sigmoid(gate) * up
        out = (inter @ Wd).astype(jnp.float16)
        return out.reshape(B, S, H)

    def _L1_attn_ref(x, bv_q, bv_k, bv_v):
        import jax, jax.numpy as jnp
        import numpy as np
        HDC_DIM = 512
        N_HEADS = 4
        HEAD_DIM = HDC_DIM // N_HEADS

        def _ste_sign(w):
            alpha = jnp.mean(jnp.abs(w), axis=-1, keepdims=True)
            hard = alpha * jnp.sign(w)
            hard = jnp.where(hard == 0, alpha, hard)
            return jax.lax.stop_gradient(hard - w) + w
        B, T, D = x.shape
        H, HD = (N_HEADS, HEAD_DIM)
        scale = HD ** (-0.5)
        q_bind = _ste_sign(bv_q)
        k_bind = _ste_sign(bv_k)
        v_bind = _ste_sign(bv_v)
        xh = x.reshape(B, T, H, HD)
        Q = xh * q_bind
        K = xh * k_bind
        V = xh * v_bind
        scores = jnp.einsum('bthd,bshd->bhts', Q, K) * scale
        causal = jnp.tril(jnp.ones((T, T), dtype=bool))
        attn = jnp.where(causal, jax.nn.sigmoid(scores * 4.0), 0.0)
        out = jnp.einsum('bhts,bshd->bthd', attn, V)
        return out.reshape(B, T, D)

    def _L1_ffn_ref(hidden_states, W, b, A, B, gate_w, gate_b):
        import jax, jax.numpy as jnp
        import numpy as np
        RANKS = (8, 16, 32, 64)
        TOPK = 1
        SCALING = 1.0 / 4
        bsz, seq, d_in = hidden_states.shape
        out = jnp.einsum('bsd,od->bso', hidden_states, W) + b
        x = hidden_states.reshape(-1, d_in)
        scores = x @ gate_w.T + gate_b
        probs = jax.nn.softmax(scores, axis=-1)
        routing_weights, selected = jax.lax.top_k(probs, TOPK)
        routing_weights = routing_weights / jnp.sum(routing_weights, axis=-1, keepdims=True)
        lora_outputs = jnp.stack([x @ A[:r, :].T @ B[:, :r].T for r in RANKS], axis=1)
        sel = jnp.take_along_axis(lora_outputs, selected[:, :, None], axis=1)
        final = jnp.sum(sel * routing_weights[:, :, None], axis=1)
        return out + final.reshape(bsz, seq, -1)

    def _L2_attn_ref(hidden_states, Wqkv, Wo):
        import jax, jax.numpy as jnp
        import numpy as np
        B, S, H = (1, 256, 512)
        N_HEADS, N_KV, HEAD_DIM = (32, 8, 128)
        ROPE_THETA = 10000.0

        def _rope_tables(seqlen, dim, theta):
            inv_freq = 1.0 / theta ** (jnp.arange(0, dim, 2, dtype=jnp.float32) / dim)
            t = jnp.arange(seqlen, dtype=jnp.float32)
            freqs = jnp.outer(t, inv_freq)
            return (jnp.cos(freqs), jnp.sin(freqs))

        def _apply_rope(x, cos, sin):
            d2 = x.shape[-1] // 2
            x1, x2 = (x[..., :d2], x[..., d2:])
            c = cos[None, :, None, :]
            s = sin[None, :, None, :]
            return jnp.concatenate([x1 * c - x2 * s, x1 * s + x2 * c], axis=-1)
        b, s, h = hidden_states.shape
        qkv = jnp.einsum('bsh,oh->bso', hidden_states, Wqkv)
        q_end = N_HEADS * HEAD_DIM
        k_end = q_end + N_KV * HEAD_DIM
        xq = qkv[..., :q_end].reshape(b, s, N_HEADS, HEAD_DIM)
        xk = qkv[..., q_end:k_end].reshape(b, s, N_KV, HEAD_DIM)
        xv = qkv[..., k_end:].reshape(b, s, N_KV, HEAD_DIM)
        cos, sin = _rope_tables(s, HEAD_DIM, ROPE_THETA)
        xq = _apply_rope(xq, cos, sin)
        xk = _apply_rope(xk, cos, sin)
        groups = N_HEADS // N_KV
        xk = jnp.repeat(xk, groups, axis=2)
        xv = jnp.repeat(xv, groups, axis=2)
        scale = 1.0 / jnp.sqrt(jnp.float32(HEAD_DIM))
        scores = jnp.einsum('bqhd,bkhd->bhqk', xq, xk) * scale
        causal = jnp.tril(jnp.ones((s, s), dtype=bool))
        scores = jnp.where(causal[None, None, :, :], scores, jnp.float32(-1e+30))
        probs = jax.nn.softmax(scores, axis=-1)
        out = jnp.einsum('bhqk,bkhd->bqhd', probs, xv).reshape(b, s, N_HEADS * HEAD_DIM)
        attn_output = jnp.einsum('bsd,hd->bsh', out, Wo)
        return attn_output

    def _L2_ffn_ref(x, W_base, b_base, A_w, B_w, router_w, cores):
        import jax, jax.numpy as jnp
        import numpy as np
        B, S, D, O, R, E = (4, 256, 512, 512, 16, 8)
        SCALING = 32.0 / 16.0
        result = jnp.einsum('bsd,od->bso', x, W_base) + b_base
        ax = jnp.einsum('bsd,rd->bsr', x, A_w)
        probs = jax.nn.softmax(jnp.einsum('bsd,ed->bse', x, router_w), axis=-1)
        per_expert = jnp.einsum('bsr,erq->bseq', ax, cores)
        mixed = jnp.einsum('bseq,bse->bsq', per_expert, probs)
        result = result + jnp.einsum('bsr,or->bso', mixed, B_w) * SCALING
        return result

    def _L3_attn_ref(hidden_states, Wq, bq, Wk, bk, Wv, bv, Wo, M, z):
        import jax, jax.numpy as jnp
        import numpy as np
        B, S, HID = (2, 512, 512)
        H, HKV, D = (32, 8, 128)
        G = H // HKV
        EPS = 1e-06

        def _reference_tuple_inner(hidden_states, Wq, bq, Wk, bk, Wv, bv, Wo, M, z):
            b, s, _ = hidden_states.shape
            q = (hidden_states @ Wq.T + bq).reshape(b, s, H, D)
            k = (hidden_states @ Wk.T + bk).reshape(b, s, HKV, D)
            v = (hidden_states @ Wv.T + bv).reshape(b, s, HKV, D)
            sig_q = jax.nn.elu(q) + 1.0
            sig_k = jax.nn.elu(k) + 1.0
            q_sel = sig_q[:, :, ::G, :]
            num = jnp.einsum('bshd,hde->bshe', q_sel, M)
            den = jnp.einsum('bshd,hd->bsh', q_sel, z)[..., None] + EPS
            retrieved = num / den
            out_heads = jnp.repeat(retrieved, G, axis=2)
            output = out_heads.reshape(b, s, H * D) @ Wo.T
            M_new = M + jnp.einsum('bshd,bshe->hde', sig_k, v)
            z_new = z + sig_k.sum(axis=(0, 1))
            return (output, M_new, z_new)
        return _reference_tuple_inner(hidden_states, Wq, bq, Wk, bk, Wv, bv, Wo, M, z)[0]

    def _L3_ffn_ref(x, weight_packed, scale, zero_point, bias):
        import jax, jax.numpy as jnp
        import numpy as np
        OUT, IN = (512, 512)
        PACKED = (OUT * IN + 1) // 2

        def _dequant_weight(weight_packed, scale, zero_point):
            low = (weight_packed & 15).astype(jnp.float32)
            high = (weight_packed >> 4 & 15).astype(jnp.float32)
            unpacked = jnp.stack([low, high], axis=1).reshape(-1)
            w = unpacked[:OUT * IN].reshape(OUT, IN)
            return (w - zero_point) * scale
        w = _dequant_weight(weight_packed, scale, zero_point)
        return jnp.einsum('bsi,oi->bso', x, w) + bias
    x = L0_attn_x
    xn = _layernorm(x, axis=-1)
    x = x + _L0_attn_ref(xn, L0_attn_wq, L0_attn_wk, L0_attn_wv, L0_attn_wo) + _L0_ffn_ref(xn, L0_ffn_gate_qweight, L0_ffn_gate_scales, L0_ffn_gate_zeros, L0_ffn_up_qweight, L0_ffn_up_scales, L0_ffn_up_zeros, L0_ffn_down_qweight, L0_ffn_down_scales, L0_ffn_down_zeros)
    xn = _layernorm(x, axis=-1)
    x = x + _L1_attn_ref(xn, L1_attn_bv_q, L1_attn_bv_k, L1_attn_bv_v) + _L1_ffn_ref(xn, L1_ffn_W, L1_ffn_b, L1_ffn_A, L1_ffn_B, L1_ffn_gate_w, L1_ffn_gate_b)
    xn = _layernorm(x, axis=-1)
    x = x + _L2_attn_ref(xn, L2_attn_Wqkv, L2_attn_Wo) + _L2_ffn_ref(xn, L2_ffn_W_base, L2_ffn_b_base, L2_ffn_A_w, L2_ffn_B_w, L2_ffn_router_w, L2_ffn_cores)
    xn = _layernorm(x, axis=-1)
    x = x + _L3_attn_ref(xn, L3_attn_Wq, L3_attn_bq, L3_attn_Wk, L3_attn_bk, L3_attn_Wv, L3_attn_bv, L3_attn_Wo, L3_attn_M, L3_attn_z) + _L3_ffn_ref(xn, L3_ffn_weight_packed, L3_ffn_scale, L3_ffn_zero_point, L3_ffn_bias)
    return x

_drawn_inputs = setup_inputs


def setup_inputs(seed=0):
    import zlib

    import numpy as np

    out = dict(_drawn_inputs(seed))
    spreads = {'L2_ffn_b_base': (0.0, 0.1),
     'L3_attn_bq': (0.0, 2.0),
     'L3_attn_bk': (0.0, 0.1),
     'L3_attn_bv': (0.0, 0.1)}
    factors = {'L1_attn_bv_q': 64.0,
     'L1_attn_bv_k': 64.0,
     'L1_ffn_b': 4.698,
     'L1_ffn_gate_w': 13.016,
     'L1_ffn_gate_b': 64.0,
     'L2_ffn_router_w': 2.765,
     'L3_attn_Wq': 45.871,
     'L3_attn_Wo': 35.317,
     'L3_attn_M': 35.654,
     'L3_attn_z': 64.0,
     'L3_ffn_zero_point': 64.0,
     'L3_ffn_bias': 6.194}
    for name, (base, spread) in spreads.items():
        noise = np.random.default_rng([zlib.crc32(name.encode()), seed]).standard_normal(out[name].shape)
        drawn = base * np.exp(spread * noise) if base else spread * noise
        out[name] = jnp.asarray(drawn.astype(out[name].dtype))
    for name, factor in factors.items():
        out[name] = (out[name] * factor).astype(out[name].dtype)
    return out
```

```python
def build_program(nc, d, out):
    from contextlib import ExitStack
    import concourse.bass as bass
    from concourse import mybir

    F32, F32R = mybir.dt.float32, mybir.dt.float32r
    BF16, F16, I32 = mybir.dt.bfloat16, mybir.dt.float16, mybir.dt.int32
    ACT, ALU, AXIS = mybir.ActivationFunctionType, mybir.AluOpType, mybir.AxisListType

    P = 128
    C = 512
    KT = C // P
    TOK = 1024
    TT = TOK // P
    SEQ = 256
    NB = TOK // SEQ
    RAW = 5
    H0, D0 = 32, 16
    G0 = H0 // 4
    S0 = 64
    NF = 11
    H2, KV2, D2 = 32, 8, 128
    H3 = 8
    R1, E1 = 64, 4
    E2, R2 = 8, 16

    U_QKV0, U_W1 = 0, 12
    U_WB2 = U_W1 + KT
    U_L2 = U_WB2 + KT
    U_L2_G = 10
    U_L3 = U_L2 + KV2 * U_L2_G
    U_M3 = U_L3 + H3

    ctx = ExitStack()
    with ctx:
        def sem(name):
            return ctx.enter_context(nc.semaphore(name))

        def keep(name, shape, dt=F32):
            return ctx.enter_context(nc.sbuf_tensor(name, list(shape), dt))

        X = keep("X", [P, TT, C])
        XNH = keep("XNH", [P, KT, TOK], F32R)
        XNL = keep("XNL", [P, KT, TOK], F32R)
        raw = keep("raw", [P, RAW, C])
        ident = keep("ident", [P, P])
        identb = keep("identb", [P, P], BF16)
        mask_ts = keep("mask_ts", [P, P], BF16)
        mask_st = keep("mask_st", [P, 4, P], BF16)
        mask01 = keep("mask01", [P, P])
        pick8 = keep("pick8", [16, 8, P], BF16)
        ones_r = keep("ones_r", [P, P], F32R)
        shift_k = keep("shift_k", [P, 1], I32)
        rope0c = keep("rope0c", [P, 2, D0])
        rope0s = keep("rope0s", [P, 2, D0])
        rope2c = keep("rope2c", [P, SEQ])
        rope2s = keep("rope2s", [P, SEQ])
        PS = ctx.enter_context(nc.psum_tensor("PS", [P, 8, C], F32))

        def phase():
            return ExitStack()

        def sb(stack, name, shape, dt=F32):
            return stack.enter_context(nc.sbuf_tensor(name, list(shape), dt))

        LN = {}

        def ln_buffers(stack, l):
            LN[l] = dict(
                stats=sb(stack, f"ln{l}_stats", [P, TT, 6]), mv=sb(stack, f"ln{l}_mv", [P, TT, 2]),
                var=sb(stack, f"ln{l}_var", [P, TT]), sd=sb(stack, f"ln{l}_sd", [P, TT]),
                tmp=sb(stack, f"ln{l}_tmp", [P, TT]), rstd=sb(stack, f"ln{l}_rstd", [P, TT]),
                xn=sb(stack, f"ln{l}_xn", [P, 2, C]))

        with phase() as st:
            WQH = sb(st, "WQH", [P, 12, C], F32R)
            WQL = sb(st, "WQL", [P, 12, C], F32R)
            wo0 = sb(st, "wo0", [P, KT, C])
            with phase() as st2:
                ln_buffers(st2, 0)
            SGH = sb(st, "SGH", [P, KT, SEQ], F32R)
            SGL = sb(st, "SGL", [P, KT, SEQ], F32R)
            A_T1 = sb(st, "A_T1", [P, H0, D0])
            A_sw = sb(st, "A_sw", [P, H0, D0])
            A_q = sb(st, "A_q", [P, H0, D0])
            STK = sb(st, "STK", [P, H0, S0])
            qT = sb(st, "qT", [P, H0 // 2, SEQ], F32R)
            kT = sb(st, "kT", [P, H0 // 2, SEQ], F32R)
            V0 = sb(st, "V0", [P, 2, H0, 2 * D0])
            P0 = sb(st, "P0", [P, 1536])
            A_O = sb(st, "A_O", [P, SEQ])
            Otok = sb(st, "Otok", [P, 2, H0, D0])
            OT0 = sb(st, "OT0", [P, KT, SEQ])
            A_mx = sb(st, "A_mx", [P, 8])
            A_mxs = sb(st, "A_mxs", [P, 16], BF16)
            A_mxT = sb(st, "A_mxT", [16, P], BF16)
            A_rec = sb(st, "A_rec", [P, 2, 4])

        with phase() as st:
            zw = sb(st, "zw", [NF, 3 * C // 8], I32)
            zshift = sb(st, "zshift", [NF, 8], I32)
            zq = sb(st, "zq", [NF, 3 * C], I32)
            z1 = sb(st, "z1", [NF, 3 * C], F16)
            words = [sb(st, f"words{p}", [P, 3, C], I32) for p in range(2)]
            zb = [sb(st, f"zb{p}", [P, 3, C], F16) for p in range(2)]
            scb = [sb(st, f"scb{p}", [P, 3, C], F16) for p in range(2)]
            F_q = sb(st, "F_q", [P, C], I32)
            F_t = sb(st, "F_t", [P, 3, C])
            F_w = sb(st, "F_w", [P, 3, C])
            FWH = [sb(st, f"FWH{p}", [P, 3, C], F32R) for p in range(2)]
            FWL = [sb(st, f"FWL{p}", [P, 3, C], F32R) for p in range(2)]
            F_sg = sb(st, "F_sg", [P, 2, C])
            F_a = sb(st, "F_a", [P, 2, C])
            F_i = sb(st, "F_i", [P, 2, C])
            FIH = [sb(st, f"FIH{p}", [P, TOK], F32R) for p in range(2)]
            FIL = [sb(st, f"FIL{p}", [P, TOK], F32R) for p in range(2)]
            F_acc = sb(st, "F_acc", [P, TT, C])
            F_half = sb(st, "F_half", [P, TT, C], F16)

        with phase() as st:
            ln_buffers(st, 1)
            XT1 = sb(st, "XT1", [P, KT, TOK])
            K1 = sb(st, "K1", [P, KT, TOK])
            V1 = sb(st, "V1", [P, TT, C])
            bv = sb(st, "bv", [P, 12])
            bvr = sb(st, "bvr", [P, 4, P])
            bv_abs = sb(st, "bv_abs", [P, 12])
            bv_sg = sb(st, "bv_sg", [P, 12])
            bv_q = sb(st, "bv_q", [P, 12])
            qk1 = sb(st, "qk1", [P, 4])
            vr_al = sb(st, "vr_al", [P, 4])
            vr_sg = sb(st, "vr_sg", [P, 4, P])
            vrow = sb(st, "vrow", [P, 4, P])
            inv = sb(st, "inv", [P, P])
            A1 = sb(st, "A1", [P, 1536])
            W1H = sb(st, "W1H", [P, KT, C], F32R)
            W1L = sb(st, "W1L", [P, KT, C], F32R)
            AG1 = sb(st, "AG1", [P, KT, R1 + E1])
            BT1 = sb(st, "BT1", [R1, C])
            b1 = sb(st, "b1", [P, C])
            gb1 = sb(st, "gb1", [P, E1])
            LA = sb(st, "LA", [P, TT, R1 + E1])
            g_m = sb(st, "g_m", [P, TT])
            g_ne = sb(st, "g_ne", [P, TT, E1])
            LAT = sb(st, "LAT", [R1, TOK])

        with phase() as st:
            ln_buffers(st, 2)
            XT2 = sb(st, "XT2", [P, KT, TOK])
            W2H = sb(st, "W2H", [P, KT, C], F32R)
            W2L = sb(st, "W2L", [P, KT, C], F32R)
            AR2 = sb(st, "AR2", [P, KT, R2 + E2])
            coresT = sb(st, "coresT", [R2, E2 * R2])
            BwT = sb(st, "BwT", [R2, C])
            b2 = sb(st, "b2", [P, C])
            axr = sb(st, "axr", [P, TT, R2 + E2])
            e_m = sb(st, "e_m", [P, TT])
            e_p = sb(st, "e_p", [P, TT, E2])
            e_s = sb(st, "e_s", [P, TT])
            U2 = sb(st, "U2", [P, TT, E2, R2])
            UH = sb(st, "UH", [P, TOK], F32R)
            UL = sb(st, "UL", [P, TOK], F32R)
            GH = sb(st, "GH", [P, C], F32R)
            GL = sb(st, "GL", [P, C], F32R)

        with phase() as st:
            E_WH = sb(st, "E_WH", [P, U_L2_G, C], F32R)
            E_WL = sb(st, "E_WL", [P, U_L2_G, C], F32R)
            E_T = sb(st, "E_T", [P, 5, SEQ])
            E_sw = sb(st, "E_sw", [P, 5, SEQ])
            QKH = [sb(st, f"QKH{p}", [P, 5, SEQ], F32R) for p in range(2)]
            QKL = [sb(st, f"QKL{p}", [P, 5, SEQ], F32R) for p in range(2)]
            vT2 = sb(st, "vT2", [P, SEQ])
            VH = [sb(st, f"VH{p}", [P, 2, P], F32R) for p in range(2)]
            VL = [sb(st, f"VL{p}", [P, 2, P], F32R) for p in range(2)]
            E_p = sb(st, "E_p", [P, 3, C])
            PH = sb(st, "PH", [P, 3, C], F32R)
            PL = sb(st, "PL", [P, 3, C], F32R)
            E_r = sb(st, "E_r", [P, 2, C])
            E_t = sb(st, "E_t", [P, 2, C])
            E_o = sb(st, "E_o", [P, 2, C])
            OH = [sb(st, f"OH{p}", [P, 2, C], F32R) for p in range(2)]
            OL = [sb(st, f"OL{p}", [P, 2, C], F32R) for p in range(2)]
            E_mx = sb(st, "E_mx", [P, 8])
            E_mxs = sb(st, "E_mxs", [P, 16], BF16)
            E_mxT = sb(st, "E_mxT", [16, P], BF16)

        with phase() as st:
            with phase() as st2:
                ln_buffers(st2, 3)
                pk3 = sb(st2, "pk3", [P, 2, C], I32)
                zp3 = sb(st2, "zp3", [P, C])
                sc3 = sb(st2, "sc3", [P, C])
                b3 = sb(st2, "b3", [P, C])
                q3 = sb(st2, "q3", [P, KT, C], I32)
                t3 = sb(st2, "t3", [P, KT, C])
                W3H = sb(st2, "W3H", [P, KT, C], F32R)
                W3L = sb(st2, "W3L", [P, KT, C], F32R)
            L3H = sb(st, "L3H", [P, H3 + 2, C], F32R)
            L3L = sb(st, "L3L", [P, H3 + 2, C], F32R)
            WSH = sb(st, "WSH", [P, H3, C], F32R)
            WSL = sb(st, "WSL", [P, H3, C], F32R)
            wo3 = sb(st, "wo3", [P, 4, C])
            G_wo = sb(st, "G_wo", [P, C])
            bq3 = sb(st, "bq3", [P, H3])
            zc3 = sb(st, "zc3", [P, H3])
            ZH = sb(st, "ZH", [P, H3, P], F32R)
            ZL = sb(st, "ZL", [P, H3, P], F32R)
            pickf = sb(st, "pickf", [H3, H3, P])
            pick3 = sb(st, "pick3", [H3, H3, P], F32R)
            G_m = sb(st, "G_m", [P, SEQ])
            G_e = sb(st, "G_e", [P, SEQ])
            G_r = sb(st, "G_r", [P, SEQ])
            G_s = sb(st, "G_s", [P, SEQ])
            SH = [sb(st, f"SH{p}", [P, SEQ], F32R) for p in range(2)]
            SL = [sb(st, f"SL{p}", [P, SEQ], F32R) for p in range(2)]
            num3 = sb(st, "num3", [P, H3, SEQ])
            den3 = sb(st, "den3", [H3, SEQ])
            RH = sb(st, "RH", [H3, SEQ], F32R)
            RL = sb(st, "RL", [H3, SEQ], F32R)
            NH3 = sb(st, "NH3", [P, H3, SEQ], F32R)
            NL3 = sb(st, "NL3", [P, H3, SEQ], F32R)

        const_in = sem("const_in")
        x_in = sem("x_in")
        small_in = sem("small_in")
        SMALL_L1, SMALL_L2, SMALL_F3, SMALL_A3 = 16 * 6, 16 * 10, 16 * 14, 16 * 17
        bias_in = sem("bias_in")
        ffn_ps = sem("ffn_ps")
        ffn_x = sem("ffn_x")
        raw_in = [sem(f"raw_in{r}") for r in range(RAW)]
        w_hi = sem("w_hi")
        w_lo = sem("w_lo")
        phase_done = sem("phase_done")
        LN_SIGNALS = dict(stat=TT, aggr=TT, var=1, sd=1, c=5, xn=TT, tp=TT, hi=TT, lo=TT)
        ln = {n: sem(f"ln_{n}") for n in LN_SIGNALS}

        def ln_wait(eng, l, name, n):
            eng.wait_ge(ln[name], l * LN_SIGNALS[name] + n)

        def sems(prefix, names):
            return {n: sem(f"{prefix}_{n}") for n in names.split()}

        a = sems("a", "stage init proj sw vcp t1 t2 q hi lo tp eva evd max red neg mxs mxt mxc shift exp pv oev ot rec "
                      "s1 otok ott otc wo_ps x")
        f = sems("f", "zin z zout in0 in1 q t w hi lo gu sg a i ih il dps acc half x")
        c1 = sems("c", "abs al c v k1 lo_ps gate st sig mask pv xa lat_ps lat_cp")
        d2 = sems("d", "lo_ps c ax g_ps gh gl tp uh ul")
        e2 = sems("e", "max red neg mxs mxt mxc shift proj sw vt t1 t2 q qhi qlo vtp vhi vlo exp phi plo pv ln r t u o ohi "
                       "olo wo x")
        g3 = sems("g", "woin s12 s wsh wsl zm zh zl pk qps m e r sum shi slo nps ncp dc rh rl bps mul nhi nlo "
                       "ops xo out")

        block = ctx.enter_context(nc.Block())

        def after(eng, signal, n):
            if not isinstance(n, int) or n > 0:
                eng.wait_ge(signal, n)

        def finish(eng, n):
            eng.drain().then_inc(phase_done, 1)
            eng.wait_ge(phase_done, 4 * n)

        def product3(o, sh, sl, mh, ml, first, last):
            nc.tensor.matmul(o, sl, mh, start=first, stop=False)
            nc.tensor.matmul(o, sh, ml, start=False, stop=False)
            return nc.tensor.matmul(o, sh, mh, start=False, stop=last)

        def f32(ap):
            return ap.bitcast(F32)

        @block.sync
        def _(sp):
            for tt in range(TT):
                sp.dma_start(X[:, tt, :], d["x"][tt]).then_inc(x_in, 16)

            def load_unit(n, slot, src):
                if not isinstance(n, int) or n >= RAW:
                    sp.wait_ge(w_lo, n - RAW + 1)
                sp.dma_start(raw[:, slot, :], src).then_inc(raw_in[slot], 16)

            for u in range(12):
                load_unit(U_QKV0 + u, u % RAW, d["w0"][u])
            for kt in range(KT):
                sp.dma_start(wo0[:, kt, :], d["w0"][12 + kt]).then_inc(x_in, 16)
            ln_wait(sp, 0, "lo", TT)
            def attend(b):
                after(sp, a["proj"], b * 6)
                sp.dma_start(f32(SGH[:, :, :]), f32(XNH[:, :, bass.ds(b * SEQ, SEQ)])).then_inc(a["stage"], 16)
                sp.dma_start(f32(SGL[:, :, :]), f32(XNL[:, :, bass.ds(b * SEQ, SEQ)])).then_inc(a["stage"], 16)

            attend(0)
            with sp.Fori(1, NB) as b:
                attend(b)
            sp.wait_ge(phase_done, 4 * 2)
            sp.dma_start(zw[:, :], d["zeros"]).then_inc(f["zin"], 16)
            sp.dma_start(zshift[:, :], d["shift_n"]).then_inc(f["zin"], 16)
            sp.wait_ge(f["z"], 3)
            sp.dma_start(d["z1_scratch"], z1[:, :]).then_inc(f["zout"], 16)
            sp.wait_ge(f["zout"], 16)

            def load_tile(n, p):
                if not isinstance(n, int) or n >= 2:
                    sp.wait_ge(f["w"], n * 3 - 3)
                for c in range(3):
                    for r in range(8):
                        sp.dma_start(words[p][r:P:8, c, :], d["words"][c, bass.ds(n, 1), :, :].rearrange("a r n -> (a r) n"))\
                          .then_inc(f[f"in{p}"], 16)
                sp.dma_start(zb[p][:, :, :], d["z1_scratch"][bass.ds(n, 1), :].rearrange("a (c n) -> a c n", c=3).broadcast_to([P, 3, C]))\
                  .then_inc(f[f"in{p}"], 16)
                sp.dma_start(scb[p][:, :, :], d["scales"][bass.ds(n, 1), :].rearrange("a (c n) -> a c n", c=3).broadcast_to([P, 3, C]))\
                  .then_inc(f[f"in{p}"], 16)

            load_tile(0, 0)
            with sp.Fori(0, (NF - 1) // 2) as i:
                load_tile(i * 2 + 1, 1)
                load_tile(i * 2 + 2, 0)
            for u in range(KT):
                load_unit(U_W1 + u, (U_W1 + u) % RAW, d["w1"][u])
            for u in range(KT):
                load_unit(U_WB2 + u, (U_WB2 + u) % RAW, d["wb2"][u])
            with sp.Fori(0, KV2) as g:
                for u in range(U_L2_G):
                    load_unit(g * U_L2_G + (U_L2 + u), (U_L2 + u) % RAW,
                              d["w2"][bass.ds(g, 1), u, :, :].rearrange("a p n -> (a p) n"))
            for u in range(H3 + 2):
                load_unit(U_L3 + u, (U_L3 + u) % RAW, d["w3"][u])
            sp.wait_ge(phase_done, 4 * 9)
            for h in range(H3):
                for q in range(4):
                    if h >= 1:
                        sp.wait_ge(g3["s"], h)
                    sp.dma_start(wo3[:, q, :], d["wo3"][h, q]).then_inc(g3["woin"], 16)
            def recall(b):
                for tl in range(2):
                    sp.wait_ge(g3["xo"], b * 2 + (tl + 1))
                    sp.dma_start(out[bass.ds(b * 2 + tl, 1), :, :].rearrange("a p c -> p (a c)"),
                                 X[:, bass.ds(b * 2 + tl, 1), :].rearrange("p a c -> p (a c)")).then_inc(g3["out"], 16)

            recall(0)
            with sp.Fori(1, NB) as b:
                recall(b)
            sp.wait_ge(g3["out"], 16 * TT)

        @block.gpsimd
        def _(pool):
            def rest(n, hi, lo, slot):
                pool.wait_ge(w_hi, n + 1)
                nc.gpsimd.tensor_tensor(lo, raw[:, slot, :], f32(hi), ALU.subtract).then_inc(w_lo, 1)

            nc.gpsimd.memset(f32(ones_r[:, :]), 1.0).then_inc(a["init"], 1)
            for u in range(12):
                rest(U_QKV0 + u, WQH[:, u, :], WQL[:, u, :], u % RAW)
            finish(pool, 1)
            nc.gpsimd.memset(STK[:, :, 3 * D0:S0], 0.0).then_inc(a["init"], 1)
            nc.gpsimd.memset(V0[:, :, :, D0:2 * D0], 1.0).then_inc(a["init"], 1)
            pool.wait_ge(const_in, 16 * 11)
            def attend(b):
                for j in range(4):
                    tl = j // 2
                    pool.wait_ge(a["sw"], b * 4 + (j + 1))
                    nc.gpsimd.tensor_tensor(A_sw[:, :, :], A_sw[:, :, :],
                                            rope0s[:, tl, :].unsqueeze(1).broadcast_to([P, H0, D0]), ALU.mult)\
                      .then_inc(a["t2"], 1)

            attend(0)
            with pool.Fori(1, NB) as b:
                attend(b)
            finish(pool, 2)
            def scale_tile(n, p):
                for c in range(3):
                    pool.wait_ge(f["t"], n * 3 + (c + 1))
                    if not isinstance(n, int) or n >= 1:
                        pool.wait_ge(f["lo"], n * 3 + (c - 2))
                    nc.gpsimd.tensor_tensor(F_w[:, c, :], F_t[:, c, :], scb[p][:, c, :], ALU.mult).then_inc(f["w"], 1)

            scale_tile(0, 0)
            with pool.Fori(0, (NF - 1) // 2) as i:
                scale_tile(i * 2 + 1, 1)
                scale_tile(i * 2 + 2, 0)
            finish(pool, 3)
            for u in range(KT):
                rest(U_W1 + u, W1H[:, u, :], W1L[:, u, :], (U_W1 + u) % RAW)
            nc.gpsimd.memset(inv[:, :], 1.0 / P).then_inc(a["init"], 1)
            finish(pool, 4)
            pool.wait_ge(small_in, SMALL_L1)
            for tt in range(TT):
                nc.gpsimd.tensor_tensor(X[:, tt, :], X[:, tt, :], b1[:, :], ALU.add).then_inc(bias_in, 1)
            finish(pool, 5)
            for u in range(KT):
                rest(U_WB2 + u, W2H[:, u, :], W2L[:, u, :], (U_WB2 + u) % RAW)
            finish(pool, 6)
            pool.wait_ge(small_in, SMALL_L2)
            for tt in range(TT):
                nc.gpsimd.tensor_tensor(X[:, tt, :], X[:, tt, :], b2[:, :], ALU.add).then_inc(bias_in, 1)
            finish(pool, 7)
            def l2_rest(g, u):
                rest(g * U_L2_G + (U_L2 + u), E_WH[:, u, :], E_WL[:, u, :], (U_L2 + u) % RAW)

            def l2_sines(i):
                pool.wait_ge(e2["sw"], i + 1)
                nc.gpsimd.tensor_tensor(E_sw[:, :, :], E_sw[:, :, :],
                                        rope2s[:, :].unsqueeze(1).broadcast_to([P, 5, SEQ]), ALU.mult).then_inc(e2["t2"], 1)

            def l2_pool_group(g, more):
                for j in range(NB):
                    l2_sines(g * NB + j)
                    if j == 1:
                        for u in range(6, U_L2_G):
                            l2_rest(g, u)
                    if j == NB - 1 and more:
                        for u in range(6):
                            l2_rest(g + 1, u)

            for u in range(6):
                l2_rest(0, u)
            with pool.Fori(0, KV2 - 1) as g:
                l2_pool_group(g, True)
            l2_pool_group(KV2 - 1, False)
            finish(pool, 8)
            pool.wait_ge(small_in, SMALL_F3)
            for k in range(KT):
                pool.wait_ge(f["t"], 3 * NF + k + 1)
                nc.gpsimd.tensor_tensor(t3[:, k, :], t3[:, k, :], sc3[:, :], ALU.mult).then_inc(f["w"], 1)
            ln_wait(pool, 3, "xn", TT)
            for tt in range(TT):
                nc.gpsimd.tensor_tensor(X[:, tt, :], X[:, tt, :], b3[:, :], ALU.add).then_inc(bias_in, 1)
            finish(pool, 9)
            for u in range(H3 + 2):
                rest(U_L3 + u, L3H[:, u, :], L3L[:, u, :], (U_L3 + u) % RAW)
            for h in range(H3):
                pool.wait_ge(g3["woin"], 64 * (h + 1))
                if h >= 1:
                    pool.wait_ge(g3["wsl"], h)
                nc.gpsimd.tensor_tensor(wo3[:, 0, :], wo3[:, 0, :], wo3[:, 1, :], ALU.add).then_inc(g3["s12"], 1)
                nc.gpsimd.tensor_tensor(wo3[:, 2, :], wo3[:, 2, :], wo3[:, 3, :], ALU.add).then_inc(g3["s12"], 1)
                pool.wait_ge(g3["s12"], 2 * h + 2)
                nc.gpsimd.tensor_tensor(G_wo[:, :], wo3[:, 0, :], wo3[:, 2, :], ALU.add).then_inc(g3["s"], 1)
                pool.wait_ge(g3["wsh"], h + 1)
                nc.gpsimd.tensor_tensor(WSL[:, h, :], G_wo[:, :], f32(WSH[:, h, :]), ALU.subtract).then_inc(g3["wsl"], 1)
            finish(pool, 10)

        @block.scalar
        def _(act):
            def copy(o, i, signal=None):
                ins = nc.scalar.activation(o, i, ACT.Copy)
                return ins.then_inc(signal, 1) if signal is not None else ins

            def head(slot, use, hi):
                act.wait_ge(raw_in[slot], use * 16)
                copy(hi, raw[:, slot, :], w_hi)

            def head_of(n, hi):
                head(n % RAW, n // RAW + 1, hi)

            def normalise(l, XT=None):
                ln_wait(act, l, "var", 1)
                nc.scalar.activation(LN[l]["sd"][:, :], LN[l]["var"][:, :], ACT.Sqrt).then_inc(ln["sd"], 1)
                for tt in range(TT):
                    ln_wait(act, l, "tp", tt + 1)
                    bank = PS[:, tt % 4, :].rearrange("p (k t) -> p k t", k=KT)
                    if XT is not None:
                        copy(XT[:, :, tt * P:(tt + 1) * P], bank)
                    copy(XNH[:, :, tt * P:(tt + 1) * P], bank, ln["hi"])

            consts = [(ident, "ident"), (identb, "identb"), (mask_ts, "mask_ts"), (mask_st, "mask_st"), (mask01, "mask01"),
                      (pick8, "pick8"), (shift_k, "shift_k"), (rope0c, "rope0c"), (rope0s, "rope0s"),
                      (rope2c, "rope2c"), (rope2s, "rope2s")]
            for t, name in consts:
                act.dma_start(t[tuple(slice(None) for _ in t.shape)], d[name]).then_inc(const_in, 16)
            normalise(0)
            for u in range(12):
                head_of(U_QKV0 + u, WQH[:, u, :])
            finish(act, 1)

            def attend(b):
                def stack_qk(j):
                    tl, is_k, pj = j // 2, j % 2, (0, 1, 3, 4)[j]
                    act.wait_ge(a["proj"], b * 6 + (pj + 1))
                    after(act, a["q"], b * 4 + j)
                    ps = PS[:, pj, :].rearrange("p (h d) -> p h d", h=H0)
                    copy(A_sw[:, :, 0:D0 // 2], ps[:, :, D0 // 2:D0])
                    copy(A_sw[:, :, D0 // 2:D0], ps[:, :, 0:D0 // 2], a["sw"])
                    act.wait_ge(a["q"], b * 4 + (j + 1))
                    after(act, a["tp"], b * 16 + 4 * j)
                    copy(STK[:, :, 0:D0].bitcast(F32R), A_q[:, :, :])
                    at = 2 * D0 if is_k else D0
                    copy(STK[:, :, at:at + D0].bitcast(F32R), A_q[:, :, :], a["hi"])
                    for x in (4 * j, 4 * j + 2):
                        act.wait_ge(a["tp"], b * 16 + (x + 1))
                        dst = (kT if is_k else qT)[:, (x % 4) * 4:(x % 4) * 4 + 4, tl * P:(tl + 1) * P]
                        copy(dst, PS[:, 6, :].rearrange("p (n t) -> p n t", n=4), a["eva"])

                def take_v(tl):
                    act.wait_ge(a["proj"], b * 6 + (3 * tl + 3))
                    copy(V0[:, tl, :, 0:D0], PS[:, 3 * tl + 2, :].rearrange("p (h d) -> p h d", h=H0), a["vcp"])

                after(act, a["pv"], b * 8)
                act.wait_ge(a["init"], 3)
                for tl in range(2):
                    stack_qk(2 * tl)
                    stack_qk(2 * tl + 1)
                    take_v(tl)

                def take_o(g):
                    act.wait_ge(a["pv"], b * 8 + (g + 1))
                    after(act, a["ot"], b * 8 + g)
                    copy(A_O[:, :], PS[:, 7, 0:SEQ], a["oev"])

                for g in range(G0):
                    if g >= 1:
                        take_o(g - 1)
                    act.wait_ge(a["mxt"], b * 8 + (g + 1))
                    after(act, a["shift"], b * 8 + g)
                    copy(A_mxT[:, :], PS[0:16, 0, 0:P // 2].bitcast(BF16), a["mxc"])
                    act.wait_ge(a["shift"], b * 8 + (g + 1))
                    after(act, a["pv"], b * 8 + g)
                    nc.scalar.activation(P0[:, :], PS[:, 4:7, :].rearrange("p n c -> p (n c)"), ACT.Exp,
                                         scale=float(D0) ** -0.5).then_inc(a["exp"], 1)
                take_o(G0 - 1)
                for tl in range(2):
                    act.wait_ge(a["ott"], b * 2 + (tl + 1))
                    after(act, a["wo_ps"], b * 2)
                    copy(OT0[:, :, tl * P:(tl + 1) * P], PS[:, tl, :].rearrange("p (k t) -> p k t", k=KT), a["otc"])

            attend(0)
            with act.Fori(1, NB) as b:
                attend(b)
            finish(act, 2)

            def ffn_heads(n, p, weights):
                for c in weights:
                    if not isinstance(n, int) or n >= 2:
                        act.wait_ge(*((f["dps"], n * 8 - 8) if c == 2 else (f["gu"], n * 2 - 2)))
                    act.wait_ge(f["w"], n * 3 + (c + 1))
                    copy(FWH[p][:, c, :], F_w[:, c, :], f["hi"])

            def ffn_gate(n, p):
                for h in range(2):
                    act.wait_ge(f["gu"], n * 2 + (h + 1))
                    if not isinstance(n, int) or n >= 1:
                        act.wait_ge(f["a"], n * 2 + (h - 1))
                    nc.scalar.activation(F_sg[:, h, :], PS[:, h, :], ACT.Sigmoid).then_inc(f["sg"], 1)
                if not isinstance(n, int) or n >= 2:
                    act.wait_ge(f["dps"], n * 8 - 8)
                for h in range(2):
                    act.wait_ge(f["i"], n * 2 + (h + 1))
                    copy(FIH[p][:, h * C:(h + 1) * C], F_i[:, h, :], f["ih"])

            def ffn_step(n, p):
                ffn_heads(n + 1, 1 - p, (0, 1))
                ffn_gate(n, p)
                ffn_heads(n + 1, 1 - p, (2,))

            ffn_heads(0, 0, (0, 1, 2))
            ffn_step(0, 0)
            with act.Fori(0, (NF - 3) // 2) as i:
                ffn_step(i * 2 + 1, 1)
                ffn_step(i * 2 + 2, 0)
            ffn_step(NF - 2, 1)
            ffn_gate(NF - 1, 0)
            finish(act, 3)

            for t, name in [(bv, "bv"), (bvr, "bvr"), (AG1, "ag1"), (BT1, "bt1"), (b1, "b1"), (gb1, "gb1")]:
                act.dma_start(t[tuple(slice(None) for _ in t.shape)], d[name]).then_inc(small_in, 16)
            for u in range(KT):
                head_of(U_W1 + u, W1H[:, u, :])
            normalise(1, XT1)
            finish(act, 4)
            for b in range(NB):
                s = 3 * (b % 2)
                act.wait_ge(c1["st"], b + 1)
                act.wait_ge(c1["pv"], 2 * b)
                nc.scalar.activation(A1[:, :], PS[:, s:s + 3, :].rearrange("p n c -> p (n c)"), ACT.Sigmoid,
                                     scale=4.0 * P ** -0.5).then_inc(c1["sig"], 1)
            for n in range(2):
                act.wait_ge(c1["lat_ps"], n + 1)
                copy(LAT[:, n * C:(n + 1) * C], PS[0:R1, 4 + n, :], c1["lat_cp"])
            finish(act, 5)

            for t, name in [(AR2, "ar2"), (coresT, "coresT"), (BwT, "bwT"), (b2, "b2")]:
                act.dma_start(t[tuple(slice(None) for _ in t.shape)], d[name]).then_inc(small_in, 16)
            for u in range(KT):
                head_of(U_WB2 + u, W2H[:, u, :])
            normalise(2, XT2)
            finish(act, 6)
            act.wait_ge(d2["g_ps"], 1)
            nc.scalar.activation(GH[:, :], PS[:, 5, :], ACT.Copy, scale=2.0).then_inc(d2["gh"], 1)
            act.wait_ge(d2["c"], 3)
            nc.scalar.activation(e_p[:, :, :], e_p[:, :, :], ACT.Exp).then_inc(d2["ax"], 1)
            for n in range(2):
                act.wait_ge(d2["tp"], n + 1)
                copy(UH[:, n * C:(n + 1) * C], PS[:, 6 + n, :], d2["uh"])
            finish(act, 7)

            def l2_heads(g, units):
                for u in units:
                    n = U_L2 + u
                    head(n % RAW, g * (U_L2_G // RAW) + (n // RAW + 1), E_WH[:, u, :])

            def l2_slot(g, j, step, one, two):
                i, p, q = g * NB + j, j % 2, 1 - j % 2
                if one:
                    act.wait_ge(e2["mxt"], i)
                    if two:
                        act.wait_ge(e2["shift"], i - 1)
                    copy(E_mxT[:, :], PS[0:16, 6, SEQ:SEQ + P // 2].bitcast(BF16), e2["mxc"])
                if step:
                    act.wait_ge(e2["proj"], i + 1)
                    act.wait_ge(e2["q"], i)
                    qk = PS[:, 3:6, :].rearrange("p n (h t) -> p (n h) t", h=2)
                    copy(E_sw[0:64, :, :], qk[64:P, 0:5, :])
                    copy(E_sw[64:P, :, :], qk[0:64, 0:5, :], e2["sw"])
                    act.wait_ge(e2["vtp"], i)
                    copy(vT2[:, :], qk[:, 5, :], e2["vt"])
                if one:
                    act.wait_ge(e2["shift"], i)
                    if two:
                        act.wait_ge(e2["plo"], i - 1)
                    nc.scalar.activation(E_p[:, :, :], PS[:, 0:3, :], ACT.Exp, scale=float(D2) ** -0.5).then_inc(e2["exp"], 1)
                if step:
                    act.wait_ge(e2["vtp"], i + 1)
                    if two:
                        act.wait_ge(e2["pv"], i * 2 - 2)
                    copy(VH[p][:, :, :], PS[:, 6, 0:SEQ].rearrange("p (s d) -> p s d", s=2), e2["vhi"])
                if one:
                    act.wait_ge(e2["exp"], i)
                    if two:
                        act.wait_ge(e2["pv"], i * 2 - 2)
                    copy(PH[:, :, :], E_p[:, :, :], e2["phi"])
                if step:
                    act.wait_ge(e2["q"], i + 1)
                    if two:
                        act.wait_ge(e2["shift"], i - 1)
                    copy(QKH[p][:, :, :], E_T[:, :, :], e2["qhi"])
                if one:
                    act.wait_ge(e2["pv"], i * 2)
                    if two:
                        act.wait_ge(e2["o"], i - 1)
                    nc.scalar.activation(E_r[:, :, :], PS[:, 5:7, :], ACT.Ln).then_inc(e2["ln"], 1)
                    act.wait_ge(e2["ln"], i)
                    nc.scalar.activation(E_r[:, :, :], E_r[:, :, :], ACT.Exp, scale=-1.0).then_inc(e2["r"], 1)
                    act.wait_ge(e2["o"], i)
                    if two:
                        act.wait_ge(e2["wo"], i * 2 - 4)
                    copy(OH[q][:, :, :], E_o[:, :, :], e2["ohi"])

            def l2_group(g, first, more):
                for j in range(NB):
                    l2_slot(g, j, True, not first or j >= 1, not first or j >= 2)
                    if j == 1:
                        if not first:
                            act.wait_ge(e2["wo"], g * 8)
                        l2_heads(g, range(6, U_L2_G))
                    if j == NB - 1 and more:
                        act.wait_ge(e2["proj"], g * NB + NB)
                        l2_heads(g + 1, range(6))

            l2_heads(0, range(6))
            l2_group(0, True, True)
            with act.Fori(1, KV2 - 1) as g:
                l2_group(g, False, True)
            l2_group(KV2 - 1, False, False)
            l2_slot(KV2, 0, False, True, True)
            finish(act, 8)

            for t, name in [(pk3, "pk3"), (zp3, "zp3"), (sc3, "sc3"), (b3, "b3")]:
                act.dma_start(t[tuple(slice(None) for _ in t.shape)], d[name]).then_inc(small_in, 16)
            for k in range(KT):
                act.wait_ge(f["w"], 3 * NF + k + 1)
                copy(W3H[:, k, :], t3[:, k, :], f["hi"])
            normalise(3)
            finish(act, 9)
            for t, name in [(bq3, "bq3"), (zc3, "zc3"), (pickf, "pickf")]:
                act.dma_start(t[tuple(slice(None) for _ in t.shape)], d[name]).then_inc(small_in, 16)
            for u in range(H3 + 2):
                head_of(U_L3 + u, L3H[:, u, :])
            act.wait_ge(small_in, SMALL_A3)
            act.wait_ge(g3["zm"], 1)
            copy(ZH[:, :, :].rearrange("p a b -> p (a b)")[:, 0:H3 * P:P + 1], zc3[:, :], g3["zh"])
            copy(pick3[:, :, :], pickf[:, :, :], g3["pk"])
            for h in range(H3):
                act.wait_ge(g3["s"], h + 1)
                copy(WSH[:, h, :], G_wo[:, :], g3["wsh"])
            def recall(b):
                for h in range(H3):
                    p, n = h % 2, b * H3 + h
                    act.wait_ge(g3["m"], n + 1)
                    after(act, g3["sum"], n)
                    nc.scalar.activation(G_e[:, :], G_m[:, :], ACT.Exp).then_inc(g3["e"], 1)
                    nc.scalar.activation(G_r[:, :], PS[:, p, 0:SEQ], ACT.Relu, bias=bq3[:, h:h + 1]).then_inc(g3["r"], 1)
                    act.wait_ge(g3["sum"], n + 1)
                    if h >= 2:
                        act.wait_ge(g3["nps"], b * H3 + (h - 1))
                    else:
                        after(act, g3["nps"], b * H3)
                    copy(SH[p][:, :], G_s[:, :], g3["shi"])
                    act.wait_ge(g3["nps"], n + 1)
                    if h == 0:
                        after(act, g3["nlo"], b * H3)
                    copy(num3[:, h, :], PS[:, 2 + p, 0:SEQ], g3["ncp"])
                act.wait_ge(g3["dc"], b * 2 + 2)
                after(act, g3["bps"], b * H3)
                copy(RH[:, :], den3[:, :], g3["rh"])
                for h in range(H3):
                    act.wait_ge(g3["mul"], b * H3 + (h + 1))
                    if h == 0:
                        after(act, g3["ops"], b * 2)
                    copy(NH3[:, h, :], num3[:, h, :], g3["nhi"])

            recall(0)
            with act.Fori(1, NB) as b:
                recall(b)
            finish(act, 10)

        @block.vector
        def _(dve):
            V = nc.vector

            def normalise(l, each=None):
                B = LN[l]
                if l == 0:
                    dve.wait_ge(x_in, 16 * TT)
                for tt in range(TT):
                    V.bn_stats(B["stats"][:, tt, :], X[:, tt, :]).then_inc(ln["stat"], 1)
                ln_wait(dve, l, "stat", TT)
                for tt in range(TT):
                    V.bn_aggr(B["mv"][:, tt, :], B["stats"][:, tt, :]).then_inc(ln["aggr"], 1)
                ln_wait(dve, l, "aggr", TT)
                V.tensor_scalar(B["var"][:, :], B["mv"][:, :, 1], 1e-5, None, ALU.add).then_inc(ln["var"], 1)
                ln_wait(dve, l, "sd", 1)
                V.reciprocal(B["tmp"][:, :], B["sd"][:, :]).then_inc(ln["c"], 1)
                ln_wait(dve, l, "c", 1)
                V.tensor_tensor(B["tmp"][:, :], B["tmp"][:, :], B["var"][:, :], ALU.mult).then_inc(ln["c"], 1)
                ln_wait(dve, l, "c", 2)
                V.tensor_tensor(B["tmp"][:, :], B["tmp"][:, :], B["sd"][:, :], ALU.add).then_inc(ln["c"], 1)
                ln_wait(dve, l, "c", 3)
                V.tensor_scalar(B["tmp"][:, :], B["tmp"][:, :], 0.5, None, ALU.mult).then_inc(ln["c"], 1)
                ln_wait(dve, l, "c", 4)
                V.reciprocal(B["rstd"][:, :], B["tmp"][:, :]).then_inc(ln["c"], 1)
                ln_wait(dve, l, "c", 5)

                def rests(tt):
                    ln_wait(dve, l, "hi", tt + 1)
                    span = slice(tt * P, (tt + 1) * P)
                    V.tensor_tensor(XNL[:, :, span], PS[:, tt % 4, :].rearrange("p (k t) -> p k t", k=KT),
                                    f32(XNH[:, :, span]), ALU.subtract).then_inc(ln["lo"], 1)

                for tt in range(TT):
                    if tt >= 2:
                        ln_wait(dve, l, "tp", tt - 1)
                    V.tensor_scalar(B["xn"][:, tt % 2, :], X[:, tt, :], B["mv"][:, tt, 0:1], B["rstd"][:, tt:tt + 1],
                                    ALU.subtract, ALU.mult).then_inc(ln["xn"], 1)
                    if each is not None:
                        ln_wait(dve, l, "xn", tt + 1)
                        each(tt, B["xn"][:, tt % 2, :])
                    if tt >= 1:
                        rests(tt - 1)
                rests(TT - 1)

            normalise(0)
            finish(dve, 1)

            dve.wait_ge(const_in, 16 * 11)
            def attend(b):
                for j in range(4):
                    tl, is_k, pj = j // 2, j % 2, (0, 1, 3, 4)[j]
                    dve.wait_ge(a["sw"], b * 4 + (j + 1))
                    V.tensor_tensor(A_T1[:, :, :], PS[:, pj, :].rearrange("p (h d) -> p h d", h=H0),
                                    rope0c[:, tl, :].unsqueeze(1).broadcast_to([P, H0, D0]), ALU.mult).then_inc(a["t1"], 1)
                    dve.wait_ge(a["t1"], b * 4 + (j + 1))
                    dve.wait_ge(a["t2"], b * 4 + (j + 1))
                    after(dve, a["hi"], b * 4 + j)
                    V.tensor_tensor(A_q[:, :, :], A_T1[:, :, :], A_sw[:, :, :], ALU.add).then_inc(a["q"], 1)
                    dve.wait_ge(a["hi"], b * 4 + (j + 1))
                    at = D0 if is_k else 2 * D0
                    V.tensor_tensor(STK[:, :, at:at + D0], A_q[:, :, :], STK[:, :, 0:D0], ALU.subtract).then_inc(a["lo"], 1)
                    for x in (4 * j + 1, 4 * j + 3):
                        dve.wait_ge(a["tp"], b * 16 + (x + 1))
                        dst = (kT if is_k else qT)[:, (x % 4) * 4:(x % 4) * 4 + 4, tl * P:(tl + 1) * P]
                        V.tensor_copy(dst, PS[:, 7, :].rearrange("p (n t) -> p n t", n=4)).then_inc(a["evd"], 1)

                def divide(g):
                    dve.wait_ge(a["ot"], b * 8 + (g + 1))
                    o = PS[:, 7, SEQ:2 * SEQ].rearrange("p (t h d) -> p t h d", t=2, h=4)
                    V.reciprocal(A_rec[:, :, :], o[:, :, :, D0]).then_inc(a["rec"], 1)
                    dve.wait_ge(a["rec"], b * 8 + (g + 1))
                    for tl in range(2):
                        V.tensor_tensor(Otok[:, tl, 4 * g:4 * g + 4, :], o[:, tl, :, 0:D0],
                                        A_rec[:, tl, :].unsqueeze(2).broadcast_to([P, 4, D0]), ALU.mult).then_inc(a["otok"], 1)

                after(dve, a["ott"], b * 2)
                for g in range(G0):
                    for tb in range(2):
                        dve.wait_ge(a["max"], b * 16 + (2 * g + tb + 1))
                        V.tensor_reduce(A_mx[:, 4 * tb:4 * tb + 4],
                                        PS[:, 2 * tb:2 * tb + 2, :].rearrange("p n (h s) -> p (n h) s", h=2)[:, :, 0:(tb + 1) * P],
                                        AXIS.X, ALU.max).then_inc(a["red"], 1)
                    dve.wait_ge(a["red"], b * 16 + (2 * g + 2))
                    after(dve, a["mxt"], b * 8 + g)
                    V.tensor_scalar(A_mxs[:, 0:8], A_mx[:, :], -1.0, None, ALU.mult).then_inc(a["neg"], 1)
                    dve.wait_ge(a["neg"], b * 8 + (g + 1))
                    V.scalar_tensor_tensor(A_mxs[:, 8:16], A_mx[:, :], -1.0, A_mxs[:, 0:8], ALU.mult, ALU.subtract)\
                     .then_inc(a["mxs"], 1)
                    if g >= 1:
                        divide(g - 1)
                divide(G0 - 1)
                for tl in range(2):
                    dve.wait_ge(a["wo_ps"], b * 2 + (tl + 1))
                    xt = X[:, bass.ds(b * 2 + tl, 1), :].rearrange("p a c -> p (a c)")
                    V.tensor_tensor(xt, xt, PS[:, 2 + tl, :], ALU.add).then_inc(a["x"], 1)

            attend(0)
            with dve.Fori(1, NB) as b:
                attend(b)
            finish(dve, 2)

            dve.wait_ge(f["zin"], 32)
            V.tensor_tensor(zq[:, :].rearrange("p (w e) -> p w e", e=8), zw[:, :].unsqueeze(2).broadcast_to([NF, 3 * C // 8, 8]),
                            zshift[:, :].unsqueeze(1).broadcast_to([NF, 3 * C // 8, 8]), ALU.logical_shift_right).then_inc(f["z"], 1)
            dve.wait_ge(f["z"], 1)
            V.tensor_scalar(zq[:, :], zq[:, :], 15, None, ALU.bitwise_and).then_inc(f["z"], 1)
            dve.wait_ge(f["z"], 2)
            V.tensor_scalar(z1[:, :], zq[:, :], 1, None, ALU.add).then_inc(f["z"], 1)
            V.memset(F_acc[:, :, :], 0.0).then_inc(f["z"], 1)

            def unpack(n, p):
                dve.wait_ge(f[f"in{p}"], in_count(n, p))
                for c in range(3):
                    if not isinstance(n, int) or n >= 1:
                        dve.wait_ge(f["w"], n * 3 + (c - 2))
                    if c or not isinstance(n, int) or n >= 1:
                        dve.wait_ge(f["t"], n * 3 + c)
                    V.tensor_scalar(F_q[:, :], words[p][:, c, :], shift_k[:, 0:1], 15, ALU.logical_shift_right, ALU.bitwise_and)\
                     .then_inc(f["q"], 1)
                    dve.wait_ge(f["q"], n * 3 + (c + 1))
                    V.tensor_tensor(F_t[:, c, :], F_q[:, :], zb[p][:, c, :], ALU.subtract).then_inc(f["t"], 1)

            LOADS = 3 * 8 + 2

            def in_count(n, p):
                if isinstance(n, int):
                    return 16 * LOADS * (n // 2 + 1)
                return n * (8 * LOADS) + (8 * LOADS if p else 16 * LOADS)

            def weight_rests(n, p, weights):
                for c in weights:
                    dve.wait_ge(f["hi"], n * 3 + (c + 1))
                    V.tensor_tensor(FWL[p][:, c, :], F_w[:, c, :], f32(FWH[p][:, c, :]), ALU.subtract).then_inc(f["lo"], 1)

            def gated(n, p):
                for h in range(2):
                    dve.wait_ge(f["sg"], n * 2 + (h + 1))
                    V.tensor_tensor(F_a[:, h, :], F_sg[:, h, :], PS[:, h, :], ALU.mult).then_inc(f["a"], 1)
                    dve.wait_ge(f["a"], n * 2 + (h + 1))
                    V.tensor_tensor(F_i[:, h, :], F_a[:, h, :], PS[:, 2 + h, :], ALU.mult).then_inc(f["i"], 1)

            def gated_rests(n, p):
                for h in range(2):
                    dve.wait_ge(f["ih"], n * 2 + (h + 1))
                    V.tensor_tensor(FIL[p][:, h * C:(h + 1) * C], F_i[:, h, :], f32(FIH[p][:, h * C:(h + 1) * C]),
                                    ALU.subtract).then_inc(f["il"], 1)

            def accumulate(n):
                dve.wait_ge(f["z"], 4)
                for tt in range(TT):
                    dve.wait_ge(f["dps"], n * 8 + (tt + 1))
                    V.tensor_tensor(F_acc[:, tt, :], F_acc[:, tt, :], PS[:, 4 + tt % 4, :], ALU.add).then_inc(f["acc"], 1)

            def ffn_step(n, p, m=None):
                unpack(n + 1, 1 - p)
                weight_rests(n + 1, 1 - p, (0, 1))
                gated(n, p)
                if m is not None:
                    accumulate(m)
                gated_rests(n, p)
                weight_rests(n + 1, 1 - p, (2,))

            unpack(0, 0)
            weight_rests(0, 0, (0, 1, 2))
            ffn_step(0, 0)
            with dve.Fori(0, (NF - 3) // 2) as i:
                ffn_step(i * 2 + 1, 1, i * 2)
                ffn_step(i * 2 + 2, 0, i * 2 + 1)
            ffn_step(NF - 2, 1, NF - 3)
            gated(NF - 1, 0)
            gated_rests(NF - 1, 0)
            accumulate(NF - 2)
            accumulate(NF - 1)
            dve.wait_ge(f["acc"], NF * TT)
            for tt in range(TT):
                V.tensor_copy(F_half[:, tt, :], F_acc[:, tt, :]).then_inc(f["half"], 1)
            for tt in range(TT):
                dve.wait_ge(f["half"], tt + 1)
                V.tensor_tensor(X[:, tt, :], X[:, tt, :], F_half[:, tt, :], ALU.add).then_inc(f["x"], 1)
            finish(dve, 3)

            count = [0]

            def chain(ins, signal):
                count[0] += 1
                ins.then_inc(signal, 1)
                dve.wait_ge(signal, count[0])

            dve.wait_ge(small_in, SMALL_L1)
            V.scalar_tensor_tensor(bv_abs[:, :], bv[:, :], -1.0, bv[:, :], ALU.mult, ALU.max).then_inc(c1["abs"], 1)
            chain(V.scalar_tensor_tensor(vrow[:, :, :], bvr[:, :, :], -1.0, bvr[:, :, :], ALU.mult, ALU.max), c1["c"])
            chain(V.tensor_reduce(vr_al[:, :], vrow[:, :, :], AXIS.X, ALU.add), c1["c"])
            chain(V.tensor_scalar(vr_al[:, :], vr_al[:, :], 1.0 / P, None, ALU.mult), c1["c"])
            chain(V.tensor_scalar(vr_sg[:, :, :], bvr[:, :, :], 0.0, 2.0, ALU.is_ge, ALU.mult), c1["c"])
            chain(V.tensor_scalar(vr_sg[:, :, :], vr_sg[:, :, :], -1.0, None, ALU.add), c1["c"])
            chain(V.tensor_tensor(vr_sg[:, :, :], vr_sg[:, :, :], vr_al[:, :].unsqueeze(2).broadcast_to([P, 4, P]), ALU.mult), c1["c"])
            chain(V.tensor_tensor(vr_sg[:, :, :], vr_sg[:, :, :], bvr[:, :, :], ALU.subtract), c1["c"])
            chain(V.tensor_tensor(vrow[:, :, :], vr_sg[:, :, :], bvr[:, :, :], ALU.add), c1["c"])
            chain(V.tensor_scalar(bv_sg[:, :], bv[:, :], 0.0, 2.0, ALU.is_ge, ALU.mult), c1["c"])
            dve.wait_ge(c1["al"], 1)
            chain(V.scalar_tensor_tensor(bv_sg[:, :], bv_sg[:, :], -1.0, PS[:, 7, 0:12], ALU.add, ALU.mult), c1["c"])
            chain(V.tensor_tensor(bv_sg[:, :], bv_sg[:, :], bv[:, :], ALU.subtract), c1["c"])
            chain(V.tensor_tensor(bv_q[:, :], bv_sg[:, :], bv[:, :], ALU.add), c1["c"])
            chain(V.tensor_tensor(qk1[:, :], bv_q[:, 0:4], bv_q[:, 4:8], ALU.mult), c1["c"])
            normalise(1, lambda tt, xn: V.tensor_tensor(V1[:, tt, :], xn, vrow[:, :, :].rearrange("p h e -> p (h e)"), ALU.mult)
                      .then_inc(c1["v"], 1))
            ln_wait(dve, 1, "hi", TT)
            for k in range(KT):
                V.tensor_scalar(K1[:, k, :], XT1[:, k, :], qk1[:, k:k + 1], None, ALU.mult).then_inc(c1["k1"], 1)
            finish(dve, 4)

            dve.wait_ge(c1["lo_ps"], 2)
            count[0] = 0
            for n in range(2):
                last = V.tensor_copy(LA[:, 4 * n:4 * n + 4, :],
                                     PS[:, 6 + n, 0:4 * (R1 + E1)].rearrange("p (t r) -> p t r", t=4))
            chain(last, c1["gate"])
            gs = LA[:, :, R1:R1 + E1]
            chain(V.tensor_tensor(gs, gs, gb1[:, :].unsqueeze(1).broadcast_to([P, TT, E1]), ALU.add), c1["gate"])
            chain(V.tensor_reduce(g_m[:, :], gs, AXIS.X, ALU.max), c1["gate"])
            chain(V.tensor_tensor(g_ne[:, :, :], gs, g_m[:, :].unsqueeze(2).broadcast_to([P, TT, E1]), ALU.is_lt), c1["gate"])
            for k in range(3):
                if k:
                    chain(V.tensor_tensor(g_ne[:, :, k], g_ne[:, :, k], g_ne[:, :, k - 1], ALU.mult), c1["gate"])
                r = 8 << k
                chain(V.tensor_tensor(LA[:, :, r:2 * r], LA[:, :, r:2 * r],
                                      g_ne[:, :, k].unsqueeze(2).broadcast_to([P, TT, r]), ALU.mult), c1["gate"])
            gates = count[0]
            assert gates == 9
            for b in range(NB):
                dve.wait_ge(c1["sig"], b + 1)
                w0 = A1[:, 0:1024].rearrange("p (h t) -> p h t", h=4)[:, :, 0:P]
                w1 = A1[:, 1024:1536].rearrange("p (h t) -> p h t", h=4)
                seen = mask01[:, :].unsqueeze(1).broadcast_to([P, 4, P])
                V.tensor_tensor(w0, w0, seen, ALU.mult)
                V.tensor_tensor(w1, w1, seen, ALU.mult).then_inc(c1["mask"], 1)
                for tb in range(2):
                    tt = 2 * b + tb
                    dve.wait_ge(c1["pv"], tt + 1)
                    dve.wait_ge(bias_in, tt + 1)
                    V.tensor_tensor(X[:, tt, :], X[:, tt, :], PS[:, 6 + tb, :], ALU.add).then_inc(c1["xa"], 1)
            for tt in range(TT):
                dve.wait_ge(ffn_ps, tt + 1)
                dve.wait_ge(c1["xa"], tt + 1)
                V.tensor_tensor(X[:, tt, :], X[:, tt, :], PS[:, tt % 4, :], ALU.add).then_inc(ffn_x, 1)
            finish(dve, 5)

            normalise(2)
            finish(dve, 6)
            dve.wait_ge(d2["gh"], 1)
            V.scalar_tensor_tensor(GL[:, :], PS[:, 5, :], 2.0, f32(GH[:, :]), ALU.mult, ALU.subtract).then_inc(d2["gl"], 1)
            dve.wait_ge(d2["lo_ps"], 1)
            count[0] = 0
            chain(V.tensor_copy(axr[:, :, :], PS[:, 4, 0:TT * (R2 + E2)].rearrange("p (t r) -> p t r", t=TT)), d2["c"])
            chain(V.tensor_reduce(e_m[:, :], axr[:, :, R2:R2 + E2], AXIS.X, ALU.max), d2["c"])
            chain(V.tensor_tensor(e_p[:, :, :], axr[:, :, R2:R2 + E2], e_m[:, :].unsqueeze(2).broadcast_to([P, TT, E2]),
                                  ALU.subtract), d2["c"])
            dve.wait_ge(d2["ax"], 1)
            chain(V.tensor_reduce(e_s[:, :], e_p[:, :, :], AXIS.X, ALU.add), d2["c"])
            chain(V.reciprocal(e_s[:, :], e_s[:, :]), d2["c"])
            chain(V.tensor_tensor(e_p[:, :, :], e_p[:, :, :], e_s[:, :].unsqueeze(2).broadcast_to([P, TT, E2]), ALU.mult), d2["c"])
            for tt in range(TT):
                last = V.tensor_tensor(U2[:, tt, :, :], e_p[:, tt, :].unsqueeze(2).broadcast_to([P, E2, R2]),
                                       axr[:, tt, 0:R2].unsqueeze(1).broadcast_to([P, E2, R2]), ALU.mult)
            chain(last, d2["c"])
            assert count[0] == 7
            for n in range(2):
                dve.wait_ge(d2["uh"], n + 1)
                V.tensor_tensor(UL[:, n * C:(n + 1) * C], PS[:, 6 + n, :], f32(UH[:, n * C:(n + 1) * C]), ALU.subtract)\
                 .then_inc(d2["ul"], 1)
            for tt in range(TT):
                dve.wait_ge(ffn_ps, TT + tt + 1)
                dve.wait_ge(bias_in, TT + tt + 1)
                V.tensor_tensor(X[:, tt, :], X[:, tt, :], PS[:, tt % 4, :], ALU.add).then_inc(ffn_x, 1)
            finish(dve, 7)

            def add_branch(i, b, tb):
                dve.wait_ge(e2["wo"], i * 2 + (tb - 3))
                tt = 2 * b + tb
                V.tensor_tensor(X[:, tt, :], X[:, tt, :], PS[:, 7, :], ALU.add).then_inc(e2["x"], 1)

            def l2_slot(g, j, step, one, two):
                i, p, q = g * NB + j, j % 2, 1 - j % 2
                b2_ = (j - 2) % NB
                if one:
                    for tb in range(2):
                        dve.wait_ge(e2["max"], i * 2 + (tb - 1))
                        V.tensor_reduce(E_mx[:, 4 * tb:4 * tb + 4],
                                        PS[:, 3 + 2 * tb:5 + 2 * tb, :].rearrange("p n (h s) -> p (n h) s", h=2)[:, :, 0:(tb + 1) * P],
                                        AXIS.X, ALU.max).then_inc(e2["red"], 1)
                    dve.wait_ge(e2["red"], i * 2)
                    if two:
                        dve.wait_ge(e2["mxt"], i - 1)
                    V.tensor_scalar(E_mxs[:, 0:8], E_mx[:, :], -1.0, None, ALU.mult).then_inc(e2["neg"], 1)
                    dve.wait_ge(e2["neg"], i)
                    V.scalar_tensor_tensor(E_mxs[:, 8:16], E_mx[:, :], -1.0, E_mxs[:, 0:8], ALU.mult, ALU.subtract)\
                     .then_inc(e2["mxs"], 1)
                if step:
                    dve.wait_ge(e2["vt"], i + 1)
                    dve.wait_ge(e2["qhi"], i)
                    V.tensor_tensor(E_T[:, :, :], PS[:, 3:6, :].rearrange("p n (h t) -> p (n h) t", h=2)[:, 0:5, :],
                                    rope2c[:, :].unsqueeze(1).broadcast_to([P, 5, SEQ]), ALU.mult).then_inc(e2["t1"], 1)
                    dve.wait_ge(e2["t1"], i + 1)
                    dve.wait_ge(e2["t2"], i + 1)
                    V.tensor_tensor(E_T[:, :, :], E_T[:, :, :], E_sw[:, :, :], ALU.add).then_inc(e2["q"], 1)
                if one:
                    dve.wait_ge(e2["phi"], i)
                    V.tensor_tensor(PL[:, :, :], E_p[:, :, :], f32(PH[:, :, :]), ALU.subtract).then_inc(e2["plo"], 1)
                if step:
                    dve.wait_ge(e2["vhi"], i + 1)
                    V.tensor_tensor(VL[p][:, :, :], PS[:, 6, 0:SEQ].rearrange("p (s d) -> p s d", s=2), f32(VH[p][:, :, :]),
                                    ALU.subtract).then_inc(e2["vlo"], 1)
                    dve.wait_ge(e2["qhi"], i + 1)
                    V.tensor_tensor(QKL[p][:, :, :], E_T[:, :, :], f32(QKH[p][:, :, :]), ALU.subtract).then_inc(e2["qlo"], 1)
                if two:
                    add_branch(i, b2_, 0)
                if one:
                    dve.wait_ge(e2["r"], i)
                    V.tensor_tensor(E_t[:, :, :], E_r[:, :, :], PS[:, 5:7, :], ALU.mult).then_inc(e2["t"], 1)
                    if two:
                        dve.wait_ge(e2["ohi"], i - 1)
                    V.tensor_tensor(E_o[:, :, :], E_r[:, :, :], PS[:, 3:5, :], ALU.mult).then_inc(e2["u"], 1)
                    dve.wait_ge(e2["t"], i)
                    dve.wait_ge(e2["u"], i)
                    V.scalar_tensor_tensor(E_o[:, :, :], E_t[:, :, :], 2.0, E_o[:, :, :], ALU.subtract, ALU.mult,
                                           reverse0=True).then_inc(e2["o"], 1)
                    dve.wait_ge(e2["ohi"], i)
                    V.tensor_tensor(OL[q][:, :, :], E_o[:, :, :], f32(OH[q][:, :, :]), ALU.subtract).then_inc(e2["olo"], 1)
                if two:
                    add_branch(i, b2_, 1)

            for j in range(NB):
                l2_slot(0, j, True, j >= 1, j >= 2)
            with dve.Fori(1, KV2) as g:
                for j in range(NB):
                    l2_slot(g, j, True, True, True)
            l2_slot(KV2, 0, False, True, True)
            l2_slot(KV2, 1, False, False, True)
            finish(dve, 8)

            dve.wait_ge(small_in, SMALL_F3)
            for k in range(KT):
                V.tensor_scalar(q3[:, k, :], pk3[:, k // 2, :], 4 * (k % 2), 15, ALU.logical_shift_right, ALU.bitwise_and)\
                 .then_inc(f["q"], 1)
            for k in range(KT):
                dve.wait_ge(f["q"], 3 * NF + k + 1)
                V.tensor_tensor(t3[:, k, :], q3[:, k, :], zp3[:, :], ALU.subtract).then_inc(f["t"], 1)
            for k in range(KT):
                dve.wait_ge(f["hi"], 3 * NF + k + 1)
                V.tensor_tensor(W3L[:, k, :], t3[:, k, :], f32(W3H[:, k, :]), ALU.subtract).then_inc(f["lo"], 1)
            normalise(3)
            for tt in range(TT):
                dve.wait_ge(ffn_ps, 2 * TT + tt + 1)
                dve.wait_ge(bias_in, 2 * TT + tt + 1)
                V.tensor_tensor(X[:, tt, :], X[:, tt, :], PS[:, 4 + tt % 4, :], ALU.add).then_inc(ffn_x, 1)
            finish(dve, 9)
            V.memset(f32(ZH[:, :, :]), 0.0)
            V.memset(f32(ZL[:, :, :]), 0.0).then_inc(g3["zm"], 1)
            dve.wait_ge(g3["zm"], 1)
            dve.wait_ge(g3["zh"], 1)
            diag = (slice(None), slice(0, H3 * P, P + 1))
            V.tensor_tensor(ZL[:, :, :].rearrange("p a b -> p (a b)")[diag], zc3[:, :],
                            f32(ZH[:, :, :].rearrange("p a b -> p (a b)")[diag]), ALU.subtract).then_inc(g3["zl"], 1)
            def recall(b):
                for h in range(H3):
                    p, n = h % 2, b * H3 + h
                    dve.wait_ge(g3["qps"], n + 1)
                    dve.wait_ge(g3["e"], n)
                    V.tensor_scalar(G_m[:, :], PS[:, p, 0:SEQ], bq3[:, h:h + 1], 0.0, ALU.add, ALU.min).then_inc(g3["m"], 1)
                    dve.wait_ge(g3["e"], n + 1)
                    dve.wait_ge(g3["r"], n + 1)
                    dve.wait_ge(g3["shi"], n)
                    V.tensor_tensor(G_s[:, :], G_e[:, :], G_r[:, :], ALU.add).then_inc(g3["sum"], 1)
                    dve.wait_ge(g3["shi"], n + 1)
                    V.tensor_tensor(SL[p][:, :], G_s[:, :], f32(SH[p][:, :]), ALU.subtract).then_inc(g3["slo"], 1)
                dve.wait_ge(g3["nps"], b * H3 + H3)
                after(dve, g3["rl"], b)
                after(dve, g3["rh"], b)
                V.tensor_scalar(den3[:, :], PS[0:H3, 4, 0:SEQ], 1e-6, None, ALU.add).then_inc(g3["dc"], 1)
                dve.wait_ge(g3["dc"], b * 2 + 1)
                V.reciprocal(den3[:, :], den3[:, :]).then_inc(g3["dc"], 1)
                dve.wait_ge(g3["rh"], b + 1)
                V.tensor_tensor(RL[:, :], den3[:, :], f32(RH[:, :]), ALU.subtract).then_inc(g3["rl"], 1)
                for h in range(H3):
                    n = b * H3 + h
                    dve.wait_ge(g3["bps"], n + 1)
                    dve.wait_ge(g3["ncp"], n + 1)
                    V.tensor_tensor(num3[:, h, :], num3[:, h, :], PS[:, 5 + h % 2, 0:SEQ], ALU.mult).then_inc(g3["mul"], 1)
                    dve.wait_ge(g3["nhi"], n + 1)
                    V.tensor_tensor(NL3[:, h, :], num3[:, h, :], f32(NH3[:, h, :]), ALU.subtract).then_inc(g3["nlo"], 1)
                for tl in range(2):
                    dve.wait_ge(g3["ops"], b * 2 + (tl + 1))
                    xt = X[:, bass.ds(b * 2 + tl, 1), :].rearrange("p a c -> p (a c)")
                    V.tensor_tensor(xt, xt, PS[:, 6 + tl, :], ALU.add).then_inc(g3["xo"], 1)

            recall(0)
            with dve.Fori(1, NB) as b:
                recall(b)
            finish(dve, 10)

        @block.tensor
        def _(pe):
            mm = nc.tensor.matmul

            def normalise(l, pairs=False):
                xn = LN[l]["xn"]
                for tt in range(TT):
                    ln_wait(pe, l, "xn", tt + 1)
                    if tt >= 4:
                        ln_wait(pe, l, "lo", tt - 3)
                    for k in range(KT):
                        src = xn[:, tt % 2, k * P:(k + 1) * P]
                        if pairs:
                            at = (k // 2) * 2 * P + k % 2
                            src = xn[:, tt % 2, at:at + 2 * P - 1:2]
                        last = nc.tensor.transpose(PS[:, tt % 4, k * P:(k + 1) * P], src, ident[:, :])
                    last.then_inc(ln["tp"], 1)

            pe.wait_ge(const_in, 16 * 11)
            normalise(0)
            finish(pe, 1)

            pe.wait_ge(w_lo, 12)
            pe.wait_ge(x_in, 16 * (TT + KT))
            pe.wait_ge(a["init"], 3)
            def attend(b):
                after(pe, a["x"], b * 2)
                pe.wait_ge(a["stage"], b * 32 + 32)
                for pj in range(6):
                    tl, w = pj // 3, pj % 3
                    for k in range(KT):
                        span = slice(tl * P, (tl + 1) * P)
                        last = product3(PS[:, pj, :], SGH[:, k, span], SGL[:, k, span], WQH[:, 4 * w + k, :],
                                        WQL[:, 4 * w + k, :], k == 0, k == KT - 1)
                    last.then_inc(a["proj"], 1)
                for j in range(4):
                    pe.wait_ge(a["lo"], b * 4 + (j + 1))
                    for x in range(4 * j, 4 * j + 4):
                        if x >= 2:
                            pe.wait_ge(a["evd" if x % 2 else "eva"], b * 8 + x // 2)
                        for n in range(4):
                            pair = (x % 4) * 4 + n
                            last = nc.tensor.transpose(PS[:, 6 + x % 2, n * P:(n + 1) * P],
                                                       STK[:, 2 * pair:2 * pair + 2, :].rearrange("p h r -> p (h r)"), ident[:, :])
                        last.then_inc(a["tp"], 1)
                pe.wait_ge(a["eva"], b * 8 + 8)
                pe.wait_ge(a["evd"], b * 8 + 8)
                pe.wait_ge(a["vcp"], b * 2 + 2)

                def rows(g, h):
                    n = 4 * g + h
                    return slice((n % 2) * S0, (n % 2 + 1) * S0), n // 2

                def place(h):
                    return (h % 2) * 2 + h // 2

                def weighted_values(g):
                    pe.wait_ge(a["exp"], b * 8 + (g + 1))
                    after(pe, a["oev"], b * 8 + g)
                    after(pe, a["otok"], b * 16 + 2 * g)
                    for h in range(4):
                        o = slice(32 * h, 32 * h + 32)
                        n = 4 * g + h
                        mm(PS[o, 7, 0:SEQ], V0[:, 0, n, :], P0[:, place(h) * SEQ:(place(h) + 1) * SEQ], start=True, stop=False,
                           skip_group_check=True, tile_position=(0, 32 * h))
                        last = mm(PS[o, 7, P:SEQ], V0[:, 1, n, :], P0[:, 1024 + h * P:1024 + (h + 1) * P], start=False, stop=True,
                                  skip_group_check=True, tile_position=(0, 32 * h))
                    last.then_inc(a["pv"], 1)

                def output_rows(g):
                    pe.wait_ge(a["oev"], b * 8 + (g + 1))
                    after(pe, a["otok"], b * 16 + 2 * g)
                    for tl in range(2):
                        last = nc.tensor.transpose(PS[:, 7, SEQ + tl * P:SEQ + (tl + 1) * P], A_O[:, tl * P:(tl + 1) * P], ident[:, :])
                    last.then_inc(a["ot"], 1)

                for g in range(G0):
                    after(pe, a["red"], b * 16 + 2 * g)
                    after(pe, a["mxc"], b * 8 + g)
                    for tb in range(2):
                        for h in range(4):
                            r, n = rows(g, h)
                            at = (h // 2) * SEQ
                            bank = 2 * tb + h % 2
                            mm(PS[:, bank, at:at + SEQ], qT[r, n, tb * P:(tb + 1) * P], kT[r, n, :], start=True, stop=False,
                               skip_group_check=True)
                            last = mm(PS[:, bank, at + tb * P:at + (tb + 1) * P], identb[:, :], mask_ts[:, :], start=False, stop=True,
                                      skip_group_check=True)
                        last.then_inc(a["max"], 1)
                    after(pe, a["exp"], b * 8 + g)
                    for h in range(4):
                        r, n = rows(g, h)
                        mm(PS[:, 4 + h % 2, (h // 2) * SEQ:(h // 2 + 1) * SEQ], kT[r, n, 0:P], qT[r, n, :], start=(h < 2), stop=False,
                           skip_group_check=True)
                    for h in (0, 2):
                        r, n = rows(g, h)
                        last = mm(PS[:, 6, h * P:(h + 1) * P], kT[r, n, P:SEQ], qT[r, n, P:SEQ], start=(h == 0), stop=False,
                                  skip_group_check=True)
                    last.then_inc(a["s1"], 1)
                    for h in range(4):
                        mm(PS[:, 4 + h % 2, (h // 2) * SEQ:(h // 2) * SEQ + P], identb[:, :], mask_st[:, 0, :], start=False, stop=False,
                           skip_group_check=True)
                    if g >= 1:
                        weighted_values(g - 1)
                    pe.wait_ge(a["s1"], b * 8 + (g + 1))
                    for h in (1, 3):
                        r, n = rows(g, h)
                        mm(PS[:, 6, h * P:(h + 1) * P], kT[r, n, P:SEQ], qT[r, n, P:SEQ], start=False, stop=False, skip_group_check=True)
                    mm(PS[:, 6, :], identb[:, :], mask_st[:, :, :], start=False, stop=False, skip_group_check=True)
                    pe.wait_ge(a["mxs"], b * 8 + (g + 1))
                    nc.tensor.transpose(PS[0:16, 0, 0:P // 2].bitcast(BF16), A_mxs[:, :], identb[:, :]).then_inc(a["mxt"], 1)
                    pe.wait_ge(a["mxc"], b * 8 + (g + 1))
                    for h in range(4):
                        for tb in range(2):
                            at = (h // 2) * SEQ + tb * P
                            mm(PS[:, 4 + h % 2, at:at + P], pick8[:, 4 * tb + place(h), :], A_mxT[:, :], start=False, stop=True,
                               skip_group_check=True)
                        last = mm(PS[:, 6, h * P:(h + 1) * P], pick8[:, 4 + place(h), :], A_mxT[:, :], start=False, stop=True,
                                  skip_group_check=True)
                    last.then_inc(a["shift"], 1)
                    if g >= 1:
                        output_rows(g - 1)
                weighted_values(G0 - 1)
                output_rows(G0 - 1)
                pe.wait_ge(a["otok"], b * 16 + 16)
                for tl in range(2):
                    for k in range(KT):
                        last = nc.tensor.transpose(PS[:, tl, k * P:(k + 1) * P],
                                                   Otok[:, tl, 8 * k:8 * k + 8, :].rearrange("p h d -> p (h d)"), ident[:, :])
                    last.then_inc(a["ott"], 1)
                for tl in range(2):
                    pe.wait_ge(a["otc"], b * 2 + (tl + 1))
                    for k in range(KT):
                        last = mm(PS[:, 2 + tl, :], OT0[:, k, tl * P:(tl + 1) * P], wo0[:, k, :], start=(k == 0), stop=(k == KT - 1))
                    last.then_inc(a["wo_ps"], 1)

            attend(0)
            with pe.Fori(1, NB) as b:
                attend(b)
            finish(pe, 2)

            def gate_up(n, p):
                if not isinstance(n, int) or n >= 1:
                    pe.wait_ge(f["i"], n * 2)
                pe.wait_ge(f["lo"], n * 3 + 2)
                for h in range(2):
                    for c in range(2):
                        for k in range(KT):
                            span, half = slice(k * P, (k + 1) * P), slice(h * C, (h + 1) * C)
                            last = product3(PS[:, 2 * c + h, :], FWH[p][:, c, span], FWL[p][:, c, span], XNH[:, k, half], XNL[:, k, half],
                                            k == 0, k == KT - 1)
                    last.then_inc(f["gu"], 1)

            def down(n, p, first=False):
                pe.wait_ge(f["lo"], n * 3 + 3)
                pe.wait_ge(f["il"], n * 2 + 2)
                for tt in range(TT):
                    if not first or tt >= 4:
                        pe.wait_ge(f["acc"], n * 8 + (tt - 3))
                    span = slice(tt * P, (tt + 1) * P)
                    product3(PS[:, 4 + tt % 4, :], FIH[p][:, span], FIL[p][:, span], FWH[p][:, 2, :], FWL[p][:, 2, :], True, True)\
                        .then_inc(f["dps"], 1)

            gate_up(0, 0)
            gate_up(1, 1)
            down(0, 0, True)
            gate_up(2, 0)
            down(1, 1)
            with pe.Fori(1, (NF - 1) // 2) as i:
                gate_up(i * 2 + 1, 1)
                down(i * 2, 0)
                gate_up(i * 2 + 2, 0)
                down(i * 2 + 1, 1)
            down(NF - 1, 0)
            finish(pe, 3)

            pe.wait_ge(a["init"], 4)
            pe.wait_ge(c1["abs"], 1)
            mm(PS[:, 7, 0:12], inv[:, :], bv_abs[:, :], start=True, stop=True).then_inc(c1["al"], 1)
            normalise(1)
            finish(pe, 4)
            for tt in range(TT):
                n = tt // 4
                at = (tt % 4) * (R1 + E1)
                for k in range(KT):
                    last = mm(PS[:, 6 + n, at:at + R1 + E1], XT1[:, k, tt * P:(tt + 1) * P], AG1[:, k, :], start=(k == 0),
                              stop=(k == KT - 1), skip_group_check=True)
                if tt % 4 == 3:
                    last.then_inc(c1["lo_ps"], 1)

            def l1_scores(b):
                s = 3 * (b % 2)
                if b >= 2:
                    pe.wait_ge(c1["sig"], b - 1)
                t0 = b * SEQ
                for h in range(4):
                    mm(PS[:, s + h // 2, (h % 2) * SEQ:(h % 2 + 1) * SEQ], K1[:, h, t0:t0 + P], XT1[:, h, t0:t0 + SEQ], start=True, stop=True,
                       skip_group_check=True)
                for h in range(4):
                    last = mm(PS[:, s + 2, h * P:(h + 1) * P], K1[:, h, t0 + P:t0 + SEQ], XT1[:, h, t0 + P:t0 + SEQ], start=True, stop=True,
                              skip_group_check=True)
                last.then_inc(c1["st"], 1)

            def l1_values(b):
                pe.wait_ge(c1["mask"], b + 1)
                pe.wait_ge(c1["gate"], 1)
                if b >= 1:
                    pe.wait_ge(c1["xa"], 2 * b)
                for tb in range(2):
                    for h in range(4):
                        o = PS[:, 6 + tb, h * P:(h + 1) * P]
                        last = mm(o, A1[:, h * SEQ + tb * P:h * SEQ + (tb + 1) * P], V1[:, 2 * b, h * P:(h + 1) * P], start=True, stop=(tb == 0),
                                  skip_group_check=True)
                        if tb:
                            last = mm(o, A1[:, 1024 + h * P:1024 + (h + 1) * P], V1[:, 2 * b + 1, h * P:(h + 1) * P], start=False, stop=True,
                                      skip_group_check=True)
                    last.then_inc(c1["pv"], 1)

            l1_scores(0)
            for b in range(NB):
                if b + 1 < NB:
                    l1_scores(b + 1)
                l1_values(b)
            pe.wait_ge(c1["gate"], 9)
            pe.wait_ge(c1["sig"], NB)
            for tt in range(TT):
                last = nc.tensor.transpose(PS[0:R1, 4 + tt // 4, (tt % 4) * P:(tt % 4 + 1) * P], LA[:, tt, 0:R1], ident[:, :])
                if tt % 4 == 3:
                    last.then_inc(c1["lat_ps"], 1)
            pe.wait_ge(w_lo, U_W1 + KT)
            for tt in range(TT):
                if tt >= 4:
                    pe.wait_ge(ffn_x, tt - 3)
                pe.wait_ge(c1["lat_cp"], tt // 4 + 1)
                span = slice(tt * P, (tt + 1) * P)
                for k in range(KT):
                    product3(PS[:, tt % 4, :], XNH[:, k, span], XNL[:, k, span], W1H[:, k, :], W1L[:, k, :], k == 0, False)
                mm(PS[:, tt % 4, :], LAT[:, span], BT1[:, :], start=False, stop=True).then_inc(ffn_ps, 1)
            finish(pe, 5)

            normalise(2)
            finish(pe, 6)
            pe.wait_ge(small_in, SMALL_L2)
            mm(PS[:, 5, :], coresT[:, :], BwT[:, :], start=True, stop=True).then_inc(d2["g_ps"], 1)
            for tt in range(TT):
                at = tt * (R2 + E2)
                for k in range(KT):
                    last = mm(PS[:, 4, at:at + R2 + E2], XT2[:, k, tt * P:(tt + 1) * P], AR2[:, k, :], start=(k == 0), stop=(k == KT - 1),
                              skip_group_check=True)
            last.then_inc(d2["lo_ps"], 1)
            pe.wait_ge(d2["c"], 7)
            for tt in range(TT):
                last = nc.tensor.transpose(PS[:, 6 + tt // 4, (tt % 4) * P:(tt % 4 + 1) * P],
                                           U2[:, tt, :, :].rearrange("p e r -> p (e r)"), ident[:, :])
                if tt % 4 == 3:
                    last.then_inc(d2["tp"], 1)
            pe.wait_ge(w_lo, U_WB2 + KT)
            pe.wait_ge(d2["gl"], 1)
            for tt in range(TT):
                if tt >= 4:
                    pe.wait_ge(ffn_x, TT + tt - 3)
                pe.wait_ge(d2["ul"], tt // 4 + 1)
                span = slice(tt * P, (tt + 1) * P)
                for k in range(KT):
                    product3(PS[:, tt % 4, :], XNH[:, k, span], XNL[:, k, span], W2H[:, k, :], W2L[:, k, :], k == 0, False)
                product3(PS[:, tt % 4, :], UH[:, span], UL[:, span], GH[:, :], GL[:, :], False, True).then_inc(ffn_ps, 1)
            finish(pe, 7)

            def attend_group(g, u):
                return g * U_L2_G + (U_L2 + u + 1)

            def output(g, j, tb):
                i, p = g * NB + j, j % 2
                if tb == 0:
                    pe.wait_ge(e2["olo"], i - 1)
                pe.wait_ge(e2["x"], i * 2 + (tb - 4))
                for h in range(4):
                    span = slice(h * P, (h + 1) * P)
                    last = product3(PS[:, 7, :], OH[p][:, tb, span], OL[p][:, tb, span], E_WH[:, 6 + h, :], E_WL[:, 6 + h, :],
                                    h == 0, h == 3)
                last.then_inc(e2["wo"], 1)

            def l2_slot(g, j, step, one, two):
                i, p, q = g * NB + j, j % 2, 1 - j % 2
                qh = QKH[q][:, 0:4, :]
                ql = QKL[q][:, 0:4, :]
                kh, kl = QKH[q][:, 4, :], QKL[q][:, 4, :]
                if one:
                    pe.wait_ge(e2["qlo"], i)
                    if two:
                        pe.wait_ge(e2["u"], i - 1)
                    for tb in range(2):
                        for h in range(4):
                            at, bank = (h % 2) * SEQ, 3 + 2 * tb + h // 2
                            mm(PS[:, bank, at:at + SEQ], qh[:, h, tb * P:(tb + 1) * P], kh, start=True, stop=False, skip_group_check=True)
                            last = mm(PS[:, bank, at + tb * P:at + (tb + 1) * P], identb[:, :], mask_ts[:, :], start=False, stop=True,
                                      skip_group_check=True)
                        last.then_inc(e2["max"], 1)
                    if two:
                        pe.wait_ge(e2["exp"], i - 1)
                    for n, (s, t) in enumerate(((0, 0), (0, 1), (1, 1))):
                        ks, ts = slice(s * P, (s + 1) * P), slice(t * P, (t + 1) * P)
                        mm(PS[:, n, :], kl[:, ks], qh[:, :, ts], start=True, stop=False, skip_group_check=True)
                        mm(PS[:, n, :], kh[:, ks], ql[:, :, ts], start=False, stop=False, skip_group_check=True)
                        mm(PS[:, n, :], kh[:, ks], qh[:, :, ts], start=False, stop=False, skip_group_check=True)
                        if s == t:
                            mm(PS[:, n, :], identb[:, :], mask_st[:, :, :], start=False, stop=False, skip_group_check=True)
                    pe.wait_ge(e2["red"], i * 2)
                if step:
                    tok = slice(j * SEQ, (j + 1) * SEQ)
                    for u in range(6):
                        pe.wait_ge(w_lo, attend_group(g, u))
                        for k in range(KT):
                            span = slice(k * P, (k + 1) * P)
                            o = PS[:, 3 + u // 2, (u % 2) * SEQ:(u % 2 + 1) * SEQ]
                            last = product3(o, E_WH[:, u, span], E_WL[:, u, span], XNH[:, k, tok], XNL[:, k, tok], k == 0, k == KT - 1)
                    last.then_inc(e2["proj"], 1)
                if one:
                    pe.wait_ge(e2["mxs"], i)
                    nc.tensor.transpose(PS[0:16, 6, SEQ:SEQ + P // 2].bitcast(BF16), E_mxs[:, :], identb[:, :]).then_inc(e2["mxt"], 1)
                    pe.wait_ge(e2["mxc"], i)
                    for h in range(4):
                        for n, tb in enumerate((0, 1, 1)):
                            last = mm(PS[:, n, h * P:(h + 1) * P], pick8[:, 4 * tb + h, :], E_mxT[:, :], start=False, stop=True,
                                      skip_group_check=True)
                    last.then_inc(e2["shift"], 1)
                if step:
                    pe.wait_ge(e2["vt"], i + 1)
                    for s in range(2):
                        last = nc.tensor.transpose(PS[:, 6, s * P:(s + 1) * P], vT2[:, s * P:(s + 1) * P], ident[:, :])
                    last.then_inc(e2["vtp"], 1)
                if two:
                    if j == 2:
                        pe.wait_ge(w_lo, attend_group(g, U_L2_G - 1))
                    output(g, j, 0)
                if one:
                    pe.wait_ge(e2["plo"], i)
                    if step:
                        pe.wait_ge(e2["t1"], i + 1)
                        pe.wait_ge(e2["sw"], i + 1)
                        pe.wait_ge(e2["vlo"], i + 1)
                    else:
                        pe.wait_ge(e2["vlo"], i)
                    for tb in range(2):
                        blocks = ((0, 0),) if tb == 0 else ((1, 0), (2, 1))
                        for m, (n, s) in enumerate(blocks):
                            product3(PS[:, 3 + tb, :], VH[q][:, s, :], VL[q][:, s, :], PH[:, n, :], PL[:, n, :], m == 0, m == len(blocks) - 1)
                        for m, (n, s) in enumerate(blocks):
                            mm(PS[:, 5 + tb, :], ones_r[:, :], PL[:, n, :], start=(m == 0), stop=False)
                            last = mm(PS[:, 5 + tb, :], ones_r[:, :], PH[:, n, :], start=False, stop=(m == len(blocks) - 1))
                        last.then_inc(e2["pv"], 1)
                if two:
                    output(g, j, 1)

            for j in range(NB):
                l2_slot(0, j, True, j >= 1, j >= 2)
            with pe.Fori(1, KV2) as g:
                for j in range(NB):
                    l2_slot(g, j, True, True, True)
            l2_slot(KV2, 0, False, True, True)
            l2_slot(KV2, 1, False, False, True)
            finish(pe, 8)

            normalise(3, True)
            pe.wait_ge(f["lo"], 3 * NF + KT)
            for tt in range(TT):
                if tt >= 4:
                    pe.wait_ge(ffn_x, 2 * TT + tt - 3)
                ln_wait(pe, 3, "lo", tt + 1)
                span = slice(tt * P, (tt + 1) * P)
                for k in range(KT):
                    last = product3(PS[:, 4 + tt % 4, :], XNH[:, k, span], XNL[:, k, span], W3H[:, k, :], W3L[:, k, :], k == 0, k == KT - 1)
                last.then_inc(ffn_ps, 1)
            finish(pe, 9)
            pe.wait_ge(g3["zl"], 1)
            pe.wait_ge(g3["pk"], 1)
            pe.wait_ge(w_lo, U_M3 + 2)
            def recall(b):
                def query(h):
                    n, p = b * H3 + h, h % 2
                    if h >= 2:
                        pe.wait_ge(g3["m"], b * H3 + (h - 1))
                        pe.wait_ge(g3["r"], b * H3 + (h - 1))
                    for k in range(KT):
                        span, tok = slice(k * P, (k + 1) * P), bass.ds(b * SEQ, SEQ)
                        last = product3(PS[:, p, 0:SEQ], L3H[:, h, span], L3L[:, h, span], XNH[:, k, tok], XNL[:, k, tok], k == 0, k == KT - 1)
                    last.then_inc(g3["qps"], 1)

                def read_out(h):
                    n, p = b * H3 + h, h % 2
                    pe.wait_ge(g3["slo"], n + 1)
                    if h >= 2:
                        pe.wait_ge(g3["ncp"], b * H3 + (h - 1))
                    unit, span = H3 + h // 4, slice((h % 4) * P, (h % 4 + 1) * P)
                    product3(PS[:, 4, 0:SEQ], ZH[:, h, :], ZL[:, h, :], SH[p][:, :], SL[p][:, :], h == 0, h == H3 - 1)
                    product3(PS[:, 2 + p, 0:SEQ], L3H[:, unit, span], L3L[:, unit, span], SH[p][:, :], SL[p][:, :], True, True)\
                        .then_inc(g3["nps"], 1)

                after(pe, g3["mul"], b * H3)
                after(pe, g3["dc"], b * 2)
                query(0)
                for h in range(H3):
                    if h + 1 < H3:
                        query(h + 1)
                    read_out(h)
                pe.wait_ge(g3["rl"], b + 1)
                after(pe, g3["xo"], b * 2)
                for h in range(H3):
                    if h >= 2:
                        pe.wait_ge(g3["mul"], b * H3 + (h - 1))
                    mm(PS[:, 5 + h % 2, 0:SEQ], pick3[:, h, :], RL[:, :], start=True, stop=False)
                    mm(PS[:, 5 + h % 2, 0:SEQ], pick3[:, h, :], RH[:, :], start=False, stop=True).then_inc(g3["bps"], 1)
                pe.wait_ge(g3["wsl"], H3)
                pe.wait_ge(g3["nlo"], b * H3 + H3)
                for tl in range(2):
                    span = slice(tl * P, (tl + 1) * P)
                    for h in range(H3):
                        last = product3(PS[:, 6 + tl, :], NH3[:, h, span], NL3[:, h, span], WSH[:, h, :], WSL[:, h, :], h == 0, h == H3 - 1)
                    last.then_inc(g3["ops"], 1)

            recall(0)
            with pe.Fori(1, NB) as b:
                recall(b)
            finish(pe, 10)


def kernel(**inputs):
    import numpy as np
    import concourse.bacc as bacc
    from concourse import mybir
    from concourse.bass_utils import run_bass_kernel_spmd

    a = {k: np.asarray(v) for k, v in inputs.items()}
    P, KT, C, NF = 128, 4, 512, 11
    f32 = np.float32

    def tiles(w):
        return w.T.reshape(-1, P, w.shape[0])

    def columns(w, order=None):
        t = w.T if order is None else w.T[order]
        return t.reshape(-1, P, w.shape[0] // P, P).transpose(2, 1, 0, 3).reshape(w.shape[0] // P, P, -1)

    def rows(v, n=P):
        return np.broadcast_to(v, (n,) + v.shape)

    def pad(x, axis, size):
        widths = [(0, 0)] * x.ndim
        widths[axis] = (0, size - x.shape[axis])
        return np.pad(x, widths)

    def inner(x, per):
        x = pad(x, 1, NF * P // per)
        return x.reshape(x.shape[0], NF, P // per).transpose(1, 0, 2)

    words = [inner(a[f"L0_ffn_{n}_qweight"], 1).reshape(NF, KT, 16, P).transpose(0, 2, 1, 3).reshape(NF, 16, C) for n in ("gate", "up")]
    words.append(pad(a["L0_ffn_down_qweight"], 0, NF * 16).reshape(NF, 16, C))
    zeros = [inner(a[f"L0_ffn_{n}_zeros"], 8).reshape(NF, C // 8) for n in ("gate", "up")] + [a["L0_ffn_down_zeros"]]
    scales = [inner(a[f"L0_ffn_{n}_scales"], 1).reshape(NF, C) for n in ("gate", "up")] + [a["L0_ffn_down_scales"]]

    qkv = columns(a["L2_attn_Wqkv"])
    wo2 = a["L2_attn_Wo"].T.reshape(32, P, C)
    w2 = np.stack([np.stack([*qkv[4 * g:4 * g + 4], qkv[32 + g], qkv[40 + g], *wo2[4 * g:4 * g + 4]]) for g in range(8)])

    order = np.arange(C).reshape(2, P, 2).transpose(0, 2, 1).reshape(C)
    read = np.arange(32 * P).reshape(8, 4, P)[:, 0].reshape(-1)
    m3 = a["L3_attn_M"].transpose(1, 0, 2).reshape(P, 2, C).transpose(1, 0, 2)
    w3 = np.concatenate([columns(a["L3_attn_Wq"][read], order), m3])

    def angles(t, h):
        pos = np.arange(t, dtype=f32)
        theta = f32(1.0) / f32(10000.0) ** (np.arange(0, h, 2, dtype=f32) / f32(h))
        return np.outer(pos, theta).astype(f32)

    t0, t2 = angles(256, 16), angles(256, 128)
    cos0 = np.concatenate([np.cos(t0), np.cos(t0)], 1)
    sin0 = np.concatenate([-np.sin(t0), np.sin(t0)], 1)
    cos2 = np.concatenate([np.cos(t2), np.cos(t2)], 1)
    sin2 = np.concatenate([-np.sin(t2), np.sin(t2)], 1)
    bf16 = mybir.dt.np(mybir.dt.bfloat16)
    p = np.arange(P)
    hidden = np.where(p[None, :] > p[:, None], -1e30, 0.0)
    arrays = dict(
        x=a["L0_attn_x"].reshape(8, P, C),
        w0=np.concatenate([tiles(a[f"L0_attn_{n}"]) for n in ("wq", "wk", "wv", "wo")]),
        words=np.stack(words), zeros=np.concatenate(zeros, 1), scales=np.concatenate(scales, 1),
        bv=np.concatenate([a[f"L1_attn_bv_{n}"].T for n in "qkv"], 1), bvr=rows(a["L1_attn_bv_v"]),
        w1=tiles(a["L1_ffn_W"]), b1=rows(a["L1_ffn_b"]), gb1=rows(a["L1_ffn_gate_b"]),
        ag1=np.concatenate([a["L1_ffn_A"].T, a["L1_ffn_gate_w"].T], 1).reshape(KT, P, 68).transpose(1, 0, 2),
        bt1=a["L1_ffn_B"].T,
        wb2=tiles(a["L2_ffn_W_base"]), b2=rows(a["L2_ffn_b_base"]),
        ar2=np.concatenate([a["L2_ffn_A_w"].T, a["L2_ffn_router_w"].T], 1).reshape(KT, P, 24).transpose(1, 0, 2),
        coresT=a["L2_ffn_cores"].transpose(2, 0, 1).reshape(16, P), bwT=a["L2_ffn_B_w"].T, w2=w2,
        w3=w3, wo3=a["L3_attn_Wo"].T.reshape(8, 4, P, C), bq3=a["L3_attn_bq"][read].reshape(8, P).T, zc3=a["L3_attn_z"].T,
        pk3=a["L3_ffn_weight_packed"].reshape(C, 2, P).transpose(2, 1, 0), zp3=rows(a["L3_ffn_zero_point"][:, 0]),
        sc3=rows(a["L3_ffn_scale"][:, 0]), b3=rows(a["L3_ffn_bias"]),
        ident=np.eye(P, dtype=f32), identb=np.eye(P, dtype=bf16), mask_ts=hidden.astype(bf16),
        mask_st=np.broadcast_to(hidden.T[:, None, :], (P, 4, P)).astype(bf16), mask01=(hidden.T == 0).astype(f32),
        pick8=(np.arange(16)[:, None, None] % 8 == np.arange(8)[None, :, None]).repeat(P, 2).astype(bf16),
        pickf=(np.arange(8)[:, None, None] == np.arange(8)[None, :, None]).repeat(P, 2).astype(f32),
        shift_k=(4 * (p % 8)).astype(np.int32)[:, None], shift_n=np.broadcast_to(4 * np.arange(8, dtype=np.int32), (NF, 8)),
        rope0c=cos0.reshape(2, P, 16).transpose(1, 0, 2), rope0s=sin0.reshape(2, P, 16).transpose(1, 0, 2),
        rope2c=cos2.T, rope2s=sin2.T)

    nc = bacc.Bacc("TRN2", target_bir_lowering=False, num_devices=1)
    fed, d = {}, {}
    for name, x in arrays.items():
        x = np.ascontiguousarray(x)
        fed[f"in_{name}"] = x
        d[name] = nc.dram_tensor(f"in_{name}", x.shape, mybir.dt.from_np(x.dtype), kind="ExternalInput").ap()
    d["z1_scratch"] = nc.dram_tensor("z1_scratch", (NF, 3 * C), mybir.dt.float16, kind="Internal").ap()
    out = nc.dram_tensor("out", (8, P, C), mybir.dt.float32, kind="ExternalOutput").ap()
    build_program(nc, d, out)
    r = run_bass_kernel_spmd(nc, [fed], core_ids=[0])
    return r.results[0]["out"].reshape(4, 256, C)
```

```python
def build_program(nc, d, out):
    from contextlib import ExitStack
    import concourse.bass as bass
    from concourse import mybir

    F32, F32R = mybir.dt.float32, mybir.dt.float32r
    BF16, F16, I32 = mybir.dt.bfloat16, mybir.dt.float16, mybir.dt.int32
    ACT, ALU, AXIS = mybir.ActivationFunctionType, mybir.AluOpType, mybir.AxisListType

    P = 128
    C = 512
    KT = C // P
    TOK = 1024
    TT = TOK // P
    SEQ = 256
    NB = TOK // SEQ
    RAW = 5
    H0, D0 = 32, 16
    G0 = H0 // 4
    HALF = C // 2
    S0 = 64
    NF = 11
    H2, KV2, D2 = 32, 8, 128
    H3 = 8
    R1, E1 = 64, 4
    E2, R2 = 8, 16

    U_QKV0, U_W1 = 0, 12
    U_WB2 = U_W1 + KT
    U_L2 = U_WB2 + KT
    U_L2_G = 10
    U_L3 = U_L2 + KV2 * U_L2_G

    ctx = ExitStack()
    with ctx:
        def sem(name):
            return ctx.enter_context(nc.semaphore(name))

        def keep(name, shape, dt=F32):
            return ctx.enter_context(nc.sbuf_tensor(name, list(shape), dt))

        X = keep("X", [P, TT, C])
        XNH = keep("XNH", [P, KT, TOK], F32R)
        XNL = keep("XNL", [P, KT, TOK], F32R)
        raw = keep("raw", [P, RAW, C])
        ident = keep("ident", [P, P])
        identb = keep("identb", [P, P], BF16)
        mask_ts = keep("mask_ts", [P, P], BF16)
        mask01 = keep("mask01", [P, P])
        shift_k = keep("shift_k", [P, 1], I32)
        rope0c = keep("rope0c", [P, 2, D0])
        rope0s = keep("rope0s", [P, 2, D0])
        rope2c = keep("rope2c", [P, SEQ])
        rope2s = keep("rope2s", [P, SEQ])
        PS = ctx.enter_context(nc.psum_tensor("PS", [P, 8, C], F32))

        def phase():
            return ExitStack()

        def sb(stack, name, shape, dt=F32):
            return stack.enter_context(nc.sbuf_tensor(name, list(shape), dt))

        LN = {}
        stats = keep("stats", [P, TT, 6])
        XNB, TB = 4, 3

        def ln_buffers(stack, l):
            LN[l] = dict(
                mv=sb(stack, f"ln{l}_mv", [P, TT, 2]),
                var=sb(stack, f"ln{l}_var", [P, TT]), sd=sb(stack, f"ln{l}_sd", [P, TT]),
                tmp=sb(stack, f"ln{l}_tmp", [P, TT]), rstd=sb(stack, f"ln{l}_rstd", [P, TT]),
                xn=sb(stack, f"ln{l}_xn", [P, XNB, C]))

        with phase() as st:
            WQH = sb(st, "WQH", [P, 12, C], F32R)
            WQL = sb(st, "WQL", [P, 12, C], F32R)
            wo0 = sb(st, "wo0", [P, KT, C])
            with phase() as st2:
                ln_buffers(st2, 0)
            SGH = sb(st, "SGH", [P, KT, SEQ], F32R)
            SGL = sb(st, "SGL", [P, KT, SEQ], F32R)
            A_T1 = sb(st, "A_T1", [P, H0 // 2, D0])
            A_sw = sb(st, "A_sw", [P, H0 // 2, D0])
            A_q = sb(st, "A_q", [P, H0 // 2, D0])
            STK = sb(st, "STK", [P, H0 // 2, S0])
            qT = sb(st, "qT", [P, H0 // 2, SEQ], F32R)
            kT = sb(st, "kT", [P, H0 // 2, SEQ], F32R)
            V0 = sb(st, "V0", [P, 2, H0 // 2, 2, 2 * D0])
            A_p = sb(st, "A_p", [P, 12, P])
            A_pT = sb(st, "A_pT", [P, 12, P])
            OT0 = sb(st, "OT0", [P, KT, SEQ])
            A_mx = sb(st, "A_mx", [P, 8])
            A_nb = sb(st, "A_nb", [P, 8])
            A_sum = sb(st, "A_sum", [P, 8])
            A_rec = sb(st, "A_rec", [P, 8])

        with phase() as st:
            zw = sb(st, "zw", [NF, 3 * C // 8], I32)
            zshift = sb(st, "zshift", [NF, 8], I32)
            zq = sb(st, "zq", [NF, 3 * C], I32)
            z1 = sb(st, "z1", [NF, 3 * C], F16)
            words = [sb(st, f"words{p}", [P, 3, C], I32) for p in range(2)]
            zb = [sb(st, f"zb{p}", [P, 3, C], F16) for p in range(2)]
            scb = [sb(st, f"scb{p}", [P, 3, C], F16) for p in range(2)]
            F_q = sb(st, "F_q", [P, C], I32)
            F_t = sb(st, "F_t", [P, 3, C])
            F_w = sb(st, "F_w", [P, 3, C])
            FWH = [sb(st, f"FWH{p}", [P, 3, C], F32R) for p in range(2)]
            FWL = [sb(st, f"FWL{p}", [P, 3, C], F32R) for p in range(2)]
            F_sg = sb(st, "F_sg", [P, 2, C])
            F_a = sb(st, "F_a", [P, 2, C])
            F_i = sb(st, "F_i", [P, 2, C])
            FIH = [sb(st, f"FIH{p}", [P, TOK], F32R) for p in range(2)]
            FIL = [sb(st, f"FIL{p}", [P, TOK], F32R) for p in range(2)]
            F_acc = sb(st, "F_acc", [P, TT, C])
            F_half = sb(st, "F_half", [P, TT, C], F16)

        with phase() as st:
            ln_buffers(st, 1)
            XT1 = sb(st, "XT1", [P, KT, TOK])
            K1 = sb(st, "K1", [P, KT, TOK])
            V1 = sb(st, "V1", [P, TT, C])
            bv = sb(st, "bv", [P, 12])
            bvr = sb(st, "bvr", [P, 4, P])
            bv_abs = sb(st, "bv_abs", [P, 12])
            bv_sg = sb(st, "bv_sg", [P, 12])
            bv_q = sb(st, "bv_q", [P, 12])
            qk1 = sb(st, "qk1", [P, 4])
            vr_al = sb(st, "vr_al", [P, 4])
            vr_sg = sb(st, "vr_sg", [P, 4, P])
            vrow = sb(st, "vrow", [P, 4, P])
            inv = sb(st, "inv", [P, P])
            A1 = sb(st, "A1", [P, 1536])
            W1H = sb(st, "W1H", [P, KT, C], F32R)
            W1L = sb(st, "W1L", [P, KT, C], F32R)
            AG1 = sb(st, "AG1", [P, KT, R1 + E1])
            BT1 = sb(st, "BT1", [R1, C])
            b1 = sb(st, "b1", [P, C])
            gb1 = sb(st, "gb1", [P, E1])
            LA = sb(st, "LA", [P, TT, R1 + E1])
            g_m = sb(st, "g_m", [P, TT])
            g_ne = sb(st, "g_ne", [P, TT, E1])
            LAT = sb(st, "LAT", [R1, TOK])

        with phase() as st:
            ln_buffers(st, 2)
            XT2 = sb(st, "XT2", [P, KT, TOK])
            W2H = sb(st, "W2H", [P, KT, C], F32R)
            W2L = sb(st, "W2L", [P, KT, C], F32R)
            AR2 = sb(st, "AR2", [P, KT, R2 + E2])
            coresT = sb(st, "coresT", [R2, E2 * R2])
            BwT = sb(st, "BwT", [R2, C])
            b2 = sb(st, "b2", [P, C])
            axr = sb(st, "axr", [P, TT, R2 + E2])
            e_m = sb(st, "e_m", [P, TT])
            e_p = sb(st, "e_p", [P, TT, E2])
            e_s = sb(st, "e_s", [P, TT])
            U2 = sb(st, "U2", [P, TT, E2, R2])
            UH = sb(st, "UH", [P, TOK], F32R)
            UL = sb(st, "UL", [P, TOK], F32R)
            GH = sb(st, "GH", [P, C], F32R)
            GL = sb(st, "GL", [P, C], F32R)

        with phase() as late:
            WSH = sb(late, "WSH", [P, H3, C], F32R)
            WSL = sb(late, "WSL", [P, H3, C], F32R)
            wo3 = sb(late, "wo3", [P, 4, C])
            G_wo = sb(late, "G_wo", [P, C])
            with phase() as st:
                E_WH = sb(st, "E_WH", [P, U_L2_G, C], F32R)
                E_WL = sb(st, "E_WL", [P, U_L2_G, C], F32R)
                E_T = sb(st, "E_T", [P, 5, SEQ])
                E_sw = sb(st, "E_sw", [P, 5, SEQ])
                QKH = sb(st, "QKH", [P, 5, SEQ], F32R)
                QKL = sb(st, "QKL", [P, 5, SEQ], F32R)
                vT2 = sb(st, "vT2", [P, SEQ])
                VH = sb(st, "VH", [P, 2, P], F32R)
                VL = sb(st, "VL", [P, 2, P], F32R)
                E_p = sb(st, "E_p", [P, 12, P])
                PH = sb(st, "PH", [P, 3, C], F32R)
                PL = sb(st, "PL", [P, 3, C], F32R)
                OH = [sb(st, f"OH{p}", [P, 2, C], F32R) for p in range(2)]
                OL = [sb(st, f"OL{p}", [P, 2, C], F32R) for p in range(2)]
                E_mx = sb(st, "E_mx", [P, 8])
                E_nb = sb(st, "E_nb", [P, 8])
                E_sum = sb(st, "E_sum", [P, 8])
                E_rec = sb(st, "E_rec", [P, 8])

            L3H = sb(late, "L3H", [P, H3, C], F32R)
            L3L = sb(late, "L3L", [P, H3, C], F32R)
            bq3 = sb(late, "bq3", [P, H3])
            MZ = sb(late, "MZ", [P, H3, P + 1])
            with phase() as st:
                ln_buffers(st, 3)
                pk3 = sb(st, "pk3", [P, 2, C], I32)
                zp3 = sb(st, "zp3", [P, C])
                sc3 = sb(st, "sc3", [P, C])
                b3 = sb(st, "b3", [P, C])
                q3 = sb(st, "q3", [P, KT, C], I32)
                t3 = sb(st, "t3", [P, KT, C])
                W3H = sb(st, "W3H", [P, KT, C], F32R)
                W3L = sb(st, "W3L", [P, KT, C], F32R)
            with phase() as st:
                G_m = sb(st, "G_m", [P, SEQ])
                G_e = sb(st, "G_e", [P, SEQ])
                G_r = sb(st, "G_r", [P, SEQ])
                G_s = [sb(st, f"G_s{p}", [P, SEQ]) for p in range(2)]
                G_rec = sb(st, "G_rec", [P, 2])
                G_o = [sb(st, f"G_o{p}", [P, 2, P]) for p in range(2)]
                NH3 = [sb(st, f"NH3{p}", [P, SEQ], F32R) for p in range(2)]
                NL3 = [sb(st, f"NL3{p}", [P, SEQ], F32R) for p in range(2)]

        const_in = sem("const_in")
        x_in = [sem(f"x_in{n}") for n in range(TT // 2)]
        wo_in = sem("wo_in")
        small_in = sem("small_in")
        SMALL_L1, SMALL_L2, SMALL_F3 = 16 * 6, 16 * 10, 16 * 14
        bias_in = sem("bias_in")
        ffn_ps = sem("ffn_ps")
        ffn_x = sem("ffn_x")
        raw_in = [sem(f"raw_in{r}") for r in range(RAW)]
        w_hi = sem("w_hi")
        w_lo = sem("w_lo")
        phase_done = sem("phase_done")
        LN_SIGNALS = dict(stat=TT, aggr=TT, var=1, sd=1, c=5, xn=TT, tp=TT, hi=TT, lo=TT)
        ln = {n: sem(f"ln_{n}") for n in LN_SIGNALS}

        def ln_wait(eng, l, name, n):
            eng.wait_ge(ln[name], l * LN_SIGNALS[name] + n)

        def sems(prefix, names):
            return {n: sem(f"{prefix}_{n}") for n in names.split()}

        a = sems("a", "stage0 stage1 init proj sw t1 t2 q hi lo tp eva evd vps vcp sc mx neg exp rec pn pt pe pv ot wo_ps x")

        def prepared(b, g, ago=0):
            v = g + 5 - ago
            at = b + v // G0
            if isinstance(at, int) and at >= NB:
                return None
            return b * G0 + v, at, v % G0 // 4, v % 4 // 2, v % 2

        FIRST = range(3, G0)

        def order(h):
            return (h % 2) * 2 + h // 2

        f = sems("f", "zin z zout in0 in1 q t w hi lo gu sg a i ih il dps acc half x")
        c1 = sems("c", "abs al c v k1 lo_ps gate st sig mask pv xa lat_ps lat_cp")
        d2 = sems("d", "lo_ps c ax g_ps gh gl tp uh ul up x")
        e2 = sems("e", "sc mx neg exp rec pn pt phi plo pv ohi olo pq pk sw vt t1 t2 q qhi qlo vtp vhi vlo wo x")
        g3 = sems("g", "in woin s12 s wsh wsl qps m e r sum nps rc mul tp hi lo wo xo out")

        def turns(n, lag):
            return not isinstance(n, int) or 0 <= n - lag < NB * H3

        block = ctx.enter_context(nc.Block())

        def after(eng, signal, n):
            if not isinstance(n, int) or n > 0:
                eng.wait_ge(signal, n)

        def finish(eng, n):
            eng.drain().then_inc(phase_done, 1)
            eng.wait_ge(phase_done, 4 * n)

        def product3(o, sh, sl, mh, ml, first, last):
            nc.tensor.matmul(o, sl, mh, start=first, stop=False)
            nc.tensor.matmul(o, sh, ml, start=False, stop=False)
            return nc.tensor.matmul(o, sh, mh, start=False, stop=last)

        def f32(ap):
            return ap.bitcast(F32)

        @block.sync
        def _(sp):
            for tt in range(TT):
                sp.dma_start(X[:, tt, :], d["x"][tt]).then_inc(x_in[tt // 2], 16)

            def load_unit(n, slot, src):
                if not isinstance(n, int) or n >= RAW:
                    sp.wait_ge(w_lo, n - RAW + 1)
                sp.dma_start(raw[:, slot, :], src).then_inc(raw_in[slot], 16)

            for u in range(12):
                load_unit(U_QKV0 + u, u % RAW, d["w0"][u])
            for kt in range(KT):
                sp.dma_start(wo0[:, kt, :], d["w0"][12 + kt]).then_inc(wo_in, 16)
            ln_wait(sp, 0, "lo", TT)
            def stage(b):
                for tl in range(2):
                    if not isinstance(b, int) or b >= 1:
                        sp.wait_ge(a["vps"], b * 4 + (tl - 1))
                    tok, at = bass.ds(b * SEQ + tl * P, P), slice(tl * P, (tl + 1) * P)
                    sp.dma_start(f32(SGH[:, :, at]), f32(XNH[:, :, tok])).then_inc(a[f"stage{tl}"], 16)
                    sp.dma_start(f32(SGL[:, :, at]), f32(XNL[:, :, tok])).then_inc(a[f"stage{tl}"], 16)

            stage(0)
            with sp.Fori(1, NB) as b:
                stage(b)
            sp.wait_ge(phase_done, 4 * 2)
            sp.dma_start(zw[:, :], d["zeros"]).then_inc(f["zin"], 16)
            sp.dma_start(zshift[:, :], d["shift_n"]).then_inc(f["zin"], 16)
            sp.wait_ge(f["z"], 3)
            sp.dma_start(d["z1_scratch"], z1[:, :]).then_inc(f["zout"], 16)
            sp.wait_ge(f["zout"], 16)

            def load_tile(n, p):
                if not isinstance(n, int) or n >= 2:
                    sp.wait_ge(f["w"], n * 3 - 3)
                for c in range(3):
                    for r in range(8):
                        sp.dma_start(words[p][r:P:8, c, :], d["words"][c, bass.ds(n, 1), :, :].rearrange("a r n -> (a r) n"))\
                          .then_inc(f[f"in{p}"], 16)
                sp.dma_start(zb[p][:, :, :], d["z1_scratch"][bass.ds(n, 1), :].rearrange("a (c n) -> a c n", c=3).broadcast_to([P, 3, C]))\
                  .then_inc(f[f"in{p}"], 16)
                sp.dma_start(scb[p][:, :, :], d["scales"][bass.ds(n, 1), :].rearrange("a (c n) -> a c n", c=3).broadcast_to([P, 3, C]))\
                  .then_inc(f[f"in{p}"], 16)

            load_tile(0, 0)
            with sp.Fori(0, (NF - 1) // 2) as i:
                load_tile(i * 2 + 1, 1)
                load_tile(i * 2 + 2, 0)
            for u in range(KT):
                load_unit(U_W1 + u, (U_W1 + u) % RAW, d["w1"][u])
            for u in range(KT):
                load_unit(U_WB2 + u, (U_WB2 + u) % RAW, d["wb2"][u])
            def group(g):
                for u in range(U_L2_G):
                    load_unit(g * U_L2_G + (U_L2 + u), (U_L2 + u) % RAW,
                              d["w2"][bass.ds(g, 1), u, :, :].rearrange("a p n -> (a p) n"))
                after(sp, g3["s"], g)
                for q in range(4):
                    sp.dma_start(wo3[:, q, :], d["wo3"][bass.ds(g, 1), q, :, :].rearrange("a p n -> (a p) n")).then_inc(g3["woin"], 16)

            group(0)
            with sp.Fori(1, KV2) as g:
                group(g)
            for u in range(H3):
                load_unit(U_L3 + u, (U_L3 + u) % RAW, d["w3"][u])
            def recall(b):
                for tl in range(2):
                    sp.wait_ge(g3["xo"], b * 2 + (tl + 1))
                    sp.dma_start(out[bass.ds(b * 2 + tl, 1), :, :].rearrange("a p c -> p (a c)"),
                                 X[:, bass.ds(b * 2 + tl, 1), :].rearrange("p a c -> p (a c)")).then_inc(g3["out"], 16)

            recall(0)
            with sp.Fori(1, NB) as b:
                recall(b)
            sp.wait_ge(g3["out"], 16 * TT)

        @block.gpsimd
        def _(pool):
            def rest(n, hi, lo, slot):
                pool.wait_ge(w_hi, n + 1)
                nc.gpsimd.tensor_tensor(lo, raw[:, slot, :], f32(hi), ALU.subtract).then_inc(w_lo, 1)

            for u in range(12):
                rest(U_QKV0 + u, WQH[:, u, :], WQL[:, u, :], u % RAW)
            finish(pool, 1)
            nc.gpsimd.memset(STK[:, :, 3 * D0:S0], 0.0).then_inc(a["init"], 1)
            nc.gpsimd.memset(V0[:, :, :, :, :], 0.0).then_inc(a["init"], 1)
            pool.wait_ge(const_in, 16 * 9)

            def sines(U, tl):
                pool.wait_ge(a["sw"], U + 1)
                nc.gpsimd.tensor_tensor(A_sw[:, :, :], A_sw[:, :, :], rope0s[:, tl, :].unsqueeze(1).broadcast_to([P, H0 // 2, D0]), ALU.mult)\
                  .then_inc(a["t2"], 1)

            def attend(b):
                for g in range(G0):
                    unit = prepared(b, g)
                    if unit:
                        sines(unit[0], unit[3])

            for g in FIRST:
                unit = prepared(-1, g)
                sines(unit[0], unit[3])
            attend(0)
            with pool.Fori(1, NB - 1) as b:
                attend(b)
            attend(NB - 1)
            finish(pool, 2)
            def scale_tile(n, p):
                for c in range(3):
                    pool.wait_ge(f["t"], n * 3 + (c + 1))
                    if not isinstance(n, int) or n >= 1:
                        pool.wait_ge(f["lo"], n * 3 + (c - 2))
                    nc.gpsimd.tensor_tensor(F_w[:, c, :], F_t[:, c, :], scb[p][:, c, :], ALU.mult).then_inc(f["w"], 1)

            scale_tile(0, 0)
            with pool.Fori(0, (NF - 1) // 2) as i:
                scale_tile(i * 2 + 1, 1)
                scale_tile(i * 2 + 2, 0)
            finish(pool, 3)
            nc.gpsimd.memset(inv[:, :], 1.0 / P).then_inc(a["init"], 1)
            for u in range(KT):
                rest(U_W1 + u, W1H[:, u, :], W1L[:, u, :], (U_W1 + u) % RAW)
            for tt in range(TT):
                ln_wait(pool, 1, "xn", tt + 1)
                nc.gpsimd.tensor_tensor(V1[:, tt, :], LN[1]["xn"][:, tt % XNB, :], vrow[:, :, :].rearrange("p h e -> p (h e)"), ALU.mult)\
                  .then_inc(c1["v"], 1)
                ln_wait(pool, 1, "hi", tt + 1)
                span = slice(tt * P, (tt + 1) * P)
                nc.gpsimd.tensor_tensor(K1[:, :, span], XT1[:, :, span], qk1[:, :].unsqueeze(2).broadcast_to([P, KT, P]), ALU.mult)\
                  .then_inc(c1["k1"], 1)
            for tt in range(TT):
                pool.wait_ge(ffn_x, tt + 1)
                nc.gpsimd.tensor_tensor(X[:, tt, :], X[:, tt, :], b1[:, :], ALU.add).then_inc(bias_in, 1)
            finish(pool, 4)
            for u in range(KT):
                rest(U_WB2 + u, W2H[:, u, :], W2L[:, u, :], (U_WB2 + u) % RAW)
            pool.wait_ge(small_in, SMALL_L2)
            for tt in range(TT):
                pool.wait_ge(ffn_x, TT + tt + 1)
                nc.gpsimd.tensor_tensor(X[:, tt, :], X[:, tt, :], b2[:, :], ALU.add).then_inc(bias_in, 1)
            finish(pool, 5)
            def l2_rest(g, u):
                rest(g * U_L2_G + (U_L2 + u), E_WH[:, u, :], E_WL[:, u, :], (U_L2 + u) % RAW)

            def l2_sines(i, n):
                heads = (slice(0, 4), slice(4, 5))[n]
                pool.wait_ge(e2["sw"], i * 2 + (n + 1))
                nc.gpsimd.tensor_tensor(E_sw[:, heads, :], E_sw[:, heads, :],
                                        rope2s[:, :].unsqueeze(1).broadcast_to([P, heads.stop - heads.start, SEQ]), ALU.mult)\
                  .then_inc(e2["t2"], 1)

            def l2_pool_group(g, more):
                for j in range(NB):
                    l2_sines(g * NB + j, 0)
                    l2_sines(g * NB + j, 1)
                    if j == 1:
                        for u in range(6, U_L2_G):
                            l2_rest(g, u)
                    if j == 2:
                        sum_wo(g)
                    if j == NB - 1 and more:
                        for u in range(6):
                            l2_rest(g + 1, u)

            def sum_wo(h):
                pool.wait_ge(g3["woin"], h * 64 + 64)
                after(pool, g3["wsl"], h)
                nc.gpsimd.tensor_tensor(wo3[:, 0, :], wo3[:, 0, :], wo3[:, 1, :], ALU.add).then_inc(g3["s12"], 1)
                nc.gpsimd.tensor_tensor(wo3[:, 2, :], wo3[:, 2, :], wo3[:, 3, :], ALU.add).then_inc(g3["s12"], 1)
                pool.wait_ge(g3["s12"], h * 2 + 2)
                nc.gpsimd.tensor_tensor(G_wo[:, :], wo3[:, 0, :], wo3[:, 2, :], ALU.add).then_inc(g3["s"], 1)
                pool.wait_ge(g3["wsh"], h + 1)
                at = bass.ds(h, 1)
                nc.gpsimd.tensor_tensor(WSL[:, at, :].rearrange("p a n -> p (a n)"), G_wo[:, :],
                                        f32(WSH[:, at, :]).rearrange("p a n -> p (a n)"), ALU.subtract).then_inc(g3["wsl"], 1)

            for u in range(6):
                l2_rest(0, u)
            l2_pool_group(0, True)
            with pool.Fori(1, KV2 - 1) as g:
                l2_pool_group(g, True)
            l2_pool_group(KV2 - 1, False)
            finish(pool, 6)
            pool.wait_ge(small_in, SMALL_F3)
            for k in range(KT):
                pool.wait_ge(f["t"], 3 * NF + k + 1)
                nc.gpsimd.tensor_tensor(t3[:, k, :], t3[:, k, :], sc3[:, :], ALU.mult).then_inc(f["w"], 1)
            for u in range(H3):
                rest(U_L3 + u, L3H[:, u, :], L3L[:, u, :], (U_L3 + u) % RAW)
            for tt in range(TT):
                pool.wait_ge(ffn_x, 2 * TT + tt + 1)
                nc.gpsimd.tensor_tensor(X[:, tt, :], X[:, tt, :], b3[:, :], ALU.add).then_inc(bias_in, 1)
            finish(pool, 7)
            finish(pool, 8)

        @block.scalar
        def _(act):
            def copy(o, i, signal=None):
                ins = nc.scalar.activation(o, i, ACT.Copy)
                return ins.then_inc(signal, 1) if signal is not None else ins

            def head(slot, use, hi):
                act.wait_ge(raw_in[slot], use * 16)
                copy(hi, raw[:, slot, :], w_hi)

            def head_of(n, hi):
                head(n % RAW, n // RAW + 1, hi)

            def normalise(l, XT=None, each=None):
                ln_wait(act, l, "var", 1)
                nc.scalar.activation(LN[l]["sd"][:, :], LN[l]["var"][:, :], ACT.Sqrt).then_inc(ln["sd"], 1)
                for tt in range(TT):
                    ln_wait(act, l, "tp", tt + 1)
                    bank = PS[:, tt % TB, :].rearrange("p (k t) -> p k t", k=KT)
                    if XT is not None:
                        copy(XT[:, :, tt * P:(tt + 1) * P], bank)
                    copy(XNH[:, :, tt * P:(tt + 1) * P], bank, ln["hi"])
                    if each is not None:
                        each(tt)

            consts = [(ident, "ident"), (identb, "identb"), (mask_ts, "mask_ts"), (mask01, "mask01"), (shift_k, "shift_k"), (rope0c, "rope0c"), (rope0s, "rope0s"),
                      (rope2c, "rope2c"), (rope2s, "rope2s")]
            for t, name in consts:
                act.dma_start(t[tuple(slice(None) for _ in t.shape)], d[name]).then_inc(const_in, 16)
            def split0(u):
                head_of(U_QKV0 + u, WQH[:, u, :])

            for u in range(7):
                split0(u)
            normalise(0, each=lambda tt: split0(7 + tt) if 7 + tt < 12 else None)
            finish(act, 1)

            act.wait_ge(a["init"], 2)

            def swap_halves(unit):
                U = unit[0]
                act.wait_ge(a["proj"], U + 1)
                after(act, a["q"], U)
                ps = PS[:, 5, 0:HALF].rearrange("p (h d) -> p h d", h=H0 // 2)
                copy(A_sw[:, :, 0:D0 // 2], ps[:, :, D0 // 2:D0])
                copy(A_sw[:, :, D0 // 2:D0], ps[:, :, 0:D0 // 2], a["sw"])

            def stack_heads(unit):
                U, _, _, _, is_k = unit
                act.wait_ge(a["q"], U + 1)
                after(act, a["tp"], U * 2)
                copy(STK[:, :, 0:D0].bitcast(F32R), A_q[:, :, :])
                at = 2 * D0 if is_k else D0
                copy(STK[:, :, at:at + D0].bitcast(F32R), A_q[:, :, :], a["hi"])

            def take_values(unit):
                U, b, half, tl, is_k = unit
                n = b * 4 + (2 * half + is_k)
                act.wait_ge(a["vps"], n + 1)
                if not isinstance(b, int) or b >= 1:
                    act.wait_ge(a["pv"], b * G0 + (4 * half - 4))
                ps = PS[:, 3, 0:HALF].rearrange("p (n e d) -> p n e d", e=2, d=D0)
                pairs = slice(8 * half, 8 * half + 8)
                copy(V0[:, is_k, pairs, 0, 0:D0], ps[:, :, 0, :])
                copy(V0[:, is_k, pairs, 1, D0:2 * D0], ps[:, :, 1, :], a["vcp"])

            def take_stacks(unit):
                U, _, half, tl, is_k = unit
                act.wait_ge(a["tp"], U * 2 + 1)
                copy((kT if is_k else qT)[:, 8 * half:8 * half + 4, tl * P:(tl + 1) * P],
                     PS[:, 6, :].rearrange("p (n t) -> p n t", n=4), a["eva"])

            def attend(b):
                for g in range(G0):
                    t, unit, earlier = b * G0 + g, prepared(b, g), prepared(b, g, 1)
                    for tb in range(2):
                        if unit and tb == 1:
                            swap_halves(unit)
                        act.wait_ge(a["neg"], t * 2 + (tb + 1))
                        after(act, a["pt"], t * 2)
                        for h in range(4):
                            n, at = order(h), (h // 2) * SEQ
                            blocks = slice(n, n + 1) if tb == 0 else slice(4 + 2 * n, 6 + 2 * n)
                            ins = nc.scalar.activation(A_p[:, blocks, :].rearrange("p n t -> p (n t)"),
                                                       PS[:, 2 * tb + h % 2, at:at + (tb + 1) * P], ACT.Exp, scale=float(D0) ** -0.5,
                                                       bias=A_nb[:, 4 * tb + n:4 * tb + n + 1], accum_out=A_sum[:, 4 * tb + n:4 * tb + n + 1])
                        ins.then_inc(a["exp"], 1)
                    if earlier:
                        take_stacks(earlier)
                    if unit:
                        stack_heads(unit)
                    if unit and g % 4 in (1, 2):
                        take_values(unit)
                    for tb in range(2):
                        act.wait_ge(a["pt"], t * 2 + (tb + 1))
                        after(act, a["pv"], t)
                        copy(A_pT[:, 4 * tb:4 + 8 * tb, :], PS[:, 5 + tb:6 + 2 * tb, :].rearrange("p n (h t) -> p (n h) t", h=4), a["pe"])

            for g in FIRST:
                unit = prepared(-1, g)
                swap_halves(unit)
                stack_heads(unit)
                if g % 4 in (1, 2):
                    take_values(unit)
                if g < G0 - 1:
                    take_stacks(unit)
            attend(0)
            with act.Fori(1, NB - 1) as b:
                attend(b)
            attend(NB - 1)
            finish(act, 2)

            def ffn_heads(n, p, weights):
                for c in weights:
                    if not isinstance(n, int) or n >= 2:
                        act.wait_ge(*((f["dps"], n * 8 - 8) if c == 2 else (f["gu"], n * 2 - 2)))
                    act.wait_ge(f["w"], n * 3 + (c + 1))
                    copy(FWH[p][:, c, :], F_w[:, c, :], f["hi"])

            def ffn_gate(n, p):
                for h in range(2):
                    act.wait_ge(f["gu"], n * 2 + (h + 1))
                    if not isinstance(n, int) or n >= 1:
                        act.wait_ge(f["a"], n * 2 + (h - 1))
                    nc.scalar.activation(F_sg[:, h, :], PS[:, h, :], ACT.Sigmoid).then_inc(f["sg"], 1)
                if not isinstance(n, int) or n >= 2:
                    act.wait_ge(f["dps"], n * 8 - 8)
                for h in range(2):
                    act.wait_ge(f["i"], n * 2 + (h + 1))
                    copy(FIH[p][:, h * C:(h + 1) * C], F_i[:, h, :], f["ih"])

            def ffn_step(n, p):
                ffn_heads(n + 1, 1 - p, (0, 1))
                ffn_gate(n, p)
                ffn_heads(n + 1, 1 - p, (2,))

            ffn_heads(0, 0, (0, 1, 2))
            ffn_step(0, 0)
            with act.Fori(0, (NF - 3) // 2) as i:
                ffn_step(i * 2 + 1, 1)
                ffn_step(i * 2 + 2, 0)
            ffn_step(NF - 2, 1)
            ffn_gate(NF - 1, 0)
            finish(act, 3)

            for t, name in [(bv, "bv"), (bvr, "bvr"), (AG1, "ag1"), (BT1, "bt1"), (b1, "b1"), (gb1, "gb1")]:
                act.dma_start(t[tuple(slice(None) for _ in t.shape)], d[name]).then_inc(small_in, 16)
            for u in range(KT):
                head_of(U_W1 + u, W1H[:, u, :])
            normalise(1, XT1)
            for b in range(NB):
                s = 3 * (b % 2)
                if b == 1:
                    for n in range(2):
                        act.wait_ge(c1["lat_ps"], n + 1)
                        copy(LAT[:, n * C:(n + 1) * C], PS[0:R1, 6 + n, :], c1["lat_cp"])
                act.wait_ge(c1["st"], b + 1)
                act.wait_ge(c1["pv"], 2 * b)
                nc.scalar.activation(A1[:, :], PS[:, s:s + 3, :].rearrange("p n c -> p (n c)"), ACT.Sigmoid,
                                     scale=4.0 * P ** -0.5).then_inc(c1["sig"], 1)
            finish(act, 4)

            for t, name in [(AR2, "ar2"), (coresT, "coresT"), (BwT, "bwT"), (b2, "b2")]:
                act.dma_start(t[tuple(slice(None) for _ in t.shape)], d[name]).then_inc(small_in, 16)
            for u in range(KT):
                head_of(U_WB2 + u, W2H[:, u, :])
            act.wait_ge(d2["g_ps"], 1)
            nc.scalar.activation(GH[:, :], PS[:, 7, :], ACT.Copy, scale=2.0).then_inc(d2["gh"], 1)
            normalise(2, XT2)
            act.wait_ge(d2["c"], 3)
            nc.scalar.activation(e_p[:, :, :], e_p[:, :, :], ACT.Exp).then_inc(d2["ax"], 1)
            for n in range(2):
                act.wait_ge(d2["tp"], n + 1)
                copy(UH[:, n * C:(n + 1) * C], PS[:, n, :], d2["uh"])
            finish(act, 5)

            def l2_heads(g, units):
                for u in units:
                    n = U_L2 + u
                    head(n % RAW, g * (U_L2_G // RAW) + (n // RAW + 1), E_WH[:, u, :])

            def l2_slot(g, j, step, one, two, next_heads=None, more_heads=None):
                i, q = g * NB + j, 1 - j % 2
                if step:
                    act.wait_ge(e2["pq"], i + 1)
                    after(act, e2["q"], i * 2)
                    qs = PS[:, 0:2, :].rearrange("p n (h t) -> p (n h) t", h=2)
                    copy(E_sw[0:64, 0:4, :], qs[64:P, :, :])
                    copy(E_sw[64:P, 0:4, :], qs[0:64, :, :], e2["sw"])
                if one:
                    for tb in range(2):
                        act.wait_ge(e2["neg"], i * 2 + (tb - 1))
                        if two:
                            act.wait_ge(e2["pt"], i * 2 + (tb - 3))
                        for h in range(4):
                            at = (h % 2) * SEQ
                            blocks = slice(h, h + 1) if tb == 0 else slice(4 + 2 * h, 6 + 2 * h)
                            last = nc.scalar.activation(E_p[:, blocks, :].rearrange("p n t -> p (n t)"),
                                                        PS[:, 3 + 2 * tb + h // 2, at:at + (tb + 1) * P], ACT.Exp, scale=float(D2) ** -0.5,
                                                        bias=E_nb[:, 4 * tb + h:4 * tb + h + 1], accum_out=E_sum[:, 4 * tb + h:4 * tb + h + 1])
                        last.then_inc(e2["exp"], 1)
                if step:
                    act.wait_ge(e2["pk"], i + 1)
                    copy(E_sw[0:64, 4, :], PS[64:P, 2, 0:SEQ])
                    copy(E_sw[64:P, 4, :], PS[0:64, 2, 0:SEQ], e2["sw"])
                    after(act, e2["vtp"], i)
                    copy(vT2[:, :], PS[:, 2, SEQ:2 * SEQ], e2["vt"])
                if one:
                    for tb, n in ((0, slice(0, 1)), (1, slice(1, 3))):
                        act.wait_ge(e2["pt"], i * 2 + (tb - 1))
                        if two:
                            act.wait_ge(e2["pv"], i * 2 + (tb - 3))
                        copy(PH[:, n, :], PS[:, 3 + n.start:3 + n.stop, :], e2["phi"])
                if step:
                    for n, heads in enumerate((slice(0, 4), slice(4, 5))):
                        act.wait_ge(e2["q"], i * 2 + (n + 1))
                        after(act, e2["sc"], i * 2)
                        copy(QKH[:, heads, :], E_T[:, heads, :], e2["qhi"])
                if next_heads is not None:
                    next_heads()
                if step:
                    act.wait_ge(e2["vtp"], i + 1)
                    after(act, e2["pv"], i * 2)
                    copy(VH[:, :, :], PS[:, 2, SEQ:2 * SEQ].rearrange("p (s d) -> p s d", s=2), e2["vhi"])
                if one:
                    for tb in range(2):
                        act.wait_ge(e2["pv"], i * 2 + (tb - 1))
                        if not isinstance(i, int) or i >= 3:
                            act.wait_ge(e2["wo"], i * 2 + (tb - 5))
                        copy(OH[q][:, tb, :], PS[:, 3 + tb, :], e2["ohi"])
                if more_heads is not None:
                    more_heads()

            def l2_group(g, first, more):
                def next_heads():
                    l2_heads(g + 1, range(6))

                def sum_head():
                    act.wait_ge(g3["s"], g + 1)
                    copy(WSH[:, bass.ds(g, 1), :].rearrange("p a n -> p (a n)"), G_wo[:, :], g3["wsh"])

                def wo_heads():
                    if not first:
                        act.wait_ge(e2["wo"], g * 8)
                    l2_heads(g, range(6, U_L2_G))

                for j in range(NB):
                    l2_slot(g, j, True, not first or j >= 1, not first or j >= 2, next_heads if j == NB - 1 and more else None,
                            {1: wo_heads, 2: sum_head}.get(j))

            l2_heads(0, range(6))
            l2_group(0, True, True)
            with act.Fori(1, KV2 - 1) as g:
                l2_group(g, False, True)
            l2_group(KV2 - 1, False, False)
            l2_slot(KV2, 0, False, True, True)
            finish(act, 6)

            for t, name in [(pk3, "pk3"), (zp3, "zp3"), (sc3, "sc3"), (b3, "b3")]:
                act.dma_start(t[tuple(slice(None) for _ in t.shape)], d[name]).then_inc(small_in, 16)
            for t, name in [(bq3, "bq3"), (MZ, "mz3")]:
                act.dma_start(t[tuple(slice(None) for _ in t.shape)], d[name]).then_inc(g3["in"], 16)
            for k in range(KT):
                act.wait_ge(f["w"], 3 * NF + k + 1)
                copy(W3H[:, k, :], t3[:, k, :], f["hi"])
            for u in range(H3):
                head_of(U_L3 + u, L3H[:, u, :])
            normalise(3)
            finish(act, 7)
            act.wait_ge(g3["in"], 16 * 2)

            def recall(b, heads):
                for h in heads:
                    n = b * H3 + h
                    if turns(n, 0):
                        act.wait_ge(g3["m"], n + 1)
                        after(act, g3["sum"], n)
                        nc.scalar.activation(G_e[:, :], G_m[:, :], ACT.Exp).then_inc(g3["e"], 1)
                        nc.scalar.activation(G_r[:, :], PS[:, h % 2, 0:SEQ], ACT.Relu, bias=bq3[:, h:h + 1]).then_inc(g3["r"], 1)
                    if turns(n, 2):
                        act.wait_ge(g3["tp"], n - 1)
                        after(act, g3["wo"], n - 3)
                        copy(NH3[h % 2][:, :], PS[:, 4 + h % 2, 0:SEQ], g3["hi"])

            recall(0, range(H3))
            with act.Fori(1, NB) as b:
                recall(b, range(H3))
            recall(NB, range(3))
            finish(act, 8)

        @block.vector
        def _(dve):
            V = nc.vector

            def statistics(l, tt):
                V.bn_stats(stats[:, tt, :], X[:, tt, :]).then_inc(ln["stat"], 1)

            def normalise(l, used=None):
                B = LN[l]
                ln_wait(dve, l, "stat", TT)
                for tt in range(TT):
                    V.bn_aggr(B["mv"][:, tt, :], stats[:, tt, :]).then_inc(ln["aggr"], 1)
                ln_wait(dve, l, "aggr", TT)
                V.tensor_scalar(B["var"][:, :], B["mv"][:, :, 1], 1e-5, None, ALU.add).then_inc(ln["var"], 1)
                ln_wait(dve, l, "sd", 1)
                V.reciprocal(B["tmp"][:, :], B["sd"][:, :]).then_inc(ln["c"], 1)
                ln_wait(dve, l, "c", 1)
                V.tensor_tensor(B["tmp"][:, :], B["tmp"][:, :], B["var"][:, :], ALU.mult).then_inc(ln["c"], 1)
                ln_wait(dve, l, "c", 2)
                V.tensor_tensor(B["tmp"][:, :], B["tmp"][:, :], B["sd"][:, :], ALU.add).then_inc(ln["c"], 1)
                ln_wait(dve, l, "c", 3)
                V.tensor_scalar(B["tmp"][:, :], B["tmp"][:, :], 0.5, None, ALU.mult).then_inc(ln["c"], 1)
                ln_wait(dve, l, "c", 4)
                V.reciprocal(B["rstd"][:, :], B["tmp"][:, :]).then_inc(ln["c"], 1)
                ln_wait(dve, l, "c", 5)
                LAG, DENSE_LAG = 2, 5
                for tt in range(TT + DENSE_LAG):
                    if tt < TT:
                        if tt >= XNB:
                            ln_wait(dve, l, "tp", tt - XNB + 1)
                            if used is not None:
                                dve.wait_ge(used, tt - XNB + 1)
                        V.tensor_scalar(B["xn"][:, tt % XNB, :], X[:, tt, :], B["mv"][:, tt, 0:1], B["rstd"][:, tt:tt + 1],
                                        ALU.subtract, ALU.mult).then_inc(ln["xn"], 1)
                    if LAG <= tt < TT + LAG:
                        t = tt - LAG
                        ln_wait(dve, l, "hi", t + 1)
                        span = slice(t * P, (t + 1) * P)
                        V.tensor_tensor(XNL[:, :, span], PS[:, t % TB, :].rearrange("p (k t) -> p k t", k=KT),
                                        f32(XNH[:, :, span]), ALU.subtract).then_inc(ln["lo"], 1)
                    if l >= 1 and tt >= DENSE_LAG:
                        add_dense(l, tt - DENSE_LAG)

            def add_dense(l, tt):
                n = (l - 1) * TT + tt
                dve.wait_ge(ffn_ps, n + 1)
                V.tensor_tensor(X[:, tt, :], X[:, tt, :], PS[:, 4 + tt % 3, :], ALU.add).then_inc(ffn_x, 1)

            for tt in range(TT):
                if tt % 2 == 0:
                    dve.wait_ge(x_in[tt // 2], 32)
                statistics(0, tt)
            normalise(0)
            finish(dve, 1)

            dve.wait_ge(const_in, 16 * 9)

            def cosines(unit):
                U, _, _, tl, _ = unit
                dve.wait_ge(a["sw"], U + 1)
                V.tensor_tensor(A_T1[:, :, :], PS[:, 5, 0:HALF].rearrange("p (h d) -> p h d", h=H0 // 2),
                                rope0c[:, tl, :].unsqueeze(1).broadcast_to([P, H0 // 2, D0]), ALU.mult).then_inc(a["t1"], 1)

            def rotate(unit):
                U = unit[0]
                dve.wait_ge(a["t1"], U + 1)
                dve.wait_ge(a["t2"], U + 1)
                after(dve, a["hi"], U)
                V.tensor_tensor(A_q[:, :, :], A_T1[:, :, :], A_sw[:, :, :], ALU.add).then_inc(a["q"], 1)

            def stack_rests(unit):
                U, _, _, _, is_k = unit
                dve.wait_ge(a["hi"], U + 1)
                at = D0 if is_k else 2 * D0
                V.tensor_tensor(STK[:, :, at:at + D0], A_q[:, :, :], STK[:, :, 0:D0], ALU.subtract).then_inc(a["lo"], 1)

            def take_stacks(unit):
                U, _, half, tl, is_k = unit
                dve.wait_ge(a["tp"], U * 2 + 2)
                V.tensor_copy((kT if is_k else qT)[:, 8 * half + 4:8 * half + 8, tl * P:(tl + 1) * P],
                              PS[:, 7, :].rearrange("p (n t) -> p n t", n=4)).then_inc(a["evd"], 1)

            def add_branch(b, tl):
                dve.wait_ge(a["wo_ps"], b * 2 + (tl + 1))
                xt = X[:, bass.ds(b * 2 + tl, 1), :].rearrange("p a c -> p (a c)")
                V.tensor_tensor(xt, xt, PS[:, 3 - tl, :], ALU.add).then_inc(a["x"], 1)

            def attend(b):
                later = not isinstance(b, int) or b >= 1
                for g in range(G0):
                    t, unit, earlier = b * G0 + g, prepared(b, g), prepared(b, g, 1)
                    for tb in range(2):
                        dve.wait_ge(a["sc"], t * 2 + (tb + 1))
                        V.tensor_reduce(A_mx[:, 4 * tb:4 * tb + 4],
                                        PS[:, 2 * tb:2 * tb + 2, :].rearrange("p n (h s) -> p (n h) s", h=2)[:, :, 0:(tb + 1) * P],
                                        AXIS.X, ALU.max).then_inc(a["mx"], 1)
                        dve.wait_ge(a["mx"], t * 2 + (tb + 1))
                        V.tensor_scalar(A_nb[:, 4 * tb:4 * tb + 4], A_mx[:, 4 * tb:4 * tb + 4], -float(D0) ** -0.5, None, ALU.mult)\
                         .then_inc(a["neg"], 1)
                    for tb in range(2):
                        if tb == 1:
                            if unit:
                                cosines(unit)
                            if earlier:
                                take_stacks(earlier)
                            if unit:
                                rotate(unit)
                        dve.wait_ge(a["exp"], t * 2 + (tb + 1))
                        V.reciprocal(A_rec[:, 4 * tb:4 * tb + 4], A_sum[:, 4 * tb:4 * tb + 4]).then_inc(a["rec"], 1)
                        dve.wait_ge(a["rec"], t * 2 + (tb + 1))
                        for n in range(4):
                            blocks = slice(n, n + 1) if tb == 0 else slice(4 + 2 * n, 6 + 2 * n)
                            ins = V.tensor_scalar(A_p[:, blocks, :], A_p[:, blocks, :], A_rec[:, 4 * tb + n:4 * tb + n + 1], None, ALU.mult)
                        ins.then_inc(a["pn"], 1)
                    if unit:
                        stack_rests(unit)
                    if g % 2 == 0 and (g or later):
                        dve.wait_ge(a["pv"], t)
                        if g == 2:
                            after(dve, a["wo_ps"], b * 2)
                        V.tensor_copy(OT0[:, (g // 2 - 1) % KT, :], PS[:, 4, 0:SEQ]).then_inc(a["ot"], 1)
                    if g < 2 and later:
                        add_branch(b - 1, g)

            for g in FIRST:
                unit = prepared(-1, g)
                cosines(unit)
                rotate(unit)
                stack_rests(unit)
                if g < G0 - 1:
                    take_stacks(unit)
            attend(0)
            with dve.Fori(1, NB - 1) as b:
                attend(b)
            attend(NB - 1)
            dve.wait_ge(a["pv"], NB * G0)
            V.tensor_copy(OT0[:, KT - 1, :], PS[:, 4, 0:SEQ]).then_inc(a["ot"], 1)
            for tl in range(2):
                add_branch(NB - 1, tl)
            finish(dve, 2)

            dve.wait_ge(f["zin"], 32)
            V.tensor_tensor(zq[:, :].rearrange("p (w e) -> p w e", e=8), zw[:, :].unsqueeze(2).broadcast_to([NF, 3 * C // 8, 8]),
                            zshift[:, :].unsqueeze(1).broadcast_to([NF, 3 * C // 8, 8]), ALU.logical_shift_right).then_inc(f["z"], 1)
            dve.wait_ge(f["z"], 1)
            V.tensor_scalar(zq[:, :], zq[:, :], 15, None, ALU.bitwise_and).then_inc(f["z"], 1)
            dve.wait_ge(f["z"], 2)
            V.tensor_scalar(z1[:, :], zq[:, :], 1, None, ALU.add).then_inc(f["z"], 1)
            V.memset(F_acc[:, :, :], 0.0).then_inc(f["z"], 1)

            def unpack(n, p):
                dve.wait_ge(f[f"in{p}"], in_count(n, p))
                for c in range(3):
                    if not isinstance(n, int) or n >= 1:
                        dve.wait_ge(f["w"], n * 3 + (c - 2))
                    if c or not isinstance(n, int) or n >= 1:
                        dve.wait_ge(f["t"], n * 3 + c)
                    V.tensor_scalar(F_q[:, :], words[p][:, c, :], shift_k[:, 0:1], 15, ALU.logical_shift_right, ALU.bitwise_and)\
                     .then_inc(f["q"], 1)
                    dve.wait_ge(f["q"], n * 3 + (c + 1))
                    V.tensor_tensor(F_t[:, c, :], F_q[:, :], zb[p][:, c, :], ALU.subtract).then_inc(f["t"], 1)

            LOADS = 3 * 8 + 2

            def in_count(n, p):
                if isinstance(n, int):
                    return 16 * LOADS * (n // 2 + 1)
                return n * (8 * LOADS) + (8 * LOADS if p else 16 * LOADS)

            def weight_rests(n, p, weights):
                for c in weights:
                    dve.wait_ge(f["hi"], n * 3 + (c + 1))
                    V.tensor_tensor(FWL[p][:, c, :], F_w[:, c, :], f32(FWH[p][:, c, :]), ALU.subtract).then_inc(f["lo"], 1)

            def gated(n, p):
                for h in range(2):
                    dve.wait_ge(f["sg"], n * 2 + (h + 1))
                    V.tensor_tensor(F_a[:, h, :], F_sg[:, h, :], PS[:, h, :], ALU.mult).then_inc(f["a"], 1)
                    dve.wait_ge(f["a"], n * 2 + (h + 1))
                    V.tensor_tensor(F_i[:, h, :], F_a[:, h, :], PS[:, 2 + h, :], ALU.mult).then_inc(f["i"], 1)

            def gated_rests(n, p):
                for h in range(2):
                    dve.wait_ge(f["ih"], n * 2 + (h + 1))
                    V.tensor_tensor(FIL[p][:, h * C:(h + 1) * C], F_i[:, h, :], f32(FIH[p][:, h * C:(h + 1) * C]),
                                    ALU.subtract).then_inc(f["il"], 1)

            def accumulate(n):
                dve.wait_ge(f["z"], 4)
                for tt in range(TT):
                    dve.wait_ge(f["dps"], n * 8 + (tt + 1))
                    V.tensor_tensor(F_acc[:, tt, :], F_acc[:, tt, :], PS[:, 4 + tt % 4, :], ALU.add).then_inc(f["acc"], 1)

            def ffn_step(n, p, m=None):
                unpack(n + 1, 1 - p)
                weight_rests(n + 1, 1 - p, (0, 1))
                gated(n, p)
                if m is not None:
                    accumulate(m)
                gated_rests(n, p)
                weight_rests(n + 1, 1 - p, (2,))

            unpack(0, 0)
            weight_rests(0, 0, (0, 1, 2))
            ffn_step(0, 0)
            with dve.Fori(0, (NF - 3) // 2) as i:
                ffn_step(i * 2 + 1, 1, i * 2)
                ffn_step(i * 2 + 2, 0, i * 2 + 1)
            ffn_step(NF - 2, 1, NF - 3)
            gated(NF - 1, 0)
            gated_rests(NF - 1, 0)
            accumulate(NF - 2)
            accumulate(NF - 1)
            dve.wait_ge(f["acc"], NF * TT)
            for tt in range(TT):
                V.tensor_copy(F_half[:, tt, :], F_acc[:, tt, :]).then_inc(f["half"], 1)
            for tt in range(TT):
                dve.wait_ge(f["half"], tt + 1)
                V.tensor_tensor(X[:, tt, :], X[:, tt, :], F_half[:, tt, :], ALU.add).then_inc(f["x"], 1)
                if tt >= 1:
                    dve.wait_ge(f["x"], tt)
                    statistics(1, tt - 1)
            dve.wait_ge(f["x"], TT)
            statistics(1, TT - 1)
            finish(dve, 3)

            count = [0]

            def chain(ins, signal):
                count[0] += 1
                ins.then_inc(signal, 1)
                dve.wait_ge(signal, count[0])

            dve.wait_ge(small_in, SMALL_L1)
            V.scalar_tensor_tensor(bv_abs[:, :], bv[:, :], -1.0, bv[:, :], ALU.mult, ALU.max).then_inc(c1["abs"], 1)
            chain(V.scalar_tensor_tensor(vrow[:, :, :], bvr[:, :, :], -1.0, bvr[:, :, :], ALU.mult, ALU.max), c1["c"])
            chain(V.tensor_reduce(vr_al[:, :], vrow[:, :, :], AXIS.X, ALU.add), c1["c"])
            chain(V.tensor_scalar(vr_al[:, :], vr_al[:, :], 1.0 / P, None, ALU.mult), c1["c"])
            chain(V.tensor_scalar(vr_sg[:, :, :], bvr[:, :, :], 0.0, 2.0, ALU.is_ge, ALU.mult), c1["c"])
            chain(V.tensor_scalar(vr_sg[:, :, :], vr_sg[:, :, :], -1.0, None, ALU.add), c1["c"])
            chain(V.tensor_tensor(vr_sg[:, :, :], vr_sg[:, :, :], vr_al[:, :].unsqueeze(2).broadcast_to([P, 4, P]), ALU.mult), c1["c"])
            chain(V.tensor_tensor(vr_sg[:, :, :], vr_sg[:, :, :], bvr[:, :, :], ALU.subtract), c1["c"])
            chain(V.tensor_tensor(vrow[:, :, :], vr_sg[:, :, :], bvr[:, :, :], ALU.add), c1["c"])
            chain(V.tensor_scalar(bv_sg[:, :], bv[:, :], 0.0, 2.0, ALU.is_ge, ALU.mult), c1["c"])
            dve.wait_ge(c1["al"], 1)
            chain(V.scalar_tensor_tensor(bv_sg[:, :], bv_sg[:, :], -1.0, PS[:, 7, 0:12], ALU.add, ALU.mult), c1["c"])
            chain(V.tensor_tensor(bv_sg[:, :], bv_sg[:, :], bv[:, :], ALU.subtract), c1["c"])
            chain(V.tensor_tensor(bv_q[:, :], bv_sg[:, :], bv[:, :], ALU.add), c1["c"])
            chain(V.tensor_tensor(qk1[:, :], bv_q[:, 0:4], bv_q[:, 4:8], ALU.mult), c1["c"])
            normalise(1, c1["v"])

            dve.wait_ge(c1["lo_ps"], 2)
            count[0] = 0
            for n in range(2):
                last = V.tensor_copy(LA[:, 4 * n:4 * n + 4, :],
                                     PS[:, 3 + 4 * n, 0:4 * (R1 + E1)].rearrange("p (t r) -> p t r", t=4))
            chain(last, c1["gate"])
            gs = LA[:, :, R1:R1 + E1]
            chain(V.tensor_tensor(gs, gs, gb1[:, :].unsqueeze(1).broadcast_to([P, TT, E1]), ALU.add), c1["gate"])
            chain(V.tensor_reduce(g_m[:, :], gs, AXIS.X, ALU.max), c1["gate"])
            chain(V.tensor_tensor(g_ne[:, :, :], gs, g_m[:, :].unsqueeze(2).broadcast_to([P, TT, E1]), ALU.is_lt), c1["gate"])
            for k in range(3):
                if k:
                    chain(V.tensor_tensor(g_ne[:, :, k], g_ne[:, :, k], g_ne[:, :, k - 1], ALU.mult), c1["gate"])
                r = 8 << k
                chain(V.tensor_tensor(LA[:, :, r:2 * r], LA[:, :, r:2 * r],
                                      g_ne[:, :, k].unsqueeze(2).broadcast_to([P, TT, r]), ALU.mult), c1["gate"])
            gates = count[0]
            assert gates == 9
            for b in range(NB):
                dve.wait_ge(c1["sig"], b + 1)
                w0 = A1[:, 0:1024].rearrange("p (h t) -> p h t", h=4)[:, :, 0:P]
                w1 = A1[:, 1024:1536].rearrange("p (h t) -> p h t", h=4)
                seen = mask01[:, :].unsqueeze(1).broadcast_to([P, 4, P])
                V.tensor_tensor(w0, w0, seen, ALU.mult)
                V.tensor_tensor(w1, w1, seen, ALU.mult).then_inc(c1["mask"], 1)
                for tb in range(2):
                    tt = 2 * b + tb
                    dve.wait_ge(c1["pv"], tt + 1)
                    dve.wait_ge(bias_in, tt + 1)
                    V.tensor_tensor(X[:, tt, :], X[:, tt, :], PS[:, 6 + tb, :], ALU.add).then_inc(c1["xa"], 1)
                for tb in range(2):
                    dve.wait_ge(c1["xa"], 2 * b + tb + 1)
                    statistics(2, 2 * b + tb)
            finish(dve, 4)

            normalise(2)
            dve.wait_ge(d2["gh"], 1)
            V.scalar_tensor_tensor(GL[:, :], PS[:, 7, :], 2.0, f32(GH[:, :]), ALU.mult, ALU.subtract).then_inc(d2["gl"], 1)
            dve.wait_ge(d2["lo_ps"], 1)
            count[0] = 0
            chain(V.tensor_copy(axr[:, :, :], PS[:, 3, 0:TT * (R2 + E2)].rearrange("p (t r) -> p t r", t=TT)), d2["c"])
            chain(V.tensor_reduce(e_m[:, :], axr[:, :, R2:R2 + E2], AXIS.X, ALU.max), d2["c"])
            chain(V.tensor_tensor(e_p[:, :, :], axr[:, :, R2:R2 + E2], e_m[:, :].unsqueeze(2).broadcast_to([P, TT, E2]),
                                  ALU.subtract), d2["c"])
            dve.wait_ge(d2["ax"], 1)
            chain(V.tensor_reduce(e_s[:, :], e_p[:, :, :], AXIS.X, ALU.add), d2["c"])
            chain(V.reciprocal(e_s[:, :], e_s[:, :]), d2["c"])
            chain(V.tensor_tensor(e_p[:, :, :], e_p[:, :, :], e_s[:, :].unsqueeze(2).broadcast_to([P, TT, E2]), ALU.mult), d2["c"])
            for tt in range(TT):
                last = V.tensor_tensor(U2[:, tt, :, :], e_p[:, tt, :].unsqueeze(2).broadcast_to([P, E2, R2]),
                                       axr[:, tt, 0:R2].unsqueeze(1).broadcast_to([P, E2, R2]), ALU.mult)
            chain(last, d2["c"])
            assert count[0] == 7
            for n in range(2):
                dve.wait_ge(d2["uh"], n + 1)
                V.tensor_tensor(UL[:, n * C:(n + 1) * C], PS[:, n, :], f32(UH[:, n * C:(n + 1) * C]), ALU.subtract)\
                 .then_inc(d2["ul"], 1)
            for tt in range(TT):
                dve.wait_ge(d2["up"], tt + 1)
                dve.wait_ge(bias_in, TT + tt + 1)
                V.tensor_tensor(X[:, tt, :], X[:, tt, :], PS[:, 2 + tt % 4, :], ALU.add).then_inc(d2["x"], 1)
            finish(dve, 5)

            def l2_slot(g, j, step, one, two, final=False):
                i, q = g * NB + j, 1 - j % 2

                def maxima(tb):
                    dve.wait_ge(e2["sc"], i * 2 + (tb - 1))
                    V.tensor_reduce(E_mx[:, 4 * tb:4 * tb + 4],
                                    PS[:, 3 + 2 * tb:5 + 2 * tb, :].rearrange("p n (h s) -> p (n h) s", h=2)[:, :, 0:(tb + 1) * P],
                                    AXIS.X, ALU.max).then_inc(e2["mx"], 1)
                    dve.wait_ge(e2["mx"], i * 2 + (tb - 1))
                    V.tensor_scalar(E_nb[:, 4 * tb:4 * tb + 4], E_mx[:, 4 * tb:4 * tb + 4], -float(D2) ** -0.5, None, ALU.mult)\
                     .then_inc(e2["neg"], 1)

                def probabilities(tb):
                    dve.wait_ge(e2["exp"], i * 2 + (tb - 1))
                    V.reciprocal(E_rec[:, 4 * tb:4 * tb + 4], E_sum[:, 4 * tb:4 * tb + 4]).then_inc(e2["rec"], 1)
                    dve.wait_ge(e2["rec"], i * 2 + (tb - 1))
                    for h in range(4):
                        blocks = slice(h, h + 1) if tb == 0 else slice(4 + 2 * h, 6 + 2 * h)
                        last = V.tensor_scalar(E_p[:, blocks, :], E_p[:, blocks, :], E_rec[:, 4 * tb + h:4 * tb + h + 1], None, ALU.mult)
                    last.then_inc(e2["pn"], 1)

                def cosines(n, heads):
                    if n == 0:
                        dve.wait_ge(e2["sw"], i * 2 + 1)
                        after(dve, e2["qhi"], i * 2)
                    else:
                        dve.wait_ge(e2["vt"], i + 1)
                    V.tensor_tensor(E_T[:, heads, :], PS[:, 0:3, :].rearrange("p n (h t) -> p (n h) t", h=2)[:, heads, :],
                                    rope2c[:, :].unsqueeze(1).broadcast_to([P, heads.stop - heads.start, SEQ]), ALU.mult)\
                     .then_inc(e2["t1"], 1)

                def rotated(n, heads):
                    dve.wait_ge(e2["t1"], i * 2 + (n + 1))
                    dve.wait_ge(e2["t2"], i * 2 + (n + 1))
                    V.tensor_tensor(E_T[:, heads, :], E_T[:, heads, :], E_sw[:, heads, :], ALU.add).then_inc(e2["q"], 1)

                def rotated_rests(n, heads):
                    dve.wait_ge(e2["qhi"], i * 2 + (n + 1))
                    V.tensor_tensor(QKL[:, heads, :], E_T[:, heads, :], f32(QKH[:, heads, :]), ALU.subtract).then_inc(e2["qlo"], 1)

                def add_branch(tb):
                    dve.wait_ge(e2["wo"], i * 2 + (tb - 3))
                    tt = 2 * ((j - 2) % NB) + tb
                    V.tensor_tensor(X[:, tt, :], X[:, tt, :], PS[:, 7 - tb, :], ALU.add).then_inc(e2["x"], 1)

                Q, K = (0, slice(0, 4)), (1, slice(4, 5))
                if one:
                    maxima(0)
                    maxima(1)
                if step:
                    cosines(*Q)
                if one:
                    probabilities(0)
                    probabilities(1)
                if step:
                    rotated(*Q)
                    cosines(*K)
                if one:
                    for tb, n in ((0, slice(0, 1)), (1, slice(1, 3))):
                        dve.wait_ge(e2["phi"], i * 2 + (tb - 1))
                        V.tensor_tensor(PL[:, n, :], PS[:, 3 + n.start:3 + n.stop, :], f32(PH[:, n, :]), ALU.subtract)\
                         .then_inc(e2["plo"], 1)
                if two:
                    add_branch(0)
                if step:
                    rotated(*K)
                    rotated_rests(*Q)
                    rotated_rests(*K)
                if two:
                    add_branch(1)
                if step:
                    dve.wait_ge(e2["vhi"], i + 1)
                    V.tensor_tensor(VL[:, :, :], PS[:, 2, SEQ:2 * SEQ].rearrange("p (s d) -> p s d", s=2), f32(VH[:, :, :]),
                                    ALU.subtract).then_inc(e2["vlo"], 1)
                if one:
                    for tb in range(2):
                        dve.wait_ge(e2["ohi"], i * 2 + (tb - 1))
                        V.tensor_tensor(OL[q][:, tb, :], PS[:, 3 + tb, :], f32(OH[q][:, tb, :]), ALU.subtract).then_inc(e2["olo"], 1)
                if final:
                    for tb in range(2):
                        dve.wait_ge(e2["x"], i * 2 + (tb - 3))
                        statistics(3, 2 * ((j - 2) % NB) + tb)


            for j in range(NB):
                l2_slot(0, j, True, j >= 1, j >= 2)
            with dve.Fori(1, KV2 - 1) as g:
                for j in range(NB):
                    l2_slot(g, j, True, True, True)
            for j in range(NB):
                l2_slot(KV2 - 1, j, True, True, True, j >= 2)
            l2_slot(KV2, 0, False, True, True, True)
            l2_slot(KV2, 1, False, False, True, True)
            finish(dve, 6)

            dve.wait_ge(small_in, SMALL_F3)
            for k in range(KT):
                V.tensor_scalar(q3[:, k, :], pk3[:, k // 2, :], 4 * (k % 2), 15, ALU.logical_shift_right, ALU.bitwise_and)\
                 .then_inc(f["q"], 1)
            for k in range(KT):
                dve.wait_ge(f["q"], 3 * NF + k + 1)
                V.tensor_tensor(t3[:, k, :], q3[:, k, :], zp3[:, :], ALU.subtract).then_inc(f["t"], 1)
            for k in range(KT):
                dve.wait_ge(f["hi"], 3 * NF + k + 1)
                V.tensor_tensor(W3L[:, k, :], t3[:, k, :], f32(W3H[:, k, :]), ALU.subtract).then_inc(f["lo"], 1)
            normalise(3)
            dve.wait_ge(bias_in, 3 * TT)
            finish(dve, 7)
            dve.wait_ge(g3["in"], 16 * 2)

            def recall(b, heads):
                for h in heads:
                    n = b * H3 + h
                    if turns(n, 0):
                        dve.wait_ge(g3["qps"], n + 1)
                        after(dve, g3["e"], n)
                        V.tensor_scalar(G_m[:, :], PS[:, h % 2, 0:SEQ], bq3[:, h:h + 1], 0.0, ALU.add, ALU.min).then_inc(g3["m"], 1)
                    if turns(n, 2):
                        dve.wait_ge(g3["hi"], n - 1)
                        V.tensor_tensor(NL3[h % 2][:, :], PS[:, 4 + h % 2, 0:SEQ], f32(NH3[h % 2][:, :]), ALU.subtract).then_inc(g3["lo"], 1)
                    if turns(n, 0):
                        dve.wait_ge(g3["e"], n + 1)
                        dve.wait_ge(g3["r"], n + 1)
                        after(dve, g3["nps"], n - 1)
                        V.tensor_tensor(G_s[h % 2][:, :], G_e[:, :], G_r[:, :], ALU.add).then_inc(g3["sum"], 1)
                    if turns(n, 1):
                        dve.wait_ge(g3["nps"], n)
                        o = PS[:, 3 - h % 2, 0:2 * (P + 1)].rearrange("p (t e) -> p t e", t=2)
                        V.tensor_scalar(G_rec[:, :], o[:, :, P], 1e-6, None, ALU.add).then_inc(g3["rc"], 1)
                        dve.wait_ge(g3["rc"], n * 2 - 1)
                        V.reciprocal(G_rec[:, :], G_rec[:, :]).then_inc(g3["rc"], 1)
                        dve.wait_ge(g3["rc"], n * 2)
                        after(dve, g3["tp"], n - 2)
                        V.tensor_tensor(G_o[1 - h % 2][:, :, :], o[:, :, 0:P], G_rec[:, :].unsqueeze(2).broadcast_to([P, 2, P]), ALU.mult)\
                         .then_inc(g3["mul"], 1)
                    if h == 2 and turns(n, H3):
                        dve.wait_ge(g3["wo"], b * H3)
                        for tl in range(2):
                            xt = X[:, bass.ds(b * 2 + (tl - 2), 1), :].rearrange("p a c -> p (a c)")
                            V.tensor_tensor(xt, xt, PS[:, 6 + tl, :], ALU.add).then_inc(g3["xo"], 1)

            recall(0, range(H3))
            with dve.Fori(1, NB) as b:
                recall(b, range(H3))
            recall(NB, range(3))
            finish(dve, 8)

        @block.tensor
        def _(pe):
            mm = nc.tensor.matmul

            def normalise(l, pairs=False, dense=None):
                xn = LN[l]["xn"]
                for tt in range(TT + 1):
                    if tt < TT:
                        ln_wait(pe, l, "xn", tt + 1)
                        if tt >= TB:
                            ln_wait(pe, l, "lo", tt - TB + 1)
                        for k in range(KT):
                            src = xn[:, tt % XNB, k * P:(k + 1) * P]
                            if pairs:
                                at = (k // 2) * 2 * P + k % 2
                                src = xn[:, tt % XNB, at:at + 2 * P - 1:2]
                            last = nc.tensor.transpose(PS[:, tt % TB, k * P:(k + 1) * P], src, ident[:, :])
                        last.then_inc(ln["tp"], 1)
                    if dense is not None and tt >= 1:
                        ln_wait(pe, l, "lo", tt)
                        dense(tt - 1)

            def dense_tile(l, tt, WH, WL):
                n = (l - 1) * TT + tt
                if tt >= 3:
                    pe.wait_ge(ffn_x, n - 2)
                span = slice(tt * P, (tt + 1) * P)
                for k in range(KT):
                    last = product3(PS[:, 4 + tt % 3, :], XNH[:, k, span], XNL[:, k, span], WH[:, k, :], WL[:, k, :], k == 0, k == KT - 1)
                last.then_inc(ffn_ps, 1)

            pe.wait_ge(const_in, 16 * 9)
            normalise(0)
            finish(pe, 1)

            pe.wait_ge(w_lo, 12)
            pe.wait_ge(wo_in, 16 * KT)
            pe.wait_ge(a["init"], 2)

            def dense(o, w, half, tl):
                for k in range(KT):
                    span, cols = slice(tl * P, (tl + 1) * P), slice(half * HALF, (half + 1) * HALF)
                    last = product3(o, SGH[:, k, span], SGL[:, k, span], WQH[:, 4 * w + k, cols], WQL[:, 4 * w + k, cols], k == 0, k == KT - 1)
                return last

            def project(unit):
                U, b, half, tl, is_k = unit
                if half == 0 and is_k == 0:
                    pe.wait_ge(a[f"stage{tl}"], b * 32 + 32)
                after(pe, a["t1"], U)
                dense(PS[:, 5, 0:HALF], is_k, half, tl).then_inc(a["proj"], 1)

            def values(unit):
                U, b, half, _, tl = unit
                after(pe, a["vcp"], b * 4 + (2 * half + tl))
                dense(PS[:, 3, 0:HALF], 2, half, tl).then_inc(a["vps"], 1)

            def transposes(unit):
                U = unit[0]
                pe.wait_ge(a["lo"], U + 1)
                for e in range(2):
                    after(pe, a["evd" if e else "eva"], U)
                    for n in range(4):
                        pair = 4 * e + n
                        last = nc.tensor.transpose(PS[:, 6 + e, n * P:(n + 1) * P],
                                                   STK[:, 2 * pair:2 * pair + 2, :].rearrange("p h r -> p (h r)"), ident[:, :])
                    last.then_inc(a["tp"], 1)

            def rows(g, h):
                return slice((h % 2) * S0, (h % 2 + 1) * S0), 2 * g + h // 2

            def weighted_values(t, g, pairs):
                pe.wait_ge(a["pe"], t * 2)
                if g % 2 == 0:
                    after(pe, a["ot"], pairs)
                for n in range(2):
                    c = (2 * g + n) % 4
                    rows32 = slice(32 * c, 32 * c + 32)
                    for s in range(2):
                        for e in range(2):
                            h = order(2 * n + e)
                            stationary = V0[:, s, 2 * g + n, e, :]
                            if s == 0:
                                last = mm(PS[rows32, 4, 0:SEQ].rearrange("p (s t) -> p s t", s=2), stationary, A_pT[:, h:8:4, :],
                                          start=(e == 0), stop=False, skip_group_check=True, tile_position=(0, 32 * c))
                            else:
                                last = mm(PS[rows32, 4, P:SEQ], stationary, A_pT[:, 8 + h, :], start=False, stop=(e == 1),
                                          skip_group_check=True, tile_position=(0, 32 * c))
                last.then_inc(a["pv"], 1)

            def output(b, tl):
                if tl == 0:
                    pe.wait_ge(a["ot"], b * 4 + 4)
                for k in range(KT):
                    last = mm(PS[:, 3 - tl, :], OT0[:, k, tl * P:(tl + 1) * P], wo0[:, k, :], start=(k == 0), stop=(k == KT - 1))
                last.then_inc(a["wo_ps"], 1)

            def attend(b):
                later = not isinstance(b, int) or b >= 1
                for g in range(G0):
                    t, unit, earlier = b * G0 + g, prepared(b, g), prepared(b, g, 1)
                    if g % 4 == 0:
                        pe.wait_ge(a["eva"], b * G0 + (g + 4))
                        pe.wait_ge(a["evd"], b * G0 + (g + 4))
                    for tb in range(2):
                        if tb == 1:
                            pe.wait_ge(a["vcp"], b * 4 + (2 + sum(g > v for v in (1, 2, 5, 6) if prepared(b, v))))
                            if later and g in (1, 2):
                                pe.wait_ge(a["x"], b * 2 + (g - 2))
                        for h in range(4):
                            r, n = rows(g, h)
                            at, bank = (h // 2) * SEQ, 2 * tb + h % 2
                            mm(PS[:, bank, at:at + SEQ], qT[r, n, tb * P:(tb + 1) * P], kT[r, n, :], start=True, stop=False,
                               skip_group_check=True)
                            last = mm(PS[:, bank, at + tb * P:at + (tb + 1) * P], identb[:, :], mask_ts[:, :], start=False, stop=True,
                                      skip_group_check=True)
                        last.then_inc(a["sc"], 1)
                    if unit:
                        after(pe, a["pe"], t * 2)
                        project(unit)
                    if earlier:
                        after(pe, a["pe"], t * 2)
                        transposes(earlier)
                    if g or later:
                        weighted_values(t, (g - 1) % G0, b * KT + (g - 1) // 2)
                    pe.wait_ge(a["exp"], t * 2 + 2)
                    if g < 2 and later:
                        output(b - 1, g)
                    if unit and g % 4 in (1, 2):
                        values(unit)
                    for tb in range(2):
                        pe.wait_ge(a["pn"], t * 2 + (tb + 1))
                        if tb == 0 and unit:
                            pe.wait_ge(a["t1"], unit[0] + 1)
                        if tb == 1 and earlier:
                            pe.wait_ge(a["eva"], earlier[0] + 1)
                            pe.wait_ge(a["evd"], earlier[0] + 1)
                        for n in range(4):
                            for s in range(tb + 1):
                                last = nc.tensor.transpose(PS[:, 5 + tb + s, n * P:(n + 1) * P], A_p[:, n if tb == 0 else 4 + 2 * n + s, :], ident[:, :])
                        last.then_inc(a["pt"], 1)

            for g in FIRST:
                unit = prepared(-1, g)
                project(unit)
                if g % 4 in (1, 2):
                    values(unit)
                if g < G0 - 1:
                    transposes(unit)
            attend(0)
            with pe.Fori(1, NB - 1) as b:
                attend(b)
            attend(NB - 1)
            weighted_values(NB * G0, G0 - 1, None)
            for tl in range(2):
                output(NB - 1, tl)
            finish(pe, 2)

            def gate_up(n, p):
                if not isinstance(n, int) or n >= 1:
                    pe.wait_ge(f["i"], n * 2)
                pe.wait_ge(f["lo"], n * 3 + 2)
                for h in range(2):
                    for c in range(2):
                        for k in range(KT):
                            span, half = slice(k * P, (k + 1) * P), slice(h * C, (h + 1) * C)
                            last = product3(PS[:, 2 * c + h, :], FWH[p][:, c, span], FWL[p][:, c, span], XNH[:, k, half], XNL[:, k, half],
                                            k == 0, k == KT - 1)
                    last.then_inc(f["gu"], 1)

            def down(n, p, first=False):
                pe.wait_ge(f["lo"], n * 3 + 3)
                pe.wait_ge(f["il"], n * 2 + 2)
                for tt in range(TT):
                    if not first or tt >= 4:
                        pe.wait_ge(f["acc"], n * 8 + (tt - 3))
                    span = slice(tt * P, (tt + 1) * P)
                    product3(PS[:, 4 + tt % 4, :], FIH[p][:, span], FIL[p][:, span], FWH[p][:, 2, :], FWL[p][:, 2, :], True, True)\
                        .then_inc(f["dps"], 1)

            gate_up(0, 0)
            gate_up(1, 1)
            down(0, 0, True)
            gate_up(2, 0)
            down(1, 1)
            with pe.Fori(1, (NF - 1) // 2) as i:
                gate_up(i * 2 + 1, 1)
                down(i * 2, 0)
                gate_up(i * 2 + 2, 0)
                down(i * 2 + 1, 1)
            down(NF - 1, 0)
            finish(pe, 3)

            pe.wait_ge(a["init"], 3)
            pe.wait_ge(c1["abs"], 1)
            mm(PS[:, 7, 0:12], inv[:, :], bv_abs[:, :], start=True, stop=True).then_inc(c1["al"], 1)
            pe.wait_ge(w_lo, U_W1 + KT)

            def l1_tile(tt):
                dense_tile(1, tt, W1H, W1L)
                at = (tt % 4) * (R1 + E1)
                for k in range(KT):
                    last = mm(PS[:, 3 + 4 * (tt // 4), at:at + R1 + E1], XT1[:, k, tt * P:(tt + 1) * P], AG1[:, k, :], start=(k == 0),
                              stop=(k == KT - 1), skip_group_check=True)
                if tt % 4 == 3:
                    last.then_inc(c1["lo_ps"], 1)

            pe.wait_ge(small_in, SMALL_L1)
            normalise(1, dense=l1_tile)

            def l1_scores(b):
                s = 3 * (b % 2)
                if b >= 2:
                    pe.wait_ge(c1["sig"], b - 1)
                elif b == 1:
                    pe.wait_ge(c1["gate"], 1)
                    pe.wait_ge(ffn_x, TT)
                t0 = b * SEQ
                for h in range(4):
                    mm(PS[:, s + h // 2, (h % 2) * SEQ:(h % 2 + 1) * SEQ], K1[:, h, t0:t0 + P], XT1[:, h, t0:t0 + SEQ], start=True, stop=True,
                       skip_group_check=True)
                for h in range(4):
                    last = mm(PS[:, s + 2, h * P:(h + 1) * P], K1[:, h, t0 + P:t0 + SEQ], XT1[:, h, t0 + P:t0 + SEQ], start=True, stop=True,
                              skip_group_check=True)
                last.then_inc(c1["st"], 1)

            def l1_values(b):
                pe.wait_ge(c1["mask"], b + 1)
                if b >= 1:
                    pe.wait_ge(c1["xa"], 2 * b)
                else:
                    pe.wait_ge(c1["lat_cp"], 2)
                for tb in range(2):
                    span = slice((2 * b + tb) * P, (2 * b + tb + 1) * P)
                    mm(PS[:, 6 + tb, :], LAT[:, span], BT1[:, :], start=True, stop=False, skip_group_check=True)
                    for h in range(4):
                        o = PS[:, 6 + tb, h * P:(h + 1) * P]
                        last = mm(o, A1[:, h * SEQ + tb * P:h * SEQ + (tb + 1) * P], V1[:, 2 * b, h * P:(h + 1) * P], start=False, stop=(tb == 0),
                                  skip_group_check=True)
                        if tb:
                            last = mm(o, A1[:, 1024 + h * P:1024 + (h + 1) * P], V1[:, 2 * b + 1, h * P:(h + 1) * P], start=False, stop=True,
                                      skip_group_check=True)
                    last.then_inc(c1["pv"], 1)

            pe.wait_ge(c1["k1"], TT)
            pe.wait_ge(c1["v"], TT)
            ln_wait(pe, 1, "lo", TT)
            l1_scores(0)
            pe.wait_ge(c1["gate"], 9)
            pe.wait_ge(ffn_x, TT)
            for tt in range(TT):
                last = nc.tensor.transpose(PS[0:R1, 6 + tt // 4, (tt % 4) * P:(tt % 4 + 1) * P], LA[:, tt, 0:R1], ident[:, :])
                if tt % 4 == 3:
                    last.then_inc(c1["lat_ps"], 1)
            for b in range(NB):
                if b + 1 < NB:
                    l1_scores(b + 1)
                l1_values(b)
            finish(pe, 4)

            pe.wait_ge(small_in, SMALL_L2)
            mm(PS[:, 7, :], coresT[:, :], BwT[:, :], start=True, stop=True).then_inc(d2["g_ps"], 1)
            pe.wait_ge(w_lo, U_WB2 + KT)

            def l2_tile(tt):
                at = tt * (R2 + E2)
                for k in range(KT):
                    last = mm(PS[:, 3, at:at + R2 + E2], XT2[:, k, tt * P:(tt + 1) * P], AR2[:, k, :], start=(k == 0), stop=(k == KT - 1),
                              skip_group_check=True)
                if tt == TT - 1:
                    last.then_inc(d2["lo_ps"], 1)
                dense_tile(2, tt, W2H, W2L)

            normalise(2, dense=l2_tile)
            pe.wait_ge(d2["c"], 7)
            for tt in range(TT):
                last = nc.tensor.transpose(PS[:, tt // 4, (tt % 4) * P:(tt % 4 + 1) * P],
                                           U2[:, tt, :, :].rearrange("p e r -> p (e r)"), ident[:, :])
                if tt % 4 == 3:
                    last.then_inc(d2["tp"], 1)
            pe.wait_ge(d2["gl"], 1)
            pe.wait_ge(ffn_x, 2 * TT)
            for tt in range(TT):
                if tt >= 4:
                    pe.wait_ge(d2["x"], tt - 3)
                pe.wait_ge(d2["ul"], tt // 4 + 1)
                span = slice(tt * P, (tt + 1) * P)
                product3(PS[:, 2 + tt % 4, :], UH[:, span], UL[:, span], GH[:, :], GL[:, :], True, True).then_inc(d2["up"], 1)
            finish(pe, 5)

            def l2_slot(g, j, step, one, two):
                i, p = g * NB + j, j % 2

                def project(units, signal):
                    for u in units:
                        pe.wait_ge(w_lo, g * U_L2_G + (U_L2 + u + 1))
                        for k in range(KT):
                            span, tok = slice(k * P, (k + 1) * P), slice(j * SEQ, (j + 1) * SEQ)
                            last = product3(PS[:, u // 2, (u % 2) * SEQ:(u % 2 + 1) * SEQ], E_WH[:, u, span], E_WL[:, u, span],
                                            XNH[:, k, tok], XNL[:, k, tok], k == 0, k == KT - 1)
                    last.then_inc(signal, 1)

                def output(tb):
                    if tb == 0:
                        pe.wait_ge(e2["olo"], i * 2 - 2)
                        if not isinstance(i, int) or i >= 3:
                            pe.wait_ge(e2["x"], i * 2 - 4)
                        if j == 2:
                            pe.wait_ge(w_lo, g * U_L2_G + (U_L2 + U_L2_G))
                    for h in range(4):
                        span = slice(h * P, (h + 1) * P)
                        last = product3(PS[:, 7 - tb, :], OH[p][:, tb, span], OL[p][:, tb, span], E_WH[:, 6 + h, :], E_WL[:, 6 + h, :],
                                        h == 0, h == 3)
                    last.then_inc(e2["wo"], 1)

                if step:
                    if not isinstance(i, int) or i >= 1:
                        pe.wait_ge(e2["t1"], i * 2 - 1)
                    project(range(4), e2["pq"])
                if one:
                    pe.wait_ge(e2["qlo"], i * 2)
                    if two:
                        pe.wait_ge(e2["olo"], i * 2 - 2)
                        after(pe, e2["x"], i * 2 - 4)
                    for tb in range(2):
                        t = slice(tb * P, (tb + 1) * P)
                        for h in range(4):
                            at, bank = (h % 2) * SEQ, 3 + 2 * tb + h // 2
                            o = PS[:, bank, at:at + SEQ]
                            mm(o, QKL[:, h, t], QKH[:, 4, :], start=True, stop=False, skip_group_check=True)
                            mm(o, QKH[:, h, t], QKL[:, 4, :], start=False, stop=False, skip_group_check=True)
                            mm(o, QKH[:, h, t], QKH[:, 4, :], start=False, stop=False, skip_group_check=True)
                            last = mm(PS[:, bank, at + tb * P:at + (tb + 1) * P], identb[:, :], mask_ts[:, :], start=False, stop=True,
                                      skip_group_check=True)
                        last.then_inc(e2["sc"], 1)
                if step:
                    after(pe, e2["vlo"], i)
                    project(range(4, 6), e2["pk"])
                if two:
                    output(0)
                if one:
                    for tb in range(2):
                        pe.wait_ge(e2["pn"], i * 2 + (tb - 1))
                        for h in range(4):
                            for s in range(tb + 1):
                                last = nc.tensor.transpose(PS[:, 3 + tb + s, h * P:(h + 1) * P],
                                                           E_p[:, h if tb == 0 else 4 + 2 * h + s, :], ident[:, :])
                        last.then_inc(e2["pt"], 1)
                if two:
                    output(1)
                if step:
                    pe.wait_ge(e2["vt"], i + 1)
                    pe.wait_ge(e2["t1"], i * 2 + 2)
                    for s in range(2):
                        last = nc.tensor.transpose(PS[:, 2, SEQ + s * P:SEQ + (s + 1) * P], vT2[:, s * P:(s + 1) * P], ident[:, :])
                    last.then_inc(e2["vtp"], 1)
                if one:
                    pe.wait_ge(e2["vlo"], i)
                    for tb in range(2):
                        pe.wait_ge(e2["plo"], i * 2 + (tb - 1))
                        for s in range(tb + 1):
                            last = product3(PS[:, 3 + tb, :], VH[:, s, :], VL[:, s, :], PH[:, tb + s, :], PL[:, tb + s, :], s == 0, s == tb)
                        last.then_inc(e2["pv"], 1)

            for j in range(NB):
                l2_slot(0, j, True, j >= 1, j >= 2)
            with pe.Fori(1, KV2) as g:
                for j in range(NB):
                    l2_slot(g, j, True, True, True)
            l2_slot(KV2, 0, False, True, True)
            l2_slot(KV2, 1, False, False, True)
            finish(pe, 6)

            pe.wait_ge(f["lo"], 3 * NF + KT)
            normalise(3, True, lambda tt: dense_tile(3, tt, W3H, W3L))
            finish(pe, 7)
            pe.wait_ge(g3["in"], 16 * 2)
            pe.wait_ge(w_lo, U_L3 + H3)
            pe.wait_ge(g3["wsl"], H3)

            def recall(b, heads):
                for h in heads:
                    n = b * H3 + h
                    if turns(n, 0):
                        after(pe, g3["sum"], n - 1)
                        tok = bass.ds(b * SEQ, SEQ)
                        for k in range(KT):
                            span = slice(k * P, (k + 1) * P)
                            last = product3(PS[:, h % 2, 0:SEQ], L3H[:, h, span], L3L[:, h, span], XNH[:, k, tok], XNL[:, k, tok],
                                            k == 0, k == KT - 1)
                        last.then_inc(g3["qps"], 1)
                    if turns(n, 3):
                        m = (h - 3) % H3
                        if m == 0:
                            after(pe, g3["xo"], b * 2)
                        pe.wait_ge(g3["lo"], n - 2)
                        for tl in range(2):
                            t = slice(tl * P, (tl + 1) * P)
                            last = product3(PS[:, 6 + tl, :], NH3[1 - h % 2][:, t], NL3[1 - h % 2][:, t], WSH[:, m, :], WSL[:, m, :],
                                            m == 0, m == H3 - 1)
                        last.then_inc(g3["wo"], 1)
                    if turns(n, 2):
                        pe.wait_ge(g3["mul"], n - 1)
                        after(pe, g3["lo"], n - 3)
                        for tl in range(2):
                            last = nc.tensor.transpose(PS[:, 4 + h % 2, tl * P:(tl + 1) * P], G_o[h % 2][:, tl, :], ident[:, :])
                        last.then_inc(g3["tp"], 1)
                    if turns(n, 1):
                        pe.wait_ge(g3["sum"], n)
                        after(pe, g3["mul"], n - 2)
                        for tl in range(2):
                            last = mm(PS[:, 3 - h % 2, tl * (P + 1):(tl + 1) * (P + 1)], G_s[1 - h % 2][:, tl * P:(tl + 1) * P],
                                      MZ[:, (h - 1) % H3, :], start=True, stop=True, skip_group_check=True)
                        last.then_inc(g3["nps"], 1)

            recall(0, range(H3))
            with pe.Fori(1, NB) as b:
                recall(b, range(H3))
            recall(NB, range(3))
            finish(pe, 8)


def kernel(**inputs):
    import numpy as np
    import concourse.bacc as bacc
    from concourse import mybir
    from concourse.bass_utils import run_bass_kernel_spmd

    a = {k: np.asarray(v) for k, v in inputs.items()}
    P, KT, C, NF = 128, 4, 512, 11
    f32 = np.float32

    def tiles(w):
        return w.T.reshape(-1, P, w.shape[0])

    def columns(w, order=None):
        t = w.T if order is None else w.T[order]
        return t.reshape(-1, P, w.shape[0] // P, P).transpose(2, 1, 0, 3).reshape(w.shape[0] // P, P, -1)

    def rows(v, n=P):
        return np.broadcast_to(v, (n,) + v.shape)

    def pad(x, axis, size):
        widths = [(0, 0)] * x.ndim
        widths[axis] = (0, size - x.shape[axis])
        return np.pad(x, widths)

    def inner(x, per):
        x = pad(x, 1, NF * P // per)
        return x.reshape(x.shape[0], NF, P // per).transpose(1, 0, 2)

    words = [inner(a[f"L0_ffn_{n}_qweight"], 1).reshape(NF, KT, 16, P).transpose(0, 2, 1, 3).reshape(NF, 16, C) for n in ("gate", "up")]
    words.append(pad(a["L0_ffn_down_qweight"], 0, NF * 16).reshape(NF, 16, C))
    zeros = [inner(a[f"L0_ffn_{n}_zeros"], 8).reshape(NF, C // 8) for n in ("gate", "up")] + [a["L0_ffn_down_zeros"]]
    scales = [inner(a[f"L0_ffn_{n}_scales"], 1).reshape(NF, C) for n in ("gate", "up")] + [a["L0_ffn_down_scales"]]

    qkv = columns(a["L2_attn_Wqkv"])
    wo2 = a["L2_attn_Wo"].T.reshape(32, P, C)
    w2 = np.stack([np.stack([*qkv[4 * g:4 * g + 4], qkv[32 + g], qkv[40 + g], *wo2[4 * g:4 * g + 4]]) for g in range(8)])

    order = np.arange(C).reshape(2, P, 2).transpose(0, 2, 1).reshape(C)
    read = np.arange(32 * P).reshape(8, 4, P)[:, 0].reshape(-1)
    w3 = columns(a["L3_attn_Wq"][read], order)

    def angles(t, h):
        pos = np.arange(t, dtype=f32)
        theta = f32(1.0) / f32(10000.0) ** (np.arange(0, h, 2, dtype=f32) / f32(h))
        return np.outer(pos, theta).astype(f32)

    t0, t2 = angles(256, 16), angles(256, 128)
    cos0 = np.concatenate([np.cos(t0), np.cos(t0)], 1)
    sin0 = np.concatenate([-np.sin(t0), np.sin(t0)], 1)
    cos2 = np.concatenate([np.cos(t2), np.cos(t2)], 1)
    sin2 = np.concatenate([-np.sin(t2), np.sin(t2)], 1)
    bf16 = mybir.dt.np(mybir.dt.bfloat16)
    p = np.arange(P)
    hidden = np.where(p[None, :] > p[:, None], -1e30, 0.0)
    arrays = dict(
        x=a["L0_attn_x"].reshape(8, P, C),
        w0=np.concatenate([tiles(a[f"L0_attn_{n}"]) for n in ("wq", "wk", "wv", "wo")]),
        words=np.stack(words), zeros=np.concatenate(zeros, 1), scales=np.concatenate(scales, 1),
        bv=np.concatenate([a[f"L1_attn_bv_{n}"].T for n in "qkv"], 1), bvr=rows(a["L1_attn_bv_v"]),
        w1=tiles(a["L1_ffn_W"]), b1=rows(a["L1_ffn_b"]), gb1=rows(a["L1_ffn_gate_b"]),
        ag1=np.concatenate([a["L1_ffn_A"].T, a["L1_ffn_gate_w"].T], 1).reshape(KT, P, 68).transpose(1, 0, 2),
        bt1=a["L1_ffn_B"].T,
        wb2=tiles(a["L2_ffn_W_base"]), b2=rows(a["L2_ffn_b_base"]),
        ar2=np.concatenate([a["L2_ffn_A_w"].T, a["L2_ffn_router_w"].T], 1).reshape(KT, P, 24).transpose(1, 0, 2),
        coresT=a["L2_ffn_cores"].transpose(2, 0, 1).reshape(16, P), bwT=a["L2_ffn_B_w"].T, w2=w2,
        w3=w3, wo3=a["L3_attn_Wo"].T.reshape(8, 4, P, C), bq3=a["L3_attn_bq"][read].reshape(8, P).T,
        mz3=np.concatenate([a["L3_attn_M"], a["L3_attn_z"][:, :, None]], 2).transpose(1, 0, 2),
        pk3=a["L3_ffn_weight_packed"].reshape(C, 2, P).transpose(2, 1, 0), zp3=rows(a["L3_ffn_zero_point"][:, 0]),
        sc3=rows(a["L3_ffn_scale"][:, 0]), b3=rows(a["L3_ffn_bias"]),
        ident=np.eye(P, dtype=f32), identb=np.eye(P, dtype=bf16), mask_ts=hidden.astype(bf16),
        mask01=(hidden.T == 0).astype(f32),
        shift_k=(4 * (p % 8)).astype(np.int32)[:, None], shift_n=np.broadcast_to(4 * np.arange(8, dtype=np.int32), (NF, 8)),
        rope0c=cos0.reshape(2, P, 16).transpose(1, 0, 2), rope0s=sin0.reshape(2, P, 16).transpose(1, 0, 2),
        rope2c=cos2.T, rope2s=sin2.T)

    nc = bacc.Bacc("TRN2", target_bir_lowering=False, num_devices=1)
    fed, d = {}, {}
    for name, x in arrays.items():
        x = np.ascontiguousarray(x)
        fed[f"in_{name}"] = x
        d[name] = nc.dram_tensor(f"in_{name}", x.shape, mybir.dt.from_np(x.dtype), kind="ExternalInput").ap()
    d["z1_scratch"] = nc.dram_tensor("z1_scratch", (NF, 3 * C), mybir.dt.float16, kind="Internal").ap()
    out = nc.dram_tensor("out", (8, P, C), mybir.dt.float32, kind="ExternalOutput").ap()
    build_program(nc, d, out)
    r = run_bass_kernel_spmd(nc, [fed], core_ids=[0])
    return r.results[0]["out"].reshape(4, 256, C)
```

```python
def build_program(nc, d, out):
    from contextlib import ExitStack
    import concourse.bass as bass
    from concourse import mybir

    F32, F32R = mybir.dt.float32, mybir.dt.float32r
    BF16, F16, I32 = mybir.dt.bfloat16, mybir.dt.float16, mybir.dt.int32
    ACT, ALU, AXIS = mybir.ActivationFunctionType, mybir.AluOpType, mybir.AxisListType

    P = 128
    C = 512
    KT = C // P
    TOK = 1024
    TT = TOK // P
    SEQ = 256
    NB = TOK // SEQ
    RAW = 5
    H0, D0 = 32, 16
    G0 = H0 // 4
    HALF = C // 2
    S0 = 64
    NF = 11
    KV2, D2 = 8, 128
    H3 = 8
    R1, E1 = 64, 4
    E2, R2 = 8, 16

    U_QKV0, U_W1 = 0, 12
    U_WB2 = U_W1 + KT
    U_L2 = U_WB2 + KT
    U_L2_G = 10
    U_L3 = U_L2 + KV2 * U_L2_G

    ctx = ExitStack()
    with ctx:
        def sem(name):
            return ctx.enter_context(nc.semaphore(name))

        def keep(name, shape, dt=F32):
            return ctx.enter_context(nc.sbuf_tensor(name, list(shape), dt))

        X = keep("X", [P, TT, C])
        XNH = keep("XNH", [P, KT, TOK], F32R)
        XNL = keep("XNL", [P, KT, TOK], F32R)
        raw = keep("raw", [P, RAW, C])
        ident = keep("ident", [P, P])
        identb = keep("identb", [P, P], BF16)
        mask_ts = keep("mask_ts", [P, P], BF16)
        mask01 = keep("mask01", [P, P])
        shift_k = keep("shift_k", [P, 1], I32)
        rope0c = keep("rope0c", [P, 2, D0])
        rope0s = keep("rope0s", [P, 2, D0])
        rope2c = keep("rope2c", [P, SEQ])
        rope2s = keep("rope2s", [P, SEQ])
        PS = ctx.enter_context(nc.psum_tensor("PS", [P, 8, C], F32))

        def phase():
            return ExitStack()

        def sb(stack, name, shape, dt=F32):
            return stack.enter_context(nc.sbuf_tensor(name, list(shape), dt))

        LN = {}
        stats = keep("stats", [P, TT, 6])
        XNB, TB = 4, 3

        def ln_buffers(stack, l):
            LN[l] = dict(
                mv=sb(stack, f"ln{l}_mv", [P, TT, 2]),
                var=sb(stack, f"ln{l}_var", [P, TT]), sd=sb(stack, f"ln{l}_sd", [P, TT]),
                tmp=sb(stack, f"ln{l}_tmp", [P, TT]), rstd=sb(stack, f"ln{l}_rstd", [P, TT]),
                xn=sb(stack, f"ln{l}_xn", [P, XNB, C]))

        with phase() as early:
            zw = sb(early, "zw", [NF, 3 * C // 8], I32)
            zshift = sb(early, "zshift", [NF, 8], I32)
            zq = sb(early, "zq", [NF, C], I32)
            z1 = sb(early, "z1", [NF, 3 * C], F16)
            words0 = sb(early, "words0", [P, 3, C], I32)
            zb0 = sb(early, "zb0", [P, 3, C], F16)
            scb0 = sb(early, "scb0", [P, 3, C], F16)

            with phase() as st:
                WQH = sb(st, "WQH", [P, 12, C], F32R)
                WQL = sb(st, "WQL", [P, 12, C], F32R)
                SGH = sb(st, "SGH", [P, KT, SEQ], F32R)
                SGL = sb(st, "SGL", [P, KT, SEQ], F32R)
                wo0 = sb(st, "wo0", [P, KT, C])
                A_T1 = sb(st, "A_T1", [P, H0 // 2, D0])
                A_sw = sb(st, "A_sw", [P, H0 // 2, D0])
                A_q = sb(st, "A_q", [P, H0 // 2, D0])
                STK = sb(st, "STK", [P, H0 // 2, S0])
                qT = sb(st, "qT", [P, H0 // 2, SEQ], F32R)
                kT = sb(st, "kT", [P, H0 // 2, SEQ], F32R)
                V0 = sb(st, "V0", [P, 2, H0 // 2, 2, 2 * D0])
                with phase() as st2:
                    ln_buffers(st2, 0)
                A_p = sb(st, "A_p", [P, 12, P])
                A_pT = sb(st, "A_pT", [P, 12, P])
                OT0 = sb(st, "OT0", [P, KT, SEQ])
                A_ps = [A_p, raw[:, 0:3, :].rearrange("p r (n t) -> p (r n) t", t=P)]
                A_mx = sb(st, "A_mx", [P, 8])
                A_nb = sb(st, "A_nb", [P, 8])
                A_sum = sb(st, "A_sum", [P, 8])
                A_rec = sb(st, "A_rec", [P, 8])

            with phase() as mid:
                bv = sb(mid, "bv", [P, 12])
                bvr = sb(mid, "bvr", [P, 4, P])
                bv_abs = sb(mid, "bv_abs", [P, 12])
                bv_sg = sb(mid, "bv_sg", [P, 12])
                bv_q = sb(mid, "bv_q", [P, 12])
                qk1 = sb(mid, "qk1", [P, 4])
                vr_al = sb(mid, "vr_al", [P, 4])
                vr_sg = sb(mid, "vr_sg", [P, 4, P])
                vrow = sb(mid, "vrow", [P, 4, P])
                inv = sb(mid, "inv", [P, P])
                AG1 = sb(mid, "AG1", [P, KT, R1 + E1])
                BT1 = sb(mid, "BT1", [R1, C])
                b1 = sb(mid, "b1", [P, C])
                gb1 = sb(mid, "gb1", [P, E1])

                with phase() as st:
                    F_q = sb(st, "F_q", [P, C], I32)
                    F_t = sb(st, "F_t", [P, 3, C])
                    F_w = sb(st, "F_w", [P, 3, C])
                    FWH0 = sb(st, "FWH0", [P, 3, C], F32R)
                    FWL0 = sb(st, "FWL0", [P, 3, C], F32R)
                    words = [words0, sb(st, "words1", [P, 3, C], I32)]
                    zb = [zb0, sb(st, "zb1", [P, 3, C], F16)]
                    scb = [scb0, sb(st, "scb1", [P, 3, C], F16)]
                    FWH = [FWH0, sb(st, "FWH1", [P, 3, C], F32R)]
                    FWL = [FWL0, sb(st, "FWL1", [P, 3, C], F32R)]
                    F_sg = sb(st, "F_sg", [P, 2, C])
                    F_a = sb(st, "F_a", [P, 2, C])
                    F_i = sb(st, "F_i", [P, 2, C])
                    FIH = [sb(st, f"FIH{p}", [P, TOK], F32R) for p in range(2)]
                    FIL = [sb(st, f"FIL{p}", [P, TOK], F32R) for p in range(2)]
                    F_acc = sb(st, "F_acc", [P, TT, C])
                    F_half = sb(st, "F_half", [P, TT, C], F16)

                with phase() as st:
                    ln_buffers(st, 1)
                    XT1 = sb(st, "XT1", [P, KT, TOK])
                    K1 = sb(st, "K1", [P, KT, TOK])
                    V1 = sb(st, "V1", [P, TT, C])
                    A1 = sb(st, "A1", [P, 1536])
                    W1H = sb(st, "W1H", [P, KT, C], F32R)
                    W1L = sb(st, "W1L", [P, KT, C], F32R)
                    LA = sb(st, "LA", [P, TT, R1 + E1])
                    g_m = sb(st, "g_m", [P, TT])
                    g_ne = sb(st, "g_ne", [P, TT, E1])
                    LAT = sb(st, "LAT", [R1, TOK])

        with phase() as late:
            WSH = sb(late, "WSH", [P, H3, C], F32R)
            WSL = sb(late, "WSL", [P, H3, C], F32R)
            with phase() as st:
                E_WH = sb(st, "E_WH", [P, U_L2_G, C], F32R)
                E_WL = sb(st, "E_WL", [P, U_L2_G, C], F32R)

                with phase() as st2:
                    ln_buffers(st2, 2)
                    XT2 = sb(st2, "XT2", [P, KT, TOK])
                    W2H = sb(st2, "W2H", [P, KT, C], F32R)
                    W2L = sb(st2, "W2L", [P, KT, C], F32R)
                    AR2 = sb(st2, "AR2", [P, KT, R2 + E2])
                    coresT = sb(st2, "coresT", [R2, E2 * R2])
                    BwT = sb(st2, "BwT", [R2, C])
                    b2 = sb(st2, "b2", [P, C])
                    axr = sb(st2, "axr", [P, TT, R2 + E2])
                    e_m = sb(st2, "e_m", [P, TT])
                    e_p = sb(st2, "e_p", [P, TT, E2])
                    e_s = sb(st2, "e_s", [P, TT])
                    U2 = sb(st2, "U2", [P, TT, E2, R2])
                    UH = sb(st2, "UH", [P, TOK], F32R)
                    UL = sb(st2, "UL", [P, TOK], F32R)
                    GH = sb(st2, "GH", [P, C], F32R)
                    GL = sb(st2, "GL", [P, C], F32R)

                wo3 = sb(st, "wo3", [P, 4, C])
                G_wo = sb(st, "G_wo", [P, C])
                E_T = sb(st, "E_T", [P, 5, SEQ])
                E_sw = sb(st, "E_sw", [P, 5, SEQ])
                QKH = sb(st, "QKH", [P, 5, SEQ], F32R)
                QKL = sb(st, "QKL", [P, 5, SEQ], F32R)
                vT2 = sb(st, "vT2", [P, SEQ])
                VH = sb(st, "VH", [P, 2, P], F32R)
                VL = sb(st, "VL", [P, 2, P], F32R)
                E_p = sb(st, "E_p", [P, 12, P])
                PH = sb(st, "PH", [P, 3, C], F32R)
                PL = sb(st, "PL", [P, 3, C], F32R)
                OH = [sb(st, f"OH{p}", [P, 2, C], F32R) for p in range(2)]
                OL = [sb(st, f"OL{p}", [P, 2, C], F32R) for p in range(2)]
                E_mx = sb(st, "E_mx", [P, 8])
                E_nb = sb(st, "E_nb", [P, 8])
                E_sum = sb(st, "E_sum", [P, 8])
                E_rec = sb(st, "E_rec", [P, 8])

            L3H = sb(late, "L3H", [P, H3, C], F32R)
            L3L = sb(late, "L3L", [P, H3, C], F32R)
            bq3 = sb(late, "bq3", [P, H3])
            MZ = sb(late, "MZ", [P, H3, P + 1])
            with phase() as st:
                ln_buffers(st, 3)
                pk3 = sb(st, "pk3", [P, 2, C], I32)
                zp3 = sb(st, "zp3", [P, C])
                sc3 = sb(st, "sc3", [P, C])
                b3 = sb(st, "b3", [P, C])
                q3 = sb(st, "q3", [P, KT, C], I32)
                t3 = sb(st, "t3", [P, KT, C])
                W3H = sb(st, "W3H", [P, KT, C], F32R)
                W3L = sb(st, "W3L", [P, KT, C], F32R)
            with phase() as st:
                G_m = sb(st, "G_m", [P, SEQ])
                G_e = sb(st, "G_e", [P, SEQ])
                G_r = sb(st, "G_r", [P, SEQ])
                G_s = [sb(st, f"G_s{p}", [P, SEQ]) for p in range(2)]
                G_rec = sb(st, "G_rec", [P, 2])
                G_o = [sb(st, f"G_o{p}", [P, 2, P]) for p in range(2)]
                NH3 = [sb(st, f"NH3{p}", [P, SEQ], F32R) for p in range(2)]
                NL3 = [sb(st, f"NL3{p}", [P, SEQ], F32R) for p in range(2)]

        const_in = sem("const_in")
        x_in = [sem(f"x_in{n}") for n in range(TT // 2)]
        wo_in = sem("wo_in")
        small_in = sem("small_in")
        SMALL_L1, SMALL_L2, SMALL_F3 = 16 * 6, 16 * 10, 16 * 14
        bias_in = sem("bias_in")
        ffn_ps = sem("ffn_ps")
        ffn_x = sem("ffn_x")
        raw_in = [sem(f"raw_in{r}") for r in range(RAW)]
        w_hi = sem("w_hi")
        w_lo = sem("w_lo")
        phase_done = sem("phase_done")
        LN_SIGNALS = dict(stat=TT, aggr=TT, var=1, sd=1, c=5, xn=TT, tp=TT, hi=TT, lo=TT)
        ln = {n: sem(f"ln_{n}") for n in LN_SIGNALS}

        def ln_wait(eng, l, name, n):
            eng.wait_ge(ln[name], l * LN_SIGNALS[name] + n)

        def sems(prefix, names):
            return {n: sem(f"{prefix}_{n}") for n in names.split()}

        a = sems("a", "stage0 stage1 init proj sw t1 t2 q hi lo tp ev vps vcp sc mx neg exp rec pn pt pe pd pv ot wo_ps x")

        def prepared(b, g, ago=0):
            v = g + 5 - ago
            at = b + v // G0
            if isinstance(at, int) and at >= NB:
                return None
            return b * G0 + v, at, v % G0 // 4, v % 4 // 2, v % 2

        def turn_before(b, g):
            return g > 0 or not isinstance(b, int) or b > 0

        FIRST = range(3, G0)

        def order(h):
            return (h % 2) * 2 + h // 2

        f = sems("f", "zin z zout in0 in1 q t w hi lo gu sg a i ih il dps acc x")
        c1 = sems("c", "abs al c v k1 lo_ps gate st sig mask pv xa lat_ps lat_cp")
        d2 = sems("d", "lo_ps c ax g_ps gh gl tp uh ul up x")
        e2 = sems("e", "sc mx neg exp rec pn pt phi plo pv ohi olo pq pk sw vt t1 t2 q qhi qlo vtp vhi vlo wo x")
        g3 = sems("g", "in woin s12 s wsh wsl qps m e r sum nps rc mul tp hi lo wo xo out")

        def turns(n, lag):
            return not isinstance(n, int) or 0 <= n - lag < NB * H3

        block = ctx.enter_context(nc.Block())

        def after(eng, signal, n):
            if not isinstance(n, int) or n > 0:
                eng.wait_ge(signal, n)

        def finish(eng, n):
            eng.drain().then_inc(phase_done, 1)
            eng.wait_ge(phase_done, 4 * n)

        def product3(o, sh, sl, mh, ml, first, last):
            nc.tensor.matmul(o, sl, mh, start=first, stop=False)
            nc.tensor.matmul(o, sh, ml, start=False, stop=False)
            return nc.tensor.matmul(o, sh, mh, start=False, stop=last)

        def f32(ap):
            return ap.bitcast(F32)

        @block.sync
        def _(sp):
            for tt in range(TT):
                sp.dma_start(X[:, tt, :], d["x"][tt]).then_inc(x_in[tt // 2], 16)

            def load_unit(n, slot, src):
                if not isinstance(n, int) or n >= RAW:
                    sp.wait_ge(w_lo, n - RAW + 1)
                sp.dma_start(raw[:, slot, :], src).then_inc(raw_in[slot], 16)

            for u in range(12):
                load_unit(U_QKV0 + u, u % RAW, d["w0"][u])
            def stage(b):
                for tl in range(2):
                    if not isinstance(b, int) or b >= 1:
                        sp.wait_ge(a["vps"], b * 4 + (tl - 1))
                    else:
                        ln_wait(sp, 0, "lo", tl + 1)
                    tok, at = bass.ds(b * SEQ + tl * P, P), slice(tl * P, (tl + 1) * P)
                    sp.dma_start(f32(SGH[:, :, at]), f32(XNH[:, :, tok])).then_inc(a[f"stage{tl}"], 16)
                    sp.dma_start(f32(SGL[:, :, at]), f32(XNL[:, :, tok])).then_inc(a[f"stage{tl}"], 16)

            sp.dma_start(zw[:, :], d["zeros"]).then_inc(f["zin"], 16)
            sp.dma_start(zshift[:, :], d["shift_n"]).then_inc(f["zin"], 16)
            stage(0)
            for kt in range(KT):
                sp.dma_start(wo0[:, kt, :], d["w0"][12 + kt]).then_inc(wo_in, 16)
            ln_wait(sp, 0, "lo", TT)
            with sp.Fori(1, NB) as b:
                stage(b)
            sp.wait_ge(f["z"], 9)
            sp.dma_start(d["z1_scratch"], z1[:, :]).then_inc(f["zout"], 16)
            sp.wait_ge(f["zout"], 16)

            def load_tile(n, p):
                if not isinstance(n, int) or n >= 2:
                    sp.wait_ge(f["w"], n * 3 - 3)
                sp.dma_start(words[p][:, :, :], d["words"][bass.ds(n, 1), :, :, :].rearrange("a p c n -> (a p) c n"))\
                  .then_inc(f[f"in{p}"], 16)
                sp.dma_start(zb[p][:, :, :], d["z1_scratch"][bass.ds(n, 1), :].rearrange("a (c n) -> a c n", c=3).broadcast_to([P, 3, C]))\
                  .then_inc(f[f"in{p}"], 16)
                sp.dma_start(scb[p][:, :, :], d["scales"][bass.ds(n, 1), :].rearrange("a (c n) -> a c n", c=3).broadcast_to([P, 3, C]))\
                  .then_inc(f[f"in{p}"], 16)

            load_tile(0, 0)
            sp.wait_ge(a["vps"], 4 * NB)
            with sp.Fori(0, (NF - 1) // 2) as i:
                load_tile(i * 2 + 1, 1)
                load_tile(i * 2 + 2, 0)
            for u in range(KT):
                load_unit(U_W1 + u, (U_W1 + u) % RAW, d["w1"][u])
            for u in range(KT):
                load_unit(U_WB2 + u, (U_WB2 + u) % RAW, d["wb2"][u])

            def load_whole(t, name, signal):
                sp.dma_start(t[tuple(slice(None) for _ in t.shape)], d[name]).then_inc(signal, 16)

            sp.wait_ge(phase_done, 4 * 4)
            for t, name in [(AR2, "ar2"), (coresT, "coresT"), (BwT, "bwT"), (b2, "b2")]:
                load_whole(t, name, small_in)
            def group(g):
                for u in range(U_L2_G):
                    load_unit(g * U_L2_G + (U_L2 + u), (U_L2 + u) % RAW,
                              d["w2"][bass.ds(g, 1), u, :, :].rearrange("a p n -> (a p) n"))
                if isinstance(g, int):
                    sp.wait_ge(phase_done, 4 * 5)
                after(sp, g3["s"], g)
                for q in range(4):
                    sp.dma_start(wo3[:, q, :], d["wo3"][bass.ds(g, 1), q, :, :].rearrange("a p n -> (a p) n")).then_inc(g3["woin"], 16)

            group(0)
            with sp.Fori(1, KV2) as g:
                group(g)
            def load_l3(units):
                for u in units:
                    load_unit(U_L3 + u, (U_L3 + u) % RAW, d["w3"][u])

            load_l3(range(RAW))
            sp.wait_ge(phase_done, 4 * 6)
            for t, name in [(pk3, "pk3"), (zp3, "zp3"), (sc3, "sc3"), (b3, "b3")]:
                load_whole(t, name, small_in)
            for t, name in [(bq3, "bq3"), (MZ, "mz3")]:
                load_whole(t, name, g3["in"])
            load_l3(range(RAW, H3))
            def recall(b):
                for tl in range(2):
                    sp.wait_ge(g3["xo"], b * 2 + (tl + 1))
                    sp.dma_start(out[bass.ds(b * 2 + tl, 1), :, :].rearrange("a p c -> p (a c)"),
                                 X[:, bass.ds(b * 2 + tl, 1), :].rearrange("p a c -> p (a c)")).then_inc(g3["out"], 16)

            recall(0)
            with sp.Fori(1, NB) as b:
                recall(b)
            sp.wait_ge(g3["out"], 16 * TT)

        @block.gpsimd
        def _(pool):
            def rest(n, hi, lo, slot):
                pool.wait_ge(w_hi, n + 1)
                nc.gpsimd.tensor_tensor(lo, raw[:, slot, :], f32(hi), ALU.subtract).then_inc(w_lo, 1)

            nc.gpsimd.memset(STK[:, :, 3 * D0:S0], 0.0).then_inc(a["init"], 1)
            nc.gpsimd.memset(V0[:, :, :, :, :], 0.0).then_inc(a["init"], 1)

            def rests0(units):
                for u in units:
                    rest(U_QKV0 + u, WQH[:, u, :], WQL[:, u, :], u % RAW)

            rests0(range(8))
            finish(pool, 1)
            rests0(range(8, 12))
            pool.wait_ge(const_in, 16 * 9)

            def sines(U, tl):
                pool.wait_ge(a["sw"], U + 1)
                nc.gpsimd.tensor_tensor(A_sw[:, :, :], A_sw[:, :, :], rope0s[:, tl, :].unsqueeze(1).broadcast_to([P, H0 // 2, D0]), ALU.mult)\
                  .then_inc(a["t2"], 1)

            def attend(b):
                for g in range(G0):
                    unit = prepared(b, g)
                    if unit:
                        sines(unit[0], unit[3])

            for g in FIRST:
                unit = prepared(-1, g)
                sines(unit[0], unit[3])
            attend(0)
            with pool.Fori(1, NB - 1) as b:
                attend(b)
            attend(NB - 1)

            def scale_tile(n, p):
                for c in range(3):
                    pool.wait_ge(f["t"], n * 3 + (c + 1))
                    if not isinstance(n, int) or n >= 1:
                        pool.wait_ge(f["lo"], n * 3 + (c - 2))
                    nc.gpsimd.tensor_tensor(F_w[:, c, :], F_t[:, c, :], scb[p][:, c, :], ALU.mult).then_inc(f["w"], 1)

            scale_tile(0, 0)
            finish(pool, 2)
            nc.gpsimd.memset(inv[:, :], 1.0 / P).then_inc(a["init"], 1)
            with pool.Fori(0, (NF - 1) // 2) as i:
                scale_tile(i * 2 + 1, 1)
                scale_tile(i * 2 + 2, 0)
            for tt in range(TT):
                pool.wait_ge(f["acc"], (NF - 2) * TT + tt + 1)
                nc.gpsimd.tensor_tensor(X[:, tt, :], X[:, tt, :], F_half[:, tt, :], ALU.add).then_inc(f["x"], 1)
            finish(pool, 3)
            for u in range(KT):
                rest(U_W1 + u, W1H[:, u, :], W1L[:, u, :], (U_W1 + u) % RAW)
            for tt in range(TT):
                ln_wait(pool, 1, "xn", tt + 1)
                nc.gpsimd.tensor_tensor(V1[:, tt, :], LN[1]["xn"][:, tt % XNB, :], vrow[:, :, :].rearrange("p h e -> p (h e)"), ALU.mult)\
                  .then_inc(c1["v"], 1)
                ln_wait(pool, 1, "hi", tt + 1)
                span = slice(tt * P, (tt + 1) * P)
                nc.gpsimd.tensor_tensor(K1[:, :, span], XT1[:, :, span], qk1[:, :].unsqueeze(2).broadcast_to([P, KT, P]), ALU.mult)\
                  .then_inc(c1["k1"], 1)
            for tt in range(TT):
                pool.wait_ge(ffn_x, tt + 1)
                nc.gpsimd.tensor_tensor(X[:, tt, :], X[:, tt, :], b1[:, :], ALU.add).then_inc(bias_in, 1)
            finish(pool, 4)
            for u in range(KT):
                rest(U_WB2 + u, W2H[:, u, :], W2L[:, u, :], (U_WB2 + u) % RAW)

            def l2_rest(g, u):
                rest(g * U_L2_G + (U_L2 + u), E_WH[:, u, :], E_WL[:, u, :], (U_L2 + u) % RAW)

            for u in range(6):
                l2_rest(0, u)
            pool.wait_ge(small_in, SMALL_L2)
            for tt in range(TT):
                pool.wait_ge(ffn_x, TT + tt + 1)
                nc.gpsimd.tensor_tensor(X[:, tt, :], X[:, tt, :], b2[:, :], ALU.add).then_inc(bias_in, 1)
            finish(pool, 5)
            def l2_sines(i, n):
                heads = (slice(0, 4), slice(4, 5))[n]
                pool.wait_ge(e2["sw"], i * 2 + (n + 1))
                nc.gpsimd.tensor_tensor(E_sw[:, heads, :], E_sw[:, heads, :],
                                        rope2s[:, :].unsqueeze(1).broadcast_to([P, heads.stop - heads.start, SEQ]), ALU.mult)\
                  .then_inc(e2["t2"], 1)

            def l2_pool_group(g, more):
                for j in range(NB):
                    l2_sines(g * NB + j, 0)
                    l2_sines(g * NB + j, 1)
                    if j == 1:
                        for u in range(6, U_L2_G):
                            l2_rest(g, u)
                    if j == 2:
                        sum_wo(g)
                    if j == NB - 1 and more:
                        for u in range(6):
                            l2_rest(g + 1, u)

            def sum_wo(h):
                pool.wait_ge(g3["woin"], h * 64 + 64)
                after(pool, g3["wsl"], h)
                nc.gpsimd.tensor_tensor(wo3[:, 0, :], wo3[:, 0, :], wo3[:, 1, :], ALU.add).then_inc(g3["s12"], 1)
                nc.gpsimd.tensor_tensor(wo3[:, 2, :], wo3[:, 2, :], wo3[:, 3, :], ALU.add).then_inc(g3["s12"], 1)
                pool.wait_ge(g3["s12"], h * 2 + 2)
                nc.gpsimd.tensor_tensor(G_wo[:, :], wo3[:, 0, :], wo3[:, 2, :], ALU.add).then_inc(g3["s"], 1)
                pool.wait_ge(g3["wsh"], h + 1)
                at = bass.ds(h, 1)
                nc.gpsimd.tensor_tensor(WSL[:, at, :].rearrange("p a n -> p (a n)"), G_wo[:, :],
                                        f32(WSH[:, at, :]).rearrange("p a n -> p (a n)"), ALU.subtract).then_inc(g3["wsl"], 1)

            l2_pool_group(0, True)
            with pool.Fori(1, KV2 - 1) as g:
                l2_pool_group(g, True)
            l2_pool_group(KV2 - 1, False)
            finish(pool, 6)
            pool.wait_ge(small_in, SMALL_F3)
            for k in range(KT):
                pool.wait_ge(f["t"], 3 * NF + k + 1)
                nc.gpsimd.tensor_tensor(t3[:, k, :], t3[:, k, :], sc3[:, :], ALU.mult).then_inc(f["w"], 1)
            for u in range(H3):
                rest(U_L3 + u, L3H[:, u, :], L3L[:, u, :], (U_L3 + u) % RAW)
            for tt in range(TT):
                pool.wait_ge(ffn_x, 2 * TT + tt + 1)
                nc.gpsimd.tensor_tensor(X[:, tt, :], X[:, tt, :], b3[:, :], ALU.add).then_inc(bias_in, 1)
            finish(pool, 7)
            finish(pool, 8)

        @block.scalar
        def _(act):
            def copy(o, i, signal=None):
                ins = nc.scalar.activation(o, i, ACT.Copy)
                return ins.then_inc(signal, 1) if signal is not None else ins

            def head(slot, use, hi):
                act.wait_ge(raw_in[slot], use * 16)
                copy(hi, raw[:, slot, :], w_hi)

            def head_of(n, hi):
                head(n % RAW, n // RAW + 1, hi)

            def normalise(l, XT=None, each=None, first=None):
                ln_wait(act, l, "var", 1)
                nc.scalar.activation(LN[l]["sd"][:, :], LN[l]["var"][:, :], ACT.Sqrt).then_inc(ln["sd"], 1)
                if first is not None:
                    first()
                for tt in range(TT):
                    ln_wait(act, l, "tp", tt + 1)
                    bank = PS[:, tt % TB, :].rearrange("p (k t) -> p k t", k=KT)
                    if XT is not None:
                        copy(XT[:, :, tt * P:(tt + 1) * P], bank)
                    copy(XNH[:, :, tt * P:(tt + 1) * P], bank, ln["hi"])
                    if each is not None:
                        each(tt)

            consts = [(ident, "ident"), (identb, "identb"), (mask_ts, "mask_ts"), (mask01, "mask01"), (shift_k, "shift_k"), (rope0c, "rope0c"), (rope0s, "rope0s"),
                      (rope2c, "rope2c"), (rope2s, "rope2s")]
            for t, name in consts:
                act.dma_start(t[tuple(slice(None) for _ in t.shape)], d[name]).then_inc(const_in, 16)
            def split0(u):
                head_of(U_QKV0 + u, WQH[:, u, :])

            def first_splits():
                for u in range(4):
                    split0(u)

            normalise(0, each=lambda tt: split0(4 + tt), first=first_splits)
            finish(act, 1)

            def ffn_heads(n, p, weights):
                for c in weights:
                    if not isinstance(n, int) or n >= 2:
                        act.wait_ge(*((f["dps"], n * 8 - 8) if c == 2 else (f["gu"], n * 2 - 2)))
                    act.wait_ge(f["w"], n * 3 + (c + 1))
                    copy(FWH[p][:, c, :], F_w[:, c, :], f["hi"])

            def swap_halves(unit):
                U = unit[0]
                act.wait_ge(a["proj"], U + 1)
                after(act, a["q"], U)
                ps = PS[:, 5, 0:HALF].rearrange("p (h d) -> p h d", h=H0 // 2)
                copy(A_sw[:, :, 0:D0 // 2], ps[:, :, D0 // 2:D0])
                copy(A_sw[:, :, D0 // 2:D0], ps[:, :, 0:D0 // 2], a["sw"])

            def stack_heads(unit):
                U, _, _, _, is_k = unit
                act.wait_ge(a["q"], U + 1)
                after(act, a["tp"], U)
                copy(STK[:, :, 0:D0].bitcast(F32R), A_q[:, :, :])
                at = 2 * D0 if is_k else D0
                copy(STK[:, :, at:at + D0].bitcast(F32R), A_q[:, :, :], a["hi"])

            def take_values(unit):
                U, b, half, tl, is_k = unit
                n = b * 4 + (2 * half + is_k)
                act.wait_ge(a["vps"], n + 1)
                if not isinstance(b, int) or b >= 1:
                    act.wait_ge(a["pv"], b * G0 + (4 * half - 4))
                ps = PS[:, 3, 0:HALF].rearrange("p (n e d) -> p n e d", e=2, d=D0)
                pairs = slice(8 * half, 8 * half + 8)
                copy(V0[:, is_k, pairs, 0, 0:D0], ps[:, :, 0, :])
                copy(V0[:, is_k, pairs, 1, D0:2 * D0], ps[:, :, 1, :], a["vcp"])

            def take_stacks(unit):
                U, _, half, tl, is_k = unit
                act.wait_ge(a["tp"], U + 1)
                copy((kT if is_k else qT)[:, 8 * half:8 * half + 8, tl * P:(tl + 1) * P],
                     PS[:, 6:8, :].rearrange("p e (n t) -> p (e n) t", n=4), a["ev"])

            def take_probabilities(t):
                act.wait_ge(a["pt"], t * 2 - 1)
                after(act, a["pv"], t - 1)
                copy(A_pT[:, 0:4, :], PS[:, 5, :].rearrange("p (h t) -> p h t", h=4), a["pe"])

            def attend(b):
                for g in range(G0):
                    t, unit, earlier = b * G0 + g, prepared(b, g), prepared(b, g, 1)
                    if turn_before(b, g):
                        take_probabilities(t)
                    for tb in range(2):
                        act.wait_ge(a["neg"], t * 2 + (tb + 1))
                        after(act, a["pt"], t * 2 - 2)
                        for h in range(4):
                            n, at = order(h), (h // 2) * SEQ
                            blocks = slice(n, n + 1) if tb == 0 else slice(4 + 2 * n, 6 + 2 * n)
                            ins = nc.scalar.activation(A_ps[g % 2][:, blocks, :].rearrange("p n t -> p (n t)"),
                                                       PS[:, 2 * tb + h % 2, at:at + (tb + 1) * P], ACT.Exp, scale=float(D0) ** -0.5,
                                                       bias=A_nb[:, 4 * tb + n:4 * tb + n + 1], accum_out=A_sum[:, 4 * tb + n:4 * tb + n + 1])
                        ins.then_inc(a["exp"], 1)
                    if earlier:
                        take_stacks(earlier)
                    if unit:
                        swap_halves(unit)
                    if unit and g % 4 in (1, 2):
                        take_values(unit)
                    if unit:
                        stack_heads(unit)
                    if isinstance(b, int) and b == NB - 1 and 4 <= g < 7:
                        ffn_heads(0, 0, (g - 4,))

            swap_halves(prepared(-1, FIRST[0]))
            act.wait_ge(a["init"], 2)
            for g in FIRST:
                unit = prepared(-1, g)
                stack_heads(unit)
                if g < G0 - 1:
                    swap_halves(prepared(-1, g + 1))
                if g % 4 in (1, 2):
                    take_values(unit)
                if g < G0 - 1:
                    take_stacks(unit)
            attend(0)
            with act.Fori(1, NB - 1) as b:
                attend(b)
            attend(NB - 1)
            take_probabilities(NB * G0)
            finish(act, 2)

            def ffn_gate(n, p):
                for h in range(2):
                    act.wait_ge(f["gu"], n * 2 + (h + 1))
                    if not isinstance(n, int) or n >= 1:
                        act.wait_ge(f["a"], n * 2 + (h - 1))
                    nc.scalar.activation(F_sg[:, h, :], PS[:, h, :], ACT.Sigmoid).then_inc(f["sg"], 1)
                if not isinstance(n, int) or n >= 2:
                    act.wait_ge(f["dps"], n * 8 - 8)
                for h in range(2):
                    act.wait_ge(f["i"], n * 2 + (h + 1))
                    copy(FIH[p][:, h * C:(h + 1) * C], F_i[:, h, :], f["ih"])

            def ffn_step(n, p):
                ffn_heads(n + 1, 1 - p, (0, 1))
                ffn_gate(n, p)
                ffn_heads(n + 1, 1 - p, (2,))

            ffn_step(0, 0)
            for t, name in [(bv, "bv"), (bvr, "bvr"), (AG1, "ag1"), (BT1, "bt1"), (b1, "b1"), (gb1, "gb1")]:
                act.dma_start(t[tuple(slice(None) for _ in t.shape)], d[name]).then_inc(small_in, 16)
            with act.Fori(0, (NF - 3) // 2) as i:
                ffn_step(i * 2 + 1, 1)
                ffn_step(i * 2 + 2, 0)
            ffn_step(NF - 2, 1)
            ffn_gate(NF - 1, 0)
            finish(act, 3)

            def dense_heads(first, WH):
                for u in range(KT):
                    head_of(first + u, WH[:, u, :])

            normalise(1, XT1, first=lambda: dense_heads(U_W1, W1H))
            for b in range(NB):
                s = 3 * (b % 2)
                if b == 1:
                    for n in range(2):
                        act.wait_ge(c1["lat_ps"], n + 1)
                        copy(LAT[:, n * C:(n + 1) * C], PS[0:R1, 6 + n, :], c1["lat_cp"])
                act.wait_ge(c1["st"], b + 1)
                act.wait_ge(c1["pv"], 2 * b)
                nc.scalar.activation(A1[:, :], PS[:, s:s + 3, :].rearrange("p n c -> p (n c)"), ACT.Sigmoid,
                                     scale=4.0 * P ** -0.5).then_inc(c1["sig"], 1)
            finish(act, 4)

            def l2_heads(g, units):
                for u in units:
                    n = U_L2 + u
                    head(n % RAW, g * (U_L2_G // RAW) + (n // RAW + 1), E_WH[:, u, :])

            normalise(2, XT2, lambda tt: l2_heads(0, range(tt - 2, tt - 1)) if tt >= 2 else None, lambda: dense_heads(U_WB2, W2H))
            act.wait_ge(d2["g_ps"], 1)
            nc.scalar.activation(GH[:, :], PS[:, 7, :], ACT.Copy, scale=2.0).then_inc(d2["gh"], 1)
            act.wait_ge(d2["c"], 3)
            nc.scalar.activation(e_p[:, :, :], e_p[:, :, :], ACT.Exp).then_inc(d2["ax"], 1)
            for n in range(2):
                act.wait_ge(d2["tp"], n + 1)
                copy(UH[:, n * C:(n + 1) * C], PS[:, n, :], d2["uh"])
            finish(act, 5)

            def l2_slot(g, j, step, one, two, next_heads=None, more_heads=None):
                i, q = g * NB + j, 1 - j % 2
                if step:
                    act.wait_ge(e2["pq"], i + 1)
                    after(act, e2["q"], i * 2)
                    qs = PS[:, 0:2, :].rearrange("p n (h t) -> p (n h) t", h=2)
                    copy(E_sw[0:64, 0:4, :], qs[64:P, :, :])
                    copy(E_sw[64:P, 0:4, :], qs[0:64, :, :], e2["sw"])
                if one:
                    for tb in range(2):
                        act.wait_ge(e2["neg"], i * 2 + (tb - 1))
                        if two:
                            act.wait_ge(e2["pt"], i * 2 + (tb - 3))
                        for h in range(4):
                            at = (h % 2) * SEQ
                            blocks = slice(h, h + 1) if tb == 0 else slice(4 + 2 * h, 6 + 2 * h)
                            last = nc.scalar.activation(E_p[:, blocks, :].rearrange("p n t -> p (n t)"),
                                                        PS[:, 3 + 2 * tb + h // 2, at:at + (tb + 1) * P], ACT.Exp, scale=float(D2) ** -0.5,
                                                        bias=E_nb[:, 4 * tb + h:4 * tb + h + 1], accum_out=E_sum[:, 4 * tb + h:4 * tb + h + 1])
                        last.then_inc(e2["exp"], 1)
                if step:
                    act.wait_ge(e2["pk"], i + 1)
                    copy(E_sw[0:64, 4, :], PS[64:P, 2, 0:SEQ])
                    copy(E_sw[64:P, 4, :], PS[0:64, 2, 0:SEQ], e2["sw"])
                    after(act, e2["vtp"], i)
                    copy(vT2[:, :], PS[:, 2, SEQ:2 * SEQ], e2["vt"])
                if one:
                    for tb, n in ((0, slice(0, 1)), (1, slice(1, 3))):
                        act.wait_ge(e2["pt"], i * 2 + (tb - 1))
                        if two:
                            act.wait_ge(e2["pv"], i * 2 + (tb - 3))
                        copy(PH[:, n, :], PS[:, 3 + n.start:3 + n.stop, :], e2["phi"])
                if step:
                    for n, heads in enumerate((slice(0, 4), slice(4, 5))):
                        act.wait_ge(e2["q"], i * 2 + (n + 1))
                        after(act, e2["sc"], i * 2)
                        copy(QKH[:, heads, :], E_T[:, heads, :], e2["qhi"])
                if next_heads is not None:
                    next_heads()
                if step:
                    act.wait_ge(e2["vtp"], i + 1)
                    after(act, e2["pv"], i * 2)
                    copy(VH[:, :, :], PS[:, 2, SEQ:2 * SEQ].rearrange("p (s d) -> p s d", s=2), e2["vhi"])
                if one:
                    for tb in range(2):
                        act.wait_ge(e2["pv"], i * 2 + (tb - 1))
                        if not isinstance(i, int) or i >= 3:
                            act.wait_ge(e2["wo"], i * 2 + (tb - 5))
                        copy(OH[q][:, tb, :], PS[:, 3 + tb, :], e2["ohi"])
                if more_heads is not None:
                    more_heads()

            def l2_group(g, first, more):
                def next_heads():
                    l2_heads(g + 1, range(6))

                def sum_head():
                    act.wait_ge(g3["s"], g + 1)
                    copy(WSH[:, bass.ds(g, 1), :].rearrange("p a n -> p (a n)"), G_wo[:, :], g3["wsh"])

                def wo_heads():
                    if not first:
                        act.wait_ge(e2["wo"], g * 8)
                    l2_heads(g, range(6, U_L2_G))

                for j in range(NB):
                    l2_slot(g, j, True, not first or j >= 1, not first or j >= 2, next_heads if j == NB - 1 and more else None,
                            {1: wo_heads, 2: sum_head}.get(j))

            l2_group(0, True, True)
            with act.Fori(1, KV2 - 1) as g:
                l2_group(g, False, True)
            l2_group(KV2 - 1, False, False)
            l2_slot(KV2, 0, False, True, True)
            finish(act, 6)

            def l3_heads(tt):
                if tt == 1:
                    for k in range(KT):
                        act.wait_ge(f["w"], 3 * NF + k + 1)
                        copy(W3H[:, k, :], t3[:, k, :], f["hi"])
                if 2 <= tt < 6:
                    for u in (2 * tt - 4, 2 * tt - 3):
                        head_of(U_L3 + u, L3H[:, u, :])

            normalise(3, each=l3_heads)
            finish(act, 7)
            act.wait_ge(g3["in"], 16 * 2)

            def recall(b, heads):
                for h in heads:
                    n = b * H3 + h
                    if turns(n, 0):
                        act.wait_ge(g3["m"], n + 1)
                        after(act, g3["sum"], n)
                        nc.scalar.activation(G_e[:, :], G_m[:, :], ACT.Exp).then_inc(g3["e"], 1)
                        nc.scalar.activation(G_r[:, :], PS[:, h % 2, 0:SEQ], ACT.Relu, bias=bq3[:, h:h + 1]).then_inc(g3["r"], 1)
                    if turns(n, 2):
                        act.wait_ge(g3["tp"], n - 1)
                        after(act, g3["wo"], n - 3)
                        copy(NH3[h % 2][:, :], PS[:, 4 + h % 2, 0:SEQ], g3["hi"])

            recall(0, range(H3))
            with act.Fori(1, NB) as b:
                recall(b, range(H3))
            recall(NB, range(3))
            finish(act, 8)

        @block.vector
        def _(dve):
            V = nc.vector

            def statistics(l, tt):
                V.bn_stats(stats[:, tt, :], X[:, tt, :]).then_inc(ln["stat"], 1)

            def normalise(l, used=None, between={}):
                B = LN[l]
                ln_wait(dve, l, "stat", TT)
                for tt in range(TT):
                    V.bn_aggr(B["mv"][:, tt, :], stats[:, tt, :]).then_inc(ln["aggr"], 1)
                ln_wait(dve, l, "aggr", TT)
                V.tensor_scalar(B["var"][:, :], B["mv"][:, :, 1], 1e-5, None, ALU.add).then_inc(ln["var"], 1)
                ln_wait(dve, l, "sd", 1)
                V.reciprocal(B["tmp"][:, :], B["sd"][:, :]).then_inc(ln["c"], 1)
                ln_wait(dve, l, "c", 1)
                V.tensor_tensor(B["tmp"][:, :], B["tmp"][:, :], B["var"][:, :], ALU.mult).then_inc(ln["c"], 1)
                ln_wait(dve, l, "c", 2)
                V.tensor_tensor(B["tmp"][:, :], B["tmp"][:, :], B["sd"][:, :], ALU.add).then_inc(ln["c"], 1)
                ln_wait(dve, l, "c", 3)
                V.tensor_scalar(B["tmp"][:, :], B["tmp"][:, :], 0.5, None, ALU.mult).then_inc(ln["c"], 1)
                ln_wait(dve, l, "c", 4)
                V.reciprocal(B["rstd"][:, :], B["tmp"][:, :]).then_inc(ln["c"], 1)
                ln_wait(dve, l, "c", 5)
                LAG, DENSE_LAG = 2, 7 if l == 2 else 5
                for tt in range(TT + DENSE_LAG):
                    if tt < TT:
                        if tt >= XNB:
                            ln_wait(dve, l, "tp", tt - XNB + 1)
                            if used is not None:
                                dve.wait_ge(used, tt - XNB + 1)
                        V.tensor_scalar(B["xn"][:, tt % XNB, :], X[:, tt, :], B["mv"][:, tt, 0:1], B["rstd"][:, tt:tt + 1],
                                        ALU.subtract, ALU.mult).then_inc(ln["xn"], 1)
                    if LAG <= tt < TT + LAG:
                        t = tt - LAG
                        ln_wait(dve, l, "hi", t + 1)
                        span = slice(t * P, (t + 1) * P)
                        V.tensor_tensor(XNL[:, :, span], PS[:, t % TB, :].rearrange("p (k t) -> p k t", k=KT),
                                        f32(XNH[:, :, span]), ALU.subtract).then_inc(ln["lo"], 1)
                    if tt in between:
                        between[tt]()
                    if l >= 1 and tt >= DENSE_LAG:
                        add_dense(l, tt - DENSE_LAG)

            def add_dense(l, tt):
                n = (l - 1) * TT + tt
                dve.wait_ge(ffn_ps, n + 1)
                V.tensor_tensor(X[:, tt, :], X[:, tt, :], PS[:, 4 + tt % 3, :], ALU.add).then_inc(ffn_x, 1)

            for tt in range(TT):
                if tt % 2 == 0:
                    dve.wait_ge(x_in[tt // 2], 32)
                statistics(0, tt)
            normalise(0)
            finish(dve, 1)

            def zeros_plus_one(c):
                if c == 0:
                    dve.wait_ge(f["zin"], 32)
                else:
                    dve.wait_ge(f["z"], 3 * c)
                V.tensor_tensor(zq[:, :].rearrange("p (w e) -> p w e", e=8),
                                zw[:, c * C // 8:(c + 1) * C // 8].unsqueeze(2).broadcast_to([NF, C // 8, 8]),
                                zshift[:, :].unsqueeze(1).broadcast_to([NF, C // 8, 8]), ALU.logical_shift_right).then_inc(f["z"], 1)
                dve.wait_ge(f["z"], 3 * c + 1)
                V.tensor_scalar(zq[:, :], zq[:, :], 15, None, ALU.bitwise_and).then_inc(f["z"], 1)
                dve.wait_ge(f["z"], 3 * c + 2)
                V.tensor_scalar(z1[:, c * C:(c + 1) * C], zq[:, :], 1, None, ALU.add).then_inc(f["z"], 1)

            dve.wait_ge(const_in, 16 * 9)

            def unpack(n, p, weights=(0, 1, 2)):
                dve.wait_ge(f[f"in{p}"], in_count(n, p))
                for c in weights:
                    if not isinstance(n, int) or n >= 1:
                        dve.wait_ge(f["w"], n * 3 + (c - 2))
                    if c or not isinstance(n, int) or n >= 1:
                        dve.wait_ge(f["t"], n * 3 + c)
                    V.tensor_scalar(F_q[:, :], words[p][:, c, :], shift_k[:, 0:1], 15, ALU.logical_shift_right, ALU.bitwise_and)\
                     .then_inc(f["q"], 1)
                    dve.wait_ge(f["q"], n * 3 + (c + 1))
                    V.tensor_tensor(F_t[:, c, :], F_q[:, :], zb[p][:, c, :], ALU.subtract).then_inc(f["t"], 1)

            LOADS = 3

            def in_count(n, p):
                if isinstance(n, int):
                    return 16 * LOADS * (n // 2 + 1)
                return n * (8 * LOADS) + (8 * LOADS if p else 16 * LOADS)

            def weight_rests(n, p, weights):
                for c in weights:
                    dve.wait_ge(f["hi"], n * 3 + (c + 1))
                    V.tensor_tensor(FWL[p][:, c, :], F_w[:, c, :], f32(FWH[p][:, c, :]), ALU.subtract).then_inc(f["lo"], 1)

            def cosines(unit):
                U, _, _, tl, _ = unit
                dve.wait_ge(a["sw"], U + 1)
                V.tensor_tensor(A_T1[:, :, :], PS[:, 5, 0:HALF].rearrange("p (h d) -> p h d", h=H0 // 2),
                                rope0c[:, tl, :].unsqueeze(1).broadcast_to([P, H0 // 2, D0]), ALU.mult).then_inc(a["t1"], 1)

            def rotate(unit):
                U = unit[0]
                dve.wait_ge(a["t1"], U + 1)
                dve.wait_ge(a["t2"], U + 1)
                after(dve, a["hi"], U)
                V.tensor_tensor(A_q[:, :, :], A_T1[:, :, :], A_sw[:, :, :], ALU.add).then_inc(a["q"], 1)

            def stack_rests(unit):
                U, _, _, _, is_k = unit
                dve.wait_ge(a["hi"], U + 1)
                at = D0 if is_k else 2 * D0
                V.tensor_tensor(STK[:, :, at:at + D0], A_q[:, :, :], STK[:, :, 0:D0], ALU.subtract).then_inc(a["lo"], 1)

            def take_probabilities(t):
                dve.wait_ge(a["pt"], t * 2)
                after(dve, a["pv"], t - 1)
                V.tensor_copy(A_pT[:, 4:12, :], PS[:, 6:8, :].rearrange("p n (h t) -> p (n h) t", h=4)).then_inc(a["pd"], 1)

            def add_branch(b, tl):
                dve.wait_ge(a["wo_ps"], b * 2 + (tl + 1))
                xt = X[:, bass.ds(b * 2 + tl, 1), :].rearrange("p a c -> p (a c)")
                V.tensor_tensor(xt, xt, PS[:, 3 - tl, :], ALU.add).then_inc(a["x"], 1)

            def attend(b):
                later = not isinstance(b, int) or b >= 1
                for g in range(G0):
                    t, unit, earlier = b * G0 + g, prepared(b, g), prepared(b, g, 1)
                    for tb in range(2):
                        dve.wait_ge(a["sc"], t * 2 + (tb + 1))
                        V.tensor_reduce(A_mx[:, 4 * tb:4 * tb + 4],
                                        PS[:, 2 * tb:2 * tb + 2, :].rearrange("p n (h s) -> p (n h) s", h=2)[:, :, 0:(tb + 1) * P],
                                        AXIS.X, ALU.max).then_inc(a["mx"], 1)
                        dve.wait_ge(a["mx"], t * 2 + (tb + 1))
                        V.tensor_scalar(A_nb[:, 4 * tb:4 * tb + 4], A_mx[:, 4 * tb:4 * tb + 4], -float(D0) ** -0.5, None, ALU.mult)\
                         .then_inc(a["neg"], 1)
                    if earlier:
                        stack_rests(earlier)
                    if turn_before(b, g):
                        take_probabilities(t)
                    for tb in range(2):
                        dve.wait_ge(a["exp"], t * 2 + (tb + 1))
                        V.reciprocal(A_rec[:, 4 * tb:4 * tb + 4], A_sum[:, 4 * tb:4 * tb + 4]).then_inc(a["rec"], 1)
                        dve.wait_ge(a["rec"], t * 2 + (tb + 1))
                        for n in range(4):
                            blocks = slice(n, n + 1) if tb == 0 else slice(4 + 2 * n, 6 + 2 * n)
                            ins = V.tensor_scalar(A_ps[g % 2][:, blocks, :], A_ps[g % 2][:, blocks, :], A_rec[:, 4 * tb + n:4 * tb + n + 1], None, ALU.mult)
                        ins.then_inc(a["pn"], 1)
                    if g % 2 == 0 and (g or later):
                        dve.wait_ge(a["pv"], t)
                        if g == 2:
                            after(dve, a["wo_ps"], b * 2)
                        V.tensor_copy(OT0[:, (g // 2 - 1) % KT, :], PS[:, 4, 0:SEQ]).then_inc(a["ot"], 1)
                    if unit:
                        cosines(unit)
                        rotate(unit)
                    if g < 2 and later:
                        add_branch(b - 1, g)
                    if isinstance(b, int) and b == NB - 1:
                        if g == 3:
                            dve.wait_ge(a["vps"], 4 * NB)
                        if 3 <= g < 6:
                            unpack(0, 0, (g - 3,))
                        if g >= 5:
                            weight_rests(0, 0, (g - 5,))

            zeros_plus_one(0)
            cosines(prepared(-1, FIRST[0]))
            for g in FIRST:
                unit = prepared(-1, g)
                rotate(unit)
                if FIRST[1] <= g <= FIRST[2]:
                    zeros_plus_one(g - FIRST[0])
                if g < G0 - 1:
                    stack_rests(unit)
                    cosines(prepared(-1, g + 1))
            attend(0)
            with dve.Fori(1, NB - 1) as b:
                attend(b)
            attend(NB - 1)
            take_probabilities(NB * G0)
            dve.wait_ge(a["pv"], NB * G0)
            V.tensor_copy(OT0[:, KT - 1, :], PS[:, 4, 0:SEQ]).then_inc(a["ot"], 1)
            for tl in range(2):
                add_branch(NB - 1, tl)
            finish(dve, 2)

            count = [0]

            def chain(ins, signal):
                count[0] += 1
                ins.then_inc(signal, 1)
                dve.wait_ge(signal, count[0])

            def value_bindings():
                chain(V.scalar_tensor_tensor(vrow[:, :, :], bvr[:, :, :], -1.0, bvr[:, :, :], ALU.mult, ALU.max), c1["c"])
                chain(V.tensor_reduce(vr_al[:, :], vrow[:, :, :], AXIS.X, ALU.add), c1["c"])
                chain(V.tensor_scalar(vr_al[:, :], vr_al[:, :], 1.0 / P, None, ALU.mult), c1["c"])
                chain(V.tensor_scalar(vr_sg[:, :, :], bvr[:, :, :], 0.0, 2.0, ALU.is_ge, ALU.mult), c1["c"])
                chain(V.tensor_scalar(vr_sg[:, :, :], vr_sg[:, :, :], -1.0, None, ALU.add), c1["c"])
                chain(V.tensor_tensor(vr_sg[:, :, :], vr_sg[:, :, :], vr_al[:, :].unsqueeze(2).broadcast_to([P, 4, P]), ALU.mult), c1["c"])
                chain(V.tensor_tensor(vr_sg[:, :, :], vr_sg[:, :, :], bvr[:, :, :], ALU.subtract), c1["c"])
                chain(V.tensor_tensor(vrow[:, :, :], vr_sg[:, :, :], bvr[:, :, :], ALU.add), c1["c"])

            def key_bindings():
                chain(V.tensor_scalar(bv_sg[:, :], bv[:, :], 0.0, 2.0, ALU.is_ge, ALU.mult), c1["c"])
                dve.wait_ge(c1["al"], 1)
                chain(V.scalar_tensor_tensor(bv_sg[:, :], bv_sg[:, :], -1.0, PS[:, 0, 0:12], ALU.add, ALU.mult), c1["c"])
                chain(V.tensor_tensor(bv_sg[:, :], bv_sg[:, :], bv[:, :], ALU.subtract), c1["c"])
                chain(V.tensor_tensor(bv_q[:, :], bv_sg[:, :], bv[:, :], ALU.add), c1["c"])
                chain(V.tensor_tensor(qk1[:, :], bv_q[:, 0:4], bv_q[:, 4:8], ALU.mult), c1["c"])

            def gated(n, p):
                for h in range(2):
                    dve.wait_ge(f["sg"], n * 2 + (h + 1))
                    V.tensor_tensor(F_a[:, h, :], F_sg[:, h, :], PS[:, h, :], ALU.mult).then_inc(f["a"], 1)
                    dve.wait_ge(f["a"], n * 2 + (h + 1))
                    V.tensor_tensor(F_i[:, h, :], F_a[:, h, :], PS[:, 2 + h, :], ALU.mult).then_inc(f["i"], 1)

            def gated_rests(n, p):
                for h in range(2):
                    dve.wait_ge(f["ih"], n * 2 + (h + 1))
                    V.tensor_tensor(FIL[p][:, h * C:(h + 1) * C], F_i[:, h, :], f32(FIH[p][:, h * C:(h + 1) * C]),
                                    ALU.subtract).then_inc(f["il"], 1)

            def accumulate(n):
                for tt in range(TT):
                    dve.wait_ge(f["dps"], n * 8 + (tt + 1))
                    share = PS[:, 4 + tt % 4, :]
                    if isinstance(n, int) and n == 0:
                        V.tensor_copy(F_acc[:, tt, :], share).then_inc(f["acc"], 1)
                    else:
                        V.tensor_tensor(F_acc[:, tt, :], F_acc[:, tt, :], share, ALU.add).then_inc(f["acc"], 1)

            def ffn_step(n, p, m=None):
                unpack(n + 1, 1 - p)
                weight_rests(n + 1, 1 - p, (0, 1))
                gated(n, p)
                if m is not None:
                    accumulate(m)
                gated_rests(n, p)
                weight_rests(n + 1, 1 - p, (2,))

            ffn_step(0, 0)
            ffn_step(1, 1, 0)
            with dve.Fori(0, (NF - 3) // 2) as i:
                ffn_step(i * 2 + 2, 0, i * 2 + 1)
                ffn_step(i * 2 + 3, 1, i * 2 + 2)
            dve.wait_ge(small_in, SMALL_L1)
            V.scalar_tensor_tensor(bv_abs[:, :], bv[:, :], -1.0, bv[:, :], ALU.mult, ALU.max).then_inc(c1["abs"], 1)
            value_bindings()
            gated(NF - 1, 0)
            gated_rests(NF - 1, 0)
            key_bindings()
            for tt in range(TT + 2):
                if tt < TT:
                    n = (NF - 2) * TT + tt + 1
                    dve.wait_ge(f["dps"], n)
                    V.tensor_tensor(F_half[:, tt, :], F_acc[:, tt, :], PS[:, 4 + tt % 4, :], ALU.add).then_inc(f["acc"], 1)
                if tt >= 2:
                    dve.wait_ge(f["x"], tt - 1)
                    statistics(1, tt - 2)
            finish(dve, 3)

            normalise(1, c1["v"])

            dve.wait_ge(c1["lo_ps"], 2)
            count[0] = 0
            for n in range(2):
                last = V.tensor_copy(LA[:, 4 * n:4 * n + 4, :],
                                     PS[:, 3 + 4 * n, 0:4 * (R1 + E1)].rearrange("p (t r) -> p t r", t=4))
            chain(last, c1["gate"])
            gs = LA[:, :, R1:R1 + E1]
            chain(V.tensor_tensor(gs, gs, gb1[:, :].unsqueeze(1).broadcast_to([P, TT, E1]), ALU.add), c1["gate"])
            chain(V.tensor_reduce(g_m[:, :], gs, AXIS.X, ALU.max), c1["gate"])
            chain(V.tensor_tensor(g_ne[:, :, :], gs, g_m[:, :].unsqueeze(2).broadcast_to([P, TT, E1]), ALU.is_lt), c1["gate"])
            for k in range(3):
                if k:
                    chain(V.tensor_tensor(g_ne[:, :, k], g_ne[:, :, k], g_ne[:, :, k - 1], ALU.mult), c1["gate"])
                r = 8 << k
                chain(V.tensor_tensor(LA[:, :, r:2 * r], LA[:, :, r:2 * r],
                                      g_ne[:, :, k].unsqueeze(2).broadcast_to([P, TT, r]), ALU.mult), c1["gate"])
            gates = count[0]
            assert gates == 9
            for b in range(NB):
                dve.wait_ge(c1["sig"], b + 1)
                w0 = A1[:, 0:1024].rearrange("p (h t) -> p h t", h=4)[:, :, 0:P]
                w1 = A1[:, 1024:1536].rearrange("p (h t) -> p h t", h=4)
                seen = mask01[:, :].unsqueeze(1).broadcast_to([P, 4, P])
                V.tensor_tensor(w0, w0, seen, ALU.mult)
                V.tensor_tensor(w1, w1, seen, ALU.mult).then_inc(c1["mask"], 1)
                for tb in range(2):
                    tt = 2 * b + tb
                    dve.wait_ge(c1["pv"], tt + 1)
                    dve.wait_ge(bias_in, tt + 1)
                    V.tensor_tensor(X[:, tt, :], X[:, tt, :], PS[:, 6 + tb, :], ALU.add).then_inc(c1["xa"], 1)
                for tb in range(2):
                    dve.wait_ge(c1["xa"], 2 * b + tb + 1)
                    statistics(2, 2 * b + tb)
            finish(dve, 4)

            def route():
                dve.wait_ge(d2["lo_ps"], 1)
                count[0] = 0
                chain(V.tensor_copy(axr[:, :, :], PS[:, 3, 0:TT * (R2 + E2)].rearrange("p (t r) -> p t r", t=TT)), d2["c"])
                chain(V.tensor_reduce(e_m[:, :], axr[:, :, R2:R2 + E2], AXIS.X, ALU.max), d2["c"])
                chain(V.tensor_tensor(e_p[:, :, :], axr[:, :, R2:R2 + E2], e_m[:, :].unsqueeze(2).broadcast_to([P, TT, E2]),
                                      ALU.subtract), d2["c"])
                dve.wait_ge(d2["ax"], 1)
                chain(V.tensor_reduce(e_s[:, :], e_p[:, :, :], AXIS.X, ALU.add), d2["c"])
                chain(V.reciprocal(e_s[:, :], e_s[:, :]), d2["c"])
                chain(V.tensor_tensor(e_p[:, :, :], e_p[:, :, :], e_s[:, :].unsqueeze(2).broadcast_to([P, TT, E2]), ALU.mult), d2["c"])
                for tt in range(TT):
                    last = V.tensor_tensor(U2[:, tt, :, :], e_p[:, tt, :].unsqueeze(2).broadcast_to([P, E2, R2]),
                                           axr[:, tt, 0:R2].unsqueeze(1).broadcast_to([P, E2, R2]), ALU.mult)
                chain(last, d2["c"])
                assert count[0] == 7

            normalise(2, between={TT + 1: route})
            dve.wait_ge(d2["gh"], 1)
            V.scalar_tensor_tensor(GL[:, :], PS[:, 7, :], 2.0, f32(GH[:, :]), ALU.mult, ALU.subtract).then_inc(d2["gl"], 1)
            for n in range(2):
                dve.wait_ge(d2["uh"], n + 1)
                V.tensor_tensor(UL[:, n * C:(n + 1) * C], PS[:, n, :], f32(UH[:, n * C:(n + 1) * C]), ALU.subtract)\
                 .then_inc(d2["ul"], 1)
            for tt in range(TT):
                dve.wait_ge(d2["up"], tt + 1)
                dve.wait_ge(bias_in, TT + tt + 1)
                V.tensor_tensor(X[:, tt, :], X[:, tt, :], PS[:, 2 + tt % 4, :], ALU.add).then_inc(d2["x"], 1)
            finish(dve, 5)

            def l2_slot(g, j, step, one, two, final=False):
                i, q = g * NB + j, 1 - j % 2

                def maxima(tb):
                    dve.wait_ge(e2["sc"], i * 2 + (tb - 1))
                    V.tensor_reduce(E_mx[:, 4 * tb:4 * tb + 4],
                                    PS[:, 3 + 2 * tb:5 + 2 * tb, :].rearrange("p n (h s) -> p (n h) s", h=2)[:, :, 0:(tb + 1) * P],
                                    AXIS.X, ALU.max).then_inc(e2["mx"], 1)
                    dve.wait_ge(e2["mx"], i * 2 + (tb - 1))
                    V.tensor_scalar(E_nb[:, 4 * tb:4 * tb + 4], E_mx[:, 4 * tb:4 * tb + 4], -float(D2) ** -0.5, None, ALU.mult)\
                     .then_inc(e2["neg"], 1)

                def probabilities(tb):
                    dve.wait_ge(e2["exp"], i * 2 + (tb - 1))
                    V.reciprocal(E_rec[:, 4 * tb:4 * tb + 4], E_sum[:, 4 * tb:4 * tb + 4]).then_inc(e2["rec"], 1)
                    dve.wait_ge(e2["rec"], i * 2 + (tb - 1))
                    for h in range(4):
                        blocks = slice(h, h + 1) if tb == 0 else slice(4 + 2 * h, 6 + 2 * h)
                        last = V.tensor_scalar(E_p[:, blocks, :], E_p[:, blocks, :], E_rec[:, 4 * tb + h:4 * tb + h + 1], None, ALU.mult)
                    last.then_inc(e2["pn"], 1)

                def cosines(n, heads):
                    if n == 0:
                        dve.wait_ge(e2["sw"], i * 2 + 1)
                        after(dve, e2["qhi"], i * 2)
                    else:
                        dve.wait_ge(e2["vt"], i + 1)
                    V.tensor_tensor(E_T[:, heads, :], PS[:, 0:3, :].rearrange("p n (h t) -> p (n h) t", h=2)[:, heads, :],
                                    rope2c[:, :].unsqueeze(1).broadcast_to([P, heads.stop - heads.start, SEQ]), ALU.mult)\
                     .then_inc(e2["t1"], 1)

                def rotated(n, heads):
                    dve.wait_ge(e2["t1"], i * 2 + (n + 1))
                    dve.wait_ge(e2["t2"], i * 2 + (n + 1))
                    V.tensor_tensor(E_T[:, heads, :], E_T[:, heads, :], E_sw[:, heads, :], ALU.add).then_inc(e2["q"], 1)

                def rotated_rests(n, heads):
                    dve.wait_ge(e2["qhi"], i * 2 + (n + 1))
                    V.tensor_tensor(QKL[:, heads, :], E_T[:, heads, :], f32(QKH[:, heads, :]), ALU.subtract).then_inc(e2["qlo"], 1)

                def add_branch(tb):
                    dve.wait_ge(e2["wo"], i * 2 + (tb - 3))
                    tt = 2 * ((j - 2) % NB) + tb
                    V.tensor_tensor(X[:, tt, :], X[:, tt, :], PS[:, 7 - tb, :], ALU.add).then_inc(e2["x"], 1)

                Q, K = (0, slice(0, 4)), (1, slice(4, 5))
                if one:
                    maxima(0)
                    maxima(1)
                if step:
                    cosines(*Q)
                if one:
                    probabilities(0)
                    probabilities(1)
                if step:
                    cosines(*K)
                    rotated(*Q)
                if one:
                    for tb, n in ((0, slice(0, 1)), (1, slice(1, 3))):
                        dve.wait_ge(e2["phi"], i * 2 + (tb - 1))
                        V.tensor_tensor(PL[:, n, :], PS[:, 3 + n.start:3 + n.stop, :], f32(PH[:, n, :]), ALU.subtract)\
                         .then_inc(e2["plo"], 1)
                if two:
                    add_branch(0)
                if step:
                    rotated(*K)
                    rotated_rests(*Q)
                    rotated_rests(*K)
                if two:
                    add_branch(1)
                if step:
                    dve.wait_ge(e2["vhi"], i + 1)
                    V.tensor_tensor(VL[:, :, :], PS[:, 2, SEQ:2 * SEQ].rearrange("p (s d) -> p s d", s=2), f32(VH[:, :, :]),
                                    ALU.subtract).then_inc(e2["vlo"], 1)
                if one:
                    for tb in range(2):
                        dve.wait_ge(e2["ohi"], i * 2 + (tb - 1))
                        V.tensor_tensor(OL[q][:, tb, :], PS[:, 3 + tb, :], f32(OH[q][:, tb, :]), ALU.subtract).then_inc(e2["olo"], 1)
                if final:
                    for tb in range(2):
                        dve.wait_ge(e2["x"], i * 2 + (tb - 3))
                        statistics(3, 2 * ((j - 2) % NB) + tb)


            for j in range(NB):
                l2_slot(0, j, True, j >= 1, j >= 2)
            with dve.Fori(1, KV2 - 1) as g:
                for j in range(NB):
                    l2_slot(g, j, True, True, True)
            for j in range(NB):
                l2_slot(KV2 - 1, j, True, True, True, j >= 2)
            l2_slot(KV2, 0, False, True, True, True)
            l2_slot(KV2, 1, False, False, True, True)
            finish(dve, 6)

            def unpack_int4():
                dve.wait_ge(small_in, SMALL_F3)
                for k in range(KT + 1):
                    if k < KT:
                        V.tensor_scalar(q3[:, k, :], pk3[:, k // 2, :], 4 * (k % 2), 15, ALU.logical_shift_right, ALU.bitwise_and)\
                         .then_inc(f["q"], 1)
                    if k:
                        dve.wait_ge(f["q"], 3 * NF + k)
                        V.tensor_tensor(t3[:, k - 1, :], q3[:, k - 1, :], zp3[:, :], ALU.subtract).then_inc(f["t"], 1)

            def int4_rests():
                for k in range(KT):
                    dve.wait_ge(f["hi"], 3 * NF + k + 1)
                    V.tensor_tensor(W3L[:, k, :], t3[:, k, :], f32(W3H[:, k, :]), ALU.subtract).then_inc(f["lo"], 1)

            normalise(3, between={1: unpack_int4, 3: int4_rests})
            dve.wait_ge(bias_in, 3 * TT)
            finish(dve, 7)
            dve.wait_ge(g3["in"], 16 * 2)

            def recall(b, heads):
                for h in heads:
                    n = b * H3 + h
                    if turns(n, 0):
                        dve.wait_ge(g3["qps"], n + 1)
                        after(dve, g3["e"], n)
                        V.tensor_scalar(G_m[:, :], PS[:, h % 2, 0:SEQ], bq3[:, h:h + 1], 0.0, ALU.add, ALU.min).then_inc(g3["m"], 1)
                    if turns(n, 2):
                        dve.wait_ge(g3["hi"], n - 1)
                        V.tensor_tensor(NL3[h % 2][:, :], PS[:, 4 + h % 2, 0:SEQ], f32(NH3[h % 2][:, :]), ALU.subtract).then_inc(g3["lo"], 1)
                    if turns(n, 0):
                        dve.wait_ge(g3["e"], n + 1)
                        dve.wait_ge(g3["r"], n + 1)
                        after(dve, g3["nps"], n - 1)
                        V.tensor_tensor(G_s[h % 2][:, :], G_e[:, :], G_r[:, :], ALU.add).then_inc(g3["sum"], 1)
                    if turns(n, 1):
                        dve.wait_ge(g3["nps"], n)
                        o = PS[:, 3 - h % 2, 0:2 * (P + 1)].rearrange("p (t e) -> p t e", t=2)
                        V.tensor_scalar(G_rec[:, :], o[:, :, P], 1e-6, None, ALU.add).then_inc(g3["rc"], 1)
                        dve.wait_ge(g3["rc"], n * 2 - 1)
                        V.reciprocal(G_rec[:, :], G_rec[:, :]).then_inc(g3["rc"], 1)
                        dve.wait_ge(g3["rc"], n * 2)
                        after(dve, g3["tp"], n - 2)
                        V.tensor_tensor(G_o[1 - h % 2][:, :, :], o[:, :, 0:P], G_rec[:, :].unsqueeze(2).broadcast_to([P, 2, P]), ALU.mult)\
                         .then_inc(g3["mul"], 1)
                    if h == 2 and turns(n, H3):
                        dve.wait_ge(g3["wo"], b * H3)
                        for tl in range(2):
                            xt = X[:, bass.ds(b * 2 + (tl - 2), 1), :].rearrange("p a c -> p (a c)")
                            V.tensor_tensor(xt, xt, PS[:, 6 + tl, :], ALU.add).then_inc(g3["xo"], 1)

            recall(0, range(H3))
            with dve.Fori(1, NB) as b:
                recall(b, range(H3))
            recall(NB, range(3))
            finish(dve, 8)

        @block.tensor
        def _(pe):
            mm = nc.tensor.matmul

            def normalise(l, pairs=False, dense=None, ahead=2, early=None):
                xn = LN[l]["xn"]
                for tt in range(TT + ahead):
                    if tt < TT:
                        ln_wait(pe, l, "xn", tt + 1)
                        if tt >= TB:
                            ln_wait(pe, l, "lo", tt - TB + 1)
                        for k in range(KT):
                            src = xn[:, tt % XNB, k * P:(k + 1) * P]
                            if pairs:
                                at = (k // 2) * 2 * P + k % 2
                                src = xn[:, tt % XNB, at:at + 2 * P - 1:2]
                            last = nc.tensor.transpose(PS[:, tt % TB, k * P:(k + 1) * P], src, ident[:, :])
                        last.then_inc(ln["tp"], 1)
                    if early is not None and 1 <= tt <= TT:
                        ln_wait(pe, l, "hi", tt)
                        early(tt - 1)
                    if dense is not None and tt >= ahead:
                        ln_wait(pe, l, "lo", tt - ahead + 1)
                        dense(tt - ahead)

            def dense_tile(l, tt, WH, WL):
                n = (l - 1) * TT + tt
                if tt >= 3:
                    pe.wait_ge(ffn_x, n - 2)
                span = slice(tt * P, (tt + 1) * P)
                for k in range(KT):
                    last = product3(PS[:, 4 + tt % 3, :], XNH[:, k, span], XNL[:, k, span], WH[:, k, :], WL[:, k, :], k == 0, k == KT - 1)
                last.then_inc(ffn_ps, 1)

            pe.wait_ge(const_in, 16 * 9)
            normalise(0)
            finish(pe, 1)

            pe.wait_ge(w_lo, 8)

            def dense(o, w, half, tl):
                for k in range(KT):
                    span, cols = slice(tl * P, (tl + 1) * P), slice(half * HALF, (half + 1) * HALF)
                    last = product3(o, SGH[:, k, span], SGL[:, k, span], WQH[:, 4 * w + k, cols], WQL[:, 4 * w + k, cols], k == 0, k == KT - 1)
                return last

            def project(unit):
                U, b, half, tl, is_k = unit
                if half == 0 and is_k == 0:
                    pe.wait_ge(a[f"stage{tl}"], b * 32 + 32)
                after(pe, a["t1"], U)
                dense(PS[:, 5, 0:HALF], is_k, half, tl).then_inc(a["proj"], 1)

            def values(unit):
                U, b, half, _, tl = unit
                after(pe, a["vcp"], b * 4 + (2 * half + tl))
                dense(PS[:, 3, 0:HALF], 2, half, tl).then_inc(a["vps"], 1)

            def transposes(unit):
                U = unit[0]
                pe.wait_ge(a["lo"], U + 1)
                after(pe, a["ev"], U)
                for n in range(8):
                    last = nc.tensor.transpose(PS[:, 6 + n // 4, (n % 4) * P:(n % 4 + 1) * P],
                                               STK[:, 2 * n:2 * n + 2, :].rearrange("p h r -> p (h r)"), ident[:, :])
                last.then_inc(a["tp"], 1)

            def rows(g, h):
                return slice((h % 2) * S0, (h % 2 + 1) * S0), 2 * g + h // 2

            def weighted_values(t, g, pairs):
                pe.wait_ge(a["pe"], t)
                pe.wait_ge(a["pd"], t)
                if g % 2 == 0:
                    after(pe, a["ot"], pairs)
                for n in range(2):
                    c = (2 * g + n) % 4
                    rows32 = slice(32 * c, 32 * c + 32)
                    for s in range(2):
                        for e in range(2):
                            h = order(2 * n + e)
                            stationary = V0[:, s, 2 * g + n, e, :]
                            if s == 0:
                                last = mm(PS[rows32, 4, 0:SEQ].rearrange("p (s t) -> p s t", s=2), stationary, A_pT[:, h:8:4, :],
                                          start=(e == 0), stop=False, skip_group_check=True, tile_position=(0, 32 * c))
                            else:
                                last = mm(PS[rows32, 4, P:SEQ], stationary, A_pT[:, 8 + h, :], start=False, stop=(e == 1),
                                          skip_group_check=True, tile_position=(0, 32 * c))
                last.then_inc(a["pv"], 1)

            def output(b, tl):
                if tl == 0:
                    pe.wait_ge(a["ot"], b * 4 + 4)
                for k in range(KT):
                    last = mm(PS[:, 3 - tl, :], OT0[:, k, tl * P:(tl + 1) * P], wo0[:, k, :], start=(k == 0), stop=(k == KT - 1))
                last.then_inc(a["wo_ps"], 1)

            def probabilities(t, g, unit, stacks):
                for tb in range(2):
                    pe.wait_ge(a["pn"], t * 2 + (tb - 1))
                    if tb == 0 and unit:
                        pe.wait_ge(a["t1"], unit[0] + 1)
                    if tb == 1 and stacks:
                        pe.wait_ge(a["ev"], stacks[0] + 1)
                    for n in range(4):
                        for s in range(tb + 1):
                            last = nc.tensor.transpose(PS[:, 5 + tb + s, n * P:(n + 1) * P],
                                                       A_ps[g % 2][:, n if tb == 0 else 4 + 2 * n + s, :], ident[:, :])
                    last.then_inc(a["pt"], 1)

            def attend(b):
                later = not isinstance(b, int) or b >= 1
                for g in range(G0):
                    t, unit, earlier = b * G0 + g, prepared(b, g), prepared(b, g, 1)
                    if g % 4 == 0:
                        pe.wait_ge(a["ev"], b * G0 + (g + 4))
                    for tb in range(2):
                        if tb == 1:
                            pe.wait_ge(a["vcp"], b * 4 + (2 + sum(g > v for v in (1, 2, 5, 6) if prepared(b, v))))
                            if later and g in (1, 2):
                                pe.wait_ge(a["x"], b * 2 + (g - 2))
                        for h in range(4):
                            r, n = rows(g, h)
                            at, bank = (h // 2) * SEQ, 2 * tb + h % 2
                            mm(PS[:, bank, at:at + SEQ], qT[r, n, tb * P:(tb + 1) * P], kT[r, n, :], start=True, stop=False,
                               skip_group_check=True)
                            last = mm(PS[:, bank, at + tb * P:at + (tb + 1) * P], identb[:, :], mask_ts[:, :], start=False, stop=True,
                                      skip_group_check=True)
                        last.then_inc(a["sc"], 1)
                    if turn_before(b, g):
                        probabilities(t, g - 1, earlier, prepared(b, g, 2))
                    if unit:
                        after(pe, a["pe"], t)
                        project(unit)
                    if earlier:
                        after(pe, a["pd"], t)
                        transposes(earlier)
                    if turn_before(b, g):
                        weighted_values(t, (g - 1) % G0, b * KT + (g - 1) // 2)
                    pe.wait_ge(a["exp"], t * 2 + 2)
                    if g < 2 and later:
                        output(b - 1, g)
                    if unit and g % 4 in (1, 2):
                        values(unit)

            project(prepared(-1, FIRST[0]))
            for g in FIRST:
                unit = prepared(-1, g)
                if g < G0 - 1:
                    project(prepared(-1, g + 1))
                if g % 4 in (1, 2):
                    pe.wait_ge(w_lo, 12)
                    values(unit)
                if g < G0 - 1:
                    transposes(unit)
            attend(0)
            pe.wait_ge(wo_in, 16 * KT)
            with pe.Fori(1, NB - 1) as b:
                attend(b)
            attend(NB - 1)
            probabilities(NB * G0, G0 - 1, None, None)
            weighted_values(NB * G0, G0 - 1, None)
            for tl in range(2):
                output(NB - 1, tl)
            finish(pe, 2)

            def gate_up(n, p):
                pe.wait_ge(f["lo"], n * 3 + 2)
                for h in range(2):
                    if not isinstance(n, int) or n >= 1:
                        pe.wait_ge(f["i"], n * 2 + (h - 1))
                    for c in range(2):
                        for k in range(KT):
                            span, half = slice(k * P, (k + 1) * P), slice(h * C, (h + 1) * C)
                            last = product3(PS[:, 2 * c + h, :], FWH[p][:, c, span], FWL[p][:, c, span], XNH[:, k, half], XNL[:, k, half],
                                            k == 0, k == KT - 1)
                    last.then_inc(f["gu"], 1)

            def down(n, p, first=False):
                pe.wait_ge(f["lo"], n * 3 + 3)
                pe.wait_ge(f["il"], n * 2 + 2)
                for tt in range(TT):
                    if not first or tt >= 4:
                        pe.wait_ge(f["acc"], n * 8 + (tt - 3))
                    span = slice(tt * P, (tt + 1) * P)
                    product3(PS[:, 4 + tt % 4, :], FIH[p][:, span], FIL[p][:, span], FWH[p][:, 2, :], FWL[p][:, 2, :], True, True)\
                        .then_inc(f["dps"], 1)

            def last_downs():
                for half in range(2):
                    for n, p in ((NF - 2, 1), (NF - 1, 0)):
                        pe.wait_ge(f["lo"], n * 3 + 3)
                        pe.wait_ge(f["il"], n * 2 + 2)
                        if half == 0 and n == NF - 1:
                            pe.wait_ge(f["i"], 2 * NF)
                            pe.wait_ge(a["init"], 3)
                            pe.wait_ge(c1["abs"], 1)
                            mm(PS[:, 0, 0:12], inv[:, :], bv_abs[:, :], start=True, stop=True).then_inc(c1["al"], 1)
                        for tt in range(4 * half, 4 * half + 4):
                            if n == NF - 2:
                                pe.wait_ge(f["acc"], n * 8 + (tt - 3))
                            span = slice(tt * P, (tt + 1) * P)
                            last = product3(PS[:, 4 + tt % 4, :], FIH[p][:, span], FIL[p][:, span], FWH[p][:, 2, :], FWL[p][:, 2, :],
                                            n == NF - 2, n == NF - 1)
                            if n == NF - 1:
                                last.then_inc(f["dps"], 1)

            gate_up(0, 0)
            gate_up(1, 1)
            down(0, 0, True)
            gate_up(2, 0)
            down(1, 1)
            with pe.Fori(1, (NF - 3) // 2) as i:
                gate_up(i * 2 + 1, 1)
                down(i * 2, 0)
                gate_up(i * 2 + 2, 0)
                down(i * 2 + 1, 1)
            gate_up(NF - 2, 1)
            down(NF - 3, 0)
            gate_up(NF - 1, 0)
            last_downs()
            finish(pe, 3)

            def l1_tile(tt):
                if tt == 0:
                    pe.wait_ge(w_lo, U_W1 + KT)
                dense_tile(1, tt, W1H, W1L)
                at = (tt % 4) * (R1 + E1)
                for k in range(KT):
                    last = mm(PS[:, 3 + 4 * (tt // 4), at:at + R1 + E1], XT1[:, k, tt * P:(tt + 1) * P], AG1[:, k, :], start=(k == 0),
                              stop=(k == KT - 1), skip_group_check=True)
                if tt % 4 == 3:
                    last.then_inc(c1["lo_ps"], 1)

            pe.wait_ge(small_in, SMALL_L1)
            normalise(1, dense=l1_tile)

            def l1_scores(b):
                s = 3 * (b % 2)
                if b >= 2:
                    pe.wait_ge(c1["sig"], b - 1)
                elif b == 1:
                    pe.wait_ge(c1["gate"], 1)
                    pe.wait_ge(ffn_x, TT)
                t0 = b * SEQ
                for h in range(4):
                    mm(PS[:, s + h // 2, (h % 2) * SEQ:(h % 2 + 1) * SEQ], K1[:, h, t0:t0 + P], XT1[:, h, t0:t0 + SEQ], start=True, stop=True,
                       skip_group_check=True)
                for h in range(4):
                    last = mm(PS[:, s + 2, h * P:(h + 1) * P], K1[:, h, t0 + P:t0 + SEQ], XT1[:, h, t0 + P:t0 + SEQ], start=True, stop=True,
                              skip_group_check=True)
                last.then_inc(c1["st"], 1)

            def l1_values(b):
                pe.wait_ge(c1["mask"], b + 1)
                if b >= 1:
                    pe.wait_ge(c1["xa"], 2 * b)
                else:
                    pe.wait_ge(c1["lat_cp"], 2)
                for tb in range(2):
                    span = slice((2 * b + tb) * P, (2 * b + tb + 1) * P)
                    mm(PS[:, 6 + tb, :], LAT[:, span], BT1[:, :], start=True, stop=False, skip_group_check=True)
                    for h in range(4):
                        o = PS[:, 6 + tb, h * P:(h + 1) * P]
                        last = mm(o, A1[:, h * SEQ + tb * P:h * SEQ + (tb + 1) * P], V1[:, 2 * b, h * P:(h + 1) * P], start=False, stop=(tb == 0),
                                  skip_group_check=True)
                        if tb:
                            last = mm(o, A1[:, 1024 + h * P:1024 + (h + 1) * P], V1[:, 2 * b + 1, h * P:(h + 1) * P], start=False, stop=True,
                                      skip_group_check=True)
                    last.then_inc(c1["pv"], 1)

            pe.wait_ge(c1["k1"], TT)
            pe.wait_ge(c1["v"], TT)
            ln_wait(pe, 1, "lo", TT)
            l1_scores(0)
            pe.wait_ge(c1["gate"], 9)
            pe.wait_ge(ffn_x, TT)
            for tt in range(TT):
                last = nc.tensor.transpose(PS[0:R1, 6 + tt // 4, (tt % 4) * P:(tt % 4 + 1) * P], LA[:, tt, 0:R1], ident[:, :])
                if tt % 4 == 3:
                    last.then_inc(c1["lat_ps"], 1)
            for b in range(NB):
                if b + 1 < NB:
                    l1_scores(b + 1)
                l1_values(b)
            finish(pe, 4)

            def l2_route(tt):
                if tt == 0:
                    pe.wait_ge(small_in, SMALL_L2)
                at = tt * (R2 + E2)
                for k in range(KT):
                    last = mm(PS[:, 3, at:at + R2 + E2], XT2[:, k, tt * P:(tt + 1) * P], AR2[:, k, :], start=(k == 0), stop=(k == KT - 1),
                              skip_group_check=True)
                if tt == TT - 1:
                    last.then_inc(d2["lo_ps"], 1)

            def l2_dense(tt):
                if tt == 0:
                    pe.wait_ge(w_lo, U_WB2 + KT)
                dense_tile(2, tt, W2H, W2L)
                if tt == 0:
                    mm(PS[:, 7, :], coresT[:, :], BwT[:, :], start=True, stop=True).then_inc(d2["g_ps"], 1)

            normalise(2, dense=l2_dense, ahead=5, early=l2_route)
            pe.wait_ge(d2["c"], 7)
            for tt in range(TT):
                last = nc.tensor.transpose(PS[:, tt // 4, (tt % 4) * P:(tt % 4 + 1) * P],
                                           U2[:, tt, :, :].rearrange("p e r -> p (e r)"), ident[:, :])
                if tt % 4 == 3:
                    last.then_inc(d2["tp"], 1)
            pe.wait_ge(d2["gl"], 1)
            pe.wait_ge(ffn_x, 2 * TT)
            for tt in range(TT):
                if tt >= 4:
                    pe.wait_ge(d2["x"], tt - 3)
                pe.wait_ge(d2["ul"], tt // 4 + 1)
                span = slice(tt * P, (tt + 1) * P)
                product3(PS[:, 2 + tt % 4, :], UH[:, span], UL[:, span], GH[:, :], GL[:, :], True, True).then_inc(d2["up"], 1)
            finish(pe, 5)

            def l2_slot(g, j, step, one, two):
                i, p = g * NB + j, j % 2

                def project(units, signal):
                    for u in units:
                        pe.wait_ge(w_lo, g * U_L2_G + (U_L2 + u + 1))
                        for k in range(KT):
                            span, tok = slice(k * P, (k + 1) * P), slice(j * SEQ, (j + 1) * SEQ)
                            last = product3(PS[:, u // 2, (u % 2) * SEQ:(u % 2 + 1) * SEQ], E_WH[:, u, span], E_WL[:, u, span],
                                            XNH[:, k, tok], XNL[:, k, tok], k == 0, k == KT - 1)
                    last.then_inc(signal, 1)

                def output(tb):
                    if tb == 0:
                        pe.wait_ge(e2["olo"], i * 2 - 2)
                        if not isinstance(i, int) or i >= 3:
                            pe.wait_ge(e2["x"], i * 2 - 4)
                        if j == 2:
                            pe.wait_ge(w_lo, g * U_L2_G + (U_L2 + U_L2_G))
                    for h in range(4):
                        span = slice(h * P, (h + 1) * P)
                        last = product3(PS[:, 7 - tb, :], OH[p][:, tb, span], OL[p][:, tb, span], E_WH[:, 6 + h, :], E_WL[:, 6 + h, :],
                                        h == 0, h == 3)
                    last.then_inc(e2["wo"], 1)

                if step:
                    if not isinstance(i, int) or i >= 1:
                        pe.wait_ge(e2["t1"], i * 2 - 1)
                    project(range(4), e2["pq"])
                if one:
                    pe.wait_ge(e2["qlo"], i * 2)
                    if two:
                        pe.wait_ge(e2["olo"], i * 2 - 2)
                        after(pe, e2["x"], i * 2 - 4)
                    for tb in range(2):
                        t = slice(tb * P, (tb + 1) * P)
                        for h in range(4):
                            at, bank = (h % 2) * SEQ, 3 + 2 * tb + h // 2
                            o = PS[:, bank, at:at + SEQ]
                            mm(o, QKL[:, h, t], QKH[:, 4, :], start=True, stop=False, skip_group_check=True)
                            mm(o, QKH[:, h, t], QKL[:, 4, :], start=False, stop=False, skip_group_check=True)
                            mm(o, QKH[:, h, t], QKH[:, 4, :], start=False, stop=False, skip_group_check=True)
                            last = mm(PS[:, bank, at + tb * P:at + (tb + 1) * P], identb[:, :], mask_ts[:, :], start=False, stop=True,
                                      skip_group_check=True)
                        last.then_inc(e2["sc"], 1)
                if step:
                    after(pe, e2["vlo"], i)
                    project(range(4, 6), e2["pk"])
                if two:
                    output(0)
                if one:
                    for tb in range(2):
                        pe.wait_ge(e2["pn"], i * 2 + (tb - 1))
                        for h in range(4):
                            for s in range(tb + 1):
                                last = nc.tensor.transpose(PS[:, 3 + tb + s, h * P:(h + 1) * P],
                                                           E_p[:, h if tb == 0 else 4 + 2 * h + s, :], ident[:, :])
                        last.then_inc(e2["pt"], 1)
                if two:
                    output(1)
                if step:
                    pe.wait_ge(e2["vt"], i + 1)
                    pe.wait_ge(e2["t1"], i * 2 + 2)
                    for s in range(2):
                        last = nc.tensor.transpose(PS[:, 2, SEQ + s * P:SEQ + (s + 1) * P], vT2[:, s * P:(s + 1) * P], ident[:, :])
                    last.then_inc(e2["vtp"], 1)
                if one:
                    pe.wait_ge(e2["vlo"], i)
                    for tb in range(2):
                        pe.wait_ge(e2["plo"], i * 2 + (tb - 1))
                        for s in range(tb + 1):
                            last = product3(PS[:, 3 + tb, :], VH[:, s, :], VL[:, s, :], PH[:, tb + s, :], PL[:, tb + s, :], s == 0, s == tb)
                        last.then_inc(e2["pv"], 1)

            for j in range(NB):
                l2_slot(0, j, True, j >= 1, j >= 2)
            with pe.Fori(1, KV2) as g:
                for j in range(NB):
                    l2_slot(g, j, True, True, True)
            l2_slot(KV2, 0, False, True, True)
            l2_slot(KV2, 1, False, False, True)
            finish(pe, 6)


            def unpacked_dense(tt):
                pe.wait_ge(f["lo"], 3 * NF + KT)
                dense_tile(3, tt, W3H, W3L)

            normalise(3, True, unpacked_dense)
            finish(pe, 7)
            pe.wait_ge(g3["in"], 16 * 2)
            pe.wait_ge(w_lo, U_L3 + H3)
            pe.wait_ge(g3["wsl"], H3)

            def through_wo(n, h):
                m = (h - 3) % H3
                pe.wait_ge(g3["lo"], n - 2)
                for tl in range(2):
                    t = slice(tl * P, (tl + 1) * P)
                    last = product3(PS[:, 6 + tl, :], NH3[1 - h % 2][:, t], NL3[1 - h % 2][:, t], WSH[:, m, :], WSL[:, m, :],
                                    m == 0, m == H3 - 1)
                last.then_inc(g3["wo"], 1)

            def recall(b, heads):
                for h in heads:
                    n = b * H3 + h
                    if turns(n, 0):
                        after(pe, g3["sum"], n - 1)
                        tok = bass.ds(b * SEQ, SEQ)
                        for k in range(KT):
                            span = slice(k * P, (k + 1) * P)
                            last = product3(PS[:, h % 2, 0:SEQ], L3H[:, h, span], L3L[:, h, span], XNH[:, k, tok], XNL[:, k, tok],
                                            k == 0, k == KT - 1)
                        last.then_inc(g3["qps"], 1)
                    if turns(n, 3) and h != 3:
                        through_wo(n, h)
                    if turns(n, 2):
                        pe.wait_ge(g3["mul"], n - 1)
                        after(pe, g3["lo"], n - 3)
                        for tl in range(2):
                            last = nc.tensor.transpose(PS[:, 4 + h % 2, tl * P:(tl + 1) * P], G_o[h % 2][:, tl, :], ident[:, :])
                        last.then_inc(g3["tp"], 1)
                    if turns(n, 1):
                        pe.wait_ge(g3["sum"], n)
                        after(pe, g3["mul"], n - 2)
                        for tl in range(2):
                            last = mm(PS[:, 3 - h % 2, tl * (P + 1):(tl + 1) * (P + 1)], G_s[1 - h % 2][:, tl * P:(tl + 1) * P],
                                      MZ[:, (h - 1) % H3, :], start=True, stop=True, skip_group_check=True)
                        last.then_inc(g3["nps"], 1)
                    if turns(n, 3) and h == 3:
                        after(pe, g3["xo"], b * 2)
                        through_wo(n, h)

            recall(0, range(H3))
            with pe.Fori(1, NB) as b:
                recall(b, range(H3))
            recall(NB, range(3))
            finish(pe, 8)


def kernel(**inputs):
    import numpy as np
    import concourse.bacc as bacc
    from concourse import mybir
    from concourse.bass_utils import run_bass_kernel_spmd

    a = {k: np.asarray(v) for k, v in inputs.items()}
    P, KT, C, NF = 128, 4, 512, 11
    f32 = np.float32

    def tiles(w):
        return w.T.reshape(-1, P, w.shape[0])

    def columns(w, order=None):
        t = w.T if order is None else w.T[order]
        return t.reshape(-1, P, w.shape[0] // P, P).transpose(2, 1, 0, 3).reshape(w.shape[0] // P, P, -1)

    def rows(v, n=P):
        return np.broadcast_to(v, (n,) + v.shape)

    def pad(x, axis, size):
        widths = [(0, 0)] * x.ndim
        widths[axis] = (0, size - x.shape[axis])
        return np.pad(x, widths)

    def inner(x, per):
        x = pad(x, 1, NF * P // per)
        return x.reshape(x.shape[0], NF, P // per).transpose(1, 0, 2)

    words = [inner(a[f"L0_ffn_{n}_qweight"], 1).reshape(NF, KT, 16, P).transpose(0, 2, 1, 3).reshape(NF, 16, C) for n in ("gate", "up")]
    words.append(pad(a["L0_ffn_down_qweight"], 0, NF * 16).reshape(NF, 16, C))
    zeros = [inner(a[f"L0_ffn_{n}_zeros"], 8).reshape(NF, C // 8) for n in ("gate", "up")] + [a["L0_ffn_down_zeros"]]
    scales = [inner(a[f"L0_ffn_{n}_scales"], 1).reshape(NF, C) for n in ("gate", "up")] + [a["L0_ffn_down_scales"]]

    qkv = columns(a["L2_attn_Wqkv"])
    wo2 = a["L2_attn_Wo"].T.reshape(32, P, C)
    w2 = np.stack([np.stack([*qkv[4 * g:4 * g + 4], qkv[32 + g], qkv[40 + g], *wo2[4 * g:4 * g + 4]]) for g in range(8)])

    order = np.arange(C).reshape(2, P, 2).transpose(0, 2, 1).reshape(C)
    read = np.arange(32 * P).reshape(8, 4, P)[:, 0].reshape(-1)
    w3 = columns(a["L3_attn_Wq"][read], order)

    def angles(t, h):
        pos = np.arange(t, dtype=f32)
        theta = f32(1.0) / f32(10000.0) ** (np.arange(0, h, 2, dtype=f32) / f32(h))
        return np.outer(pos, theta).astype(f32)

    t0, t2 = angles(256, 16), angles(256, 128)
    cos0 = np.concatenate([np.cos(t0), np.cos(t0)], 1)
    sin0 = np.concatenate([-np.sin(t0), np.sin(t0)], 1)
    cos2 = np.concatenate([np.cos(t2), np.cos(t2)], 1)
    sin2 = np.concatenate([-np.sin(t2), np.sin(t2)], 1)
    bf16 = mybir.dt.np(mybir.dt.bfloat16)
    p = np.arange(P)
    hidden = np.where(p[None, :] > p[:, None], -1e30, 0.0)
    arrays = dict(
        x=a["L0_attn_x"].reshape(8, P, C),
        w0=np.concatenate([tiles(a[f"L0_attn_{n}"]) for n in ("wq", "wk", "wv", "wo")]),
        words=np.stack(words, 2).repeat(8, 1), zeros=np.concatenate(zeros, 1), scales=np.concatenate(scales, 1),
        bv=np.concatenate([a[f"L1_attn_bv_{n}"].T for n in "qkv"], 1), bvr=rows(a["L1_attn_bv_v"]),
        w1=tiles(a["L1_ffn_W"]), b1=rows(a["L1_ffn_b"]), gb1=rows(a["L1_ffn_gate_b"]),
        ag1=np.concatenate([a["L1_ffn_A"].T, a["L1_ffn_gate_w"].T], 1).reshape(KT, P, 68).transpose(1, 0, 2),
        bt1=a["L1_ffn_B"].T,
        wb2=tiles(a["L2_ffn_W_base"]), b2=rows(a["L2_ffn_b_base"]),
        ar2=np.concatenate([a["L2_ffn_A_w"].T, a["L2_ffn_router_w"].T], 1).reshape(KT, P, 24).transpose(1, 0, 2),
        coresT=a["L2_ffn_cores"].transpose(2, 0, 1).reshape(16, P), bwT=a["L2_ffn_B_w"].T, w2=w2,
        w3=w3, wo3=a["L3_attn_Wo"].T.reshape(8, 4, P, C), bq3=a["L3_attn_bq"][read].reshape(8, P).T,
        mz3=np.concatenate([a["L3_attn_M"], a["L3_attn_z"][:, :, None]], 2).transpose(1, 0, 2),
        pk3=a["L3_ffn_weight_packed"].reshape(C, 2, P).transpose(2, 1, 0), zp3=rows(a["L3_ffn_zero_point"][:, 0]),
        sc3=rows(a["L3_ffn_scale"][:, 0]), b3=rows(a["L3_ffn_bias"]),
        ident=np.eye(P, dtype=f32), identb=np.eye(P, dtype=bf16), mask_ts=hidden.astype(bf16),
        mask01=(hidden.T == 0).astype(f32),
        shift_k=(4 * (p % 8)).astype(np.int32)[:, None], shift_n=np.broadcast_to(4 * np.arange(8, dtype=np.int32), (NF, 8)),
        rope0c=cos0.reshape(2, P, 16).transpose(1, 0, 2), rope0s=sin0.reshape(2, P, 16).transpose(1, 0, 2),
        rope2c=cos2.T, rope2s=sin2.T)

    nc = bacc.Bacc("TRN2", target_bir_lowering=False, num_devices=1)
    fed, d = {}, {}
    for name, x in arrays.items():
        x = np.ascontiguousarray(x)
        fed[f"in_{name}"] = x
        d[name] = nc.dram_tensor(f"in_{name}", x.shape, mybir.dt.from_np(x.dtype), kind="ExternalInput").ap()
    d["z1_scratch"] = nc.dram_tensor("z1_scratch", (NF, 3 * C), mybir.dt.float16, kind="Internal").ap()
    out = nc.dram_tensor("out", (8, P, C), mybir.dt.float32, kind="ExternalOutput").ap()
    build_program(nc, d, out)
    r = run_bass_kernel_spmd(nc, [fed], core_ids=[0])
    return r.results[0]["out"].reshape(4, 256, C)
```
